# Optimizing a Trainium2 kernel written in Bass

```python
import numpy as np
import jax
import jax.numpy as jnp

def _softmax(x, axis=-1):
    return jax.nn.softmax(x, axis=axis)

def _gelu(x):
    return jax.nn.gelu(x, approximate=True)

def _silu(x):
    return jax.nn.silu(x)

def _sigmoid(x):
    return jax.nn.sigmoid(x)

def _layernorm(x, axis=-1, eps=1e-05):
    m = jnp.mean(x, axis=axis, keepdims=True)
    v = jnp.var(x, axis=axis, keepdims=True)
    return (x - m) / jnp.sqrt(v + eps)

def _scatter_add(tgt, idx, src, axis=0):
    return tgt.at[idx].add(src)

def _segment_sum(src, seg, n):
    return jax.ops.segment_sum(src, seg, n)
kernel_name = 'mk_sandwich_d2_jaxref_r4_9da3b2'

def setup_inputs(seed: int=0):
    np.random.seed(seed)
    _w = jnp.asarray

    def _L0_attn_setup():
        import jax, jax.numpy as jnp
        import numpy as np
        import math
        D_MODEL, D_C, D_R, NH = (256, 128, 32, 16)
        HD = D_MODEL // NH
        B, T = (2, 512)

        def _rope_tables(T, d_R):
            inv_freq = 1.0 / 10000.0 ** (jnp.arange(0, d_R, 2, dtype=jnp.float32) / d_R)
            t = jnp.arange(T, dtype=jnp.float32)
            freqs = jnp.outer(t, inv_freq)
            return (jnp.cos(freqs), jnp.sin(freqs))

        def _rotary_apply(x, cos, sin):
            d = x.shape[-1]
            x1, x2 = (x[..., :d // 2], x[..., d // 2:])
            return jnp.concatenate([x1 * cos - x2 * sin, x2 * cos + x1 * sin], axis=-1)
        key = jax.random.key(seed)
        ks = jax.random.split(key, 8)
        s = lambda fan_in: 1.0 / math.sqrt(fan_in)
        return {'x': jax.random.normal(ks[0], (B, T, D_MODEL), jnp.float32), 'W_kv_down': jax.random.normal(ks[1], (D_MODEL, D_C), jnp.float32) * s(D_MODEL), 'W_k_up': jax.random.normal(ks[2], (D_C, D_MODEL), jnp.float32) * s(D_C), 'W_v_up': jax.random.normal(ks[3], (D_C, D_MODEL), jnp.float32) * s(D_C), 'W_q': jax.random.normal(ks[4], (D_MODEL, D_MODEL), jnp.float32) * s(D_MODEL), 'W_q_rope': jax.random.normal(ks[5], (D_MODEL, D_R), jnp.float32) * s(D_MODEL), 'W_k_rope': jax.random.normal(ks[6], (D_C, D_R), jnp.float32) * s(D_C), 'W_o': jax.random.normal(ks[7], (D_MODEL, D_MODEL), jnp.float32) * s(D_MODEL)}
    _L0_attn_in = _L0_attn_setup()

    def _L0_ffn_setup():
        import jax, jax.numpy as jnp
        import numpy as np

        def _bitlinear(x, w_latent):
            scale = jax.lax.stop_gradient(jnp.clip(jnp.mean(jnp.abs(w_latent), axis=1, keepdims=True), 1e-05, None))
            tern = jnp.clip(jnp.round(w_latent / scale), -1.0, 1.0)
            w = w_latent + jax.lax.stop_gradient(tern - w_latent)
            return x @ (w * scale).T
        key = jax.random.key(seed)
        ks = jax.random.split(key, 6)
        dim, hidden, rank = (256, 1024, 16)
        B, S = (4, 1024)
        x = jax.random.normal(ks[0], (B, S, dim), dtype=jnp.float32)
        w_fc = 0.02 * jax.random.normal(ks[1], (hidden, dim), dtype=jnp.float32)
        w_proj = 0.02 * jax.random.normal(ks[2], (dim, hidden), dtype=jnp.float32)
        u = 0.02 * jax.random.normal(ks[3], (hidden, rank), dtype=jnp.float32)
        v = 0.02 * jax.random.normal(ks[4], (rank, dim), dtype=jnp.float32)
        fast_b = jax.random.normal(ks[5], (rank, rank), dtype=jnp.float32)
        gate = jnp.float32(0.05)
        return {'x': x, 'fast_b': fast_b, 'w_fc': w_fc, 'w_proj': w_proj, 'u': u, 'v': v, 'gate': gate}
    _L0_ffn_in = _L0_ffn_setup()

    def _L1_attn_setup():
        import jax, jax.numpy as jnp
        from jax import lax
        import numpy as np
        D_MODEL = 256
        K = 32
        K_Q = 4
        N_ANCHOR = 4
        N_DECAY = K - N_ANCHOR
        M = 8
        KS = 4
        H = D_MODEL // K
        N_REP = K // K_Q
        DIM_K = D_MODEL
        DIM_DECAY = K
        DIM_Q = K_Q * H * M * 2
        TOTAL = DIM_K + DIM_DECAY + DIM_Q
        B, L = (2, 512)
        key = jax.random.key(seed)
        ks = jax.random.split(key, 8)
        x = jax.random.normal(ks[0], (B, L, D_MODEL), jnp.float32)
        W_in = jax.random.normal(ks[1], (D_MODEL, TOTAL), jnp.float32) * D_MODEL ** (-0.5)
        conv_k = jax.random.normal(ks[2], (KS, 1, DIM_K + DIM_DECAY), jnp.float32) * 0.3
        grid = np.linspace(-np.pi / 3, np.pi / 3, M)
        theta = jnp.asarray(np.tile(grid.reshape(1, 1, 1, 1, M), (1, 1, K, H, 1)), jnp.float32)
        decay_slopes = jnp.log(jnp.exp(jnp.asarray(np.geomspace(0.001, 0.1, N_DECAY), jnp.float32)) - 1.0)
        anchor_slopes = jnp.log(jnp.exp(jnp.asarray(np.geomspace(0.01, 0.1, N_ANCHOR), jnp.float32)) - 1.0)
        score_scale = jnp.ones((K,), jnp.float32)
        lim = float(np.sqrt(6.0 / (H + H)))
        W_re = jax.random.uniform(ks[3], (H, H), jnp.float32, -lim, lim)
        W_im = jax.random.uniform(ks[4], (H, H), jnp.float32, -lim, lim)
        norm_scale = jnp.ones((2 * H,), jnp.float32)
        W_out = jax.random.normal(ks[5], (D_MODEL, D_MODEL), jnp.float32) * D_MODEL ** (-0.5)
        return dict(x=x, W_in=W_in, conv_k=conv_k, theta=theta, decay_slopes=decay_slopes, anchor_slopes=anchor_slopes, score_scale=score_scale, W_re=W_re, W_im=W_im, norm_scale=norm_scale, W_out=W_out)
    _L1_attn_in = _L1_attn_setup()

    def _L1_ffn_setup():
        import jax, jax.numpy as jnp
        import numpy as np
        HIDDEN = 256
        INTER = 1024
        key = jax.random.key(seed)
        k1, k2, k3, k4, k5 = jax.random.split(key, 5)
        hidden_states = jax.random.normal(k1, (4, 512, HIDDEN), dtype=jnp.float32)
        W1 = jax.random.normal(k2, (HIDDEN, INTER), dtype=jnp.float32) * (1.0 / np.sqrt(HIDDEN))
        b1 = jax.random.normal(k3, (INTER,), dtype=jnp.float32) * 0.02
        W2 = jax.random.normal(k4, (INTER, HIDDEN), dtype=jnp.float32) * (1.0 / np.sqrt(INTER))
        b2 = jax.random.normal(k5, (HIDDEN,), dtype=jnp.float32) * 0.02
        return {'hidden_states': hidden_states, 'W1': W1, 'b1': b1, 'W2': W2, 'b2': b2}
    _L1_ffn_in = _L1_ffn_setup()
    _d = {'L0_attn_x': _L0_attn_in['x'], 'L0_attn_W_kv_down': _L0_attn_in['W_kv_down'], 'L0_attn_W_k_up': _L0_attn_in['W_k_up'], 'L0_attn_W_v_up': _L0_attn_in['W_v_up'], 'L0_attn_W_q': _L0_attn_in['W_q'], 'L0_attn_W_q_rope': _L0_attn_in['W_q_rope'], 'L0_attn_W_k_rope': _L0_attn_in['W_k_rope'], 'L0_attn_W_o': _L0_attn_in['W_o'], 'L0_ffn_fast_b': _L0_ffn_in['fast_b'], 'L0_ffn_w_fc': _L0_ffn_in['w_fc'], 'L0_ffn_w_proj': _L0_ffn_in['w_proj'], 'L0_ffn_u': _L0_ffn_in['u'], 'L0_ffn_v': _L0_ffn_in['v'], 'L0_ffn_gate': _L0_ffn_in['gate'], 'L1_attn_W_in': _L1_attn_in['W_in'], 'L1_attn_conv_k': _L1_attn_in['conv_k'], 'L1_attn_theta': _L1_attn_in['theta'], 'L1_attn_decay_slopes': _L1_attn_in['decay_slopes'], 'L1_attn_anchor_slopes': _L1_attn_in['anchor_slopes'], 'L1_attn_score_scale': _L1_attn_in['score_scale'], 'L1_attn_W_re': _L1_attn_in['W_re'], 'L1_attn_W_im': _L1_attn_in['W_im'], 'L1_attn_norm_scale': _L1_attn_in['norm_scale'], 'L1_attn_W_out': _L1_attn_in['W_out'], 'L1_ffn_W1': _L1_ffn_in['W1'], 'L1_ffn_b1': _L1_ffn_in['b1'], 'L1_ffn_W2': _L1_ffn_in['W2'], 'L1_ffn_b2': _L1_ffn_in['b2']}
    _x0 = _d['L0_attn_x']
    _d['L0_attn_x'] = jax.random.normal(jax.random.fold_in(jax.random.key(seed), 1), (8, 512, 256), dtype=_x0.dtype)
    del _x0
    return _d

def reference(L0_attn_x, L0_attn_W_kv_down, L0_attn_W_k_up, L0_attn_W_v_up, L0_attn_W_q, L0_attn_W_q_rope, L0_attn_W_k_rope, L0_attn_W_o, L0_ffn_fast_b, L0_ffn_w_fc, L0_ffn_w_proj, L0_ffn_u, L0_ffn_v, L0_ffn_gate, L1_attn_W_in, L1_attn_conv_k, L1_attn_theta, L1_attn_decay_slopes, L1_attn_anchor_slopes, L1_attn_score_scale, L1_attn_W_re, L1_attn_W_im, L1_attn_norm_scale, L1_attn_W_out, L1_ffn_W1, L1_ffn_b1, L1_ffn_W2, L1_ffn_b2):

    def _L0_attn_ref(x, W_kv_down, W_k_up, W_v_up, W_q, W_q_rope, W_k_rope, W_o):
        import jax, jax.numpy as jnp
        import numpy as np
        import math
        D_MODEL, D_C, D_R, NH = (256, 128, 32, 16)
        HD = D_MODEL // NH
        B, T = (2, 512)

        def _rope_tables(T, d_R):
            inv_freq = 1.0 / 10000.0 ** (jnp.arange(0, d_R, 2, dtype=jnp.float32) / d_R)
            t = jnp.arange(T, dtype=jnp.float32)
            freqs = jnp.outer(t, inv_freq)
            return (jnp.cos(freqs), jnp.sin(freqs))

        def _rotary_apply(x, cos, sin):
            d = x.shape[-1]
            x1, x2 = (x[..., :d // 2], x[..., d // 2:])
            return jnp.concatenate([x1 * cos - x2 * sin, x2 * cos + x1 * sin], axis=-1)
        Bb, Tt, _ = x.shape
        cos, sin = _rope_tables(Tt, D_R)
        cos = cos[None]
        sin = sin[None]
        c_kv = x @ W_kv_down
        k_rope = _rotary_apply(c_kv @ W_k_rope, cos, sin)
        k = (c_kv @ W_k_up).reshape(Bb, Tt, NH, HD)
        v = (c_kv @ W_v_up).reshape(Bb, Tt, NH, HD)
        q = (x @ W_q).reshape(Bb, Tt, NH, HD)
        q_rope = _rotary_apply(x @ W_q_rope, cos, sin)
        scale = math.sqrt(HD + D_R)
        scores = jnp.einsum('bqhd,bkhd->bhqk', q, k)
        scores = scores + jnp.einsum('bqr,bkr->bqk', q_rope, k_rope)[:, None]
        scores = scores / scale
        causal = jnp.triu(jnp.ones((Tt, Tt), dtype=bool), k=1)
        scores = jnp.where(causal[None, None], -jnp.inf, scores)
        w = jax.nn.softmax(scores, axis=-1)
        attn = jnp.einsum('bhqk,bkhd->bqhd', w, v).reshape(Bb, Tt, D_MODEL)
        return attn @ W_o

    def _L0_ffn_ref(x, fast_b, w_fc, w_proj, u, v, gate):
        import jax, jax.numpy as jnp
        import numpy as np

        def _bitlinear(x, w_latent):
            scale = jax.lax.stop_gradient(jnp.clip(jnp.mean(jnp.abs(w_latent), axis=1, keepdims=True), 1e-05, None))
            tern = jnp.clip(jnp.round(w_latent / scale), -1.0, 1.0)
            w = w_latent + jax.lax.stop_gradient(tern - w_latent)
            return x @ (w * scale).T
        h = _bitlinear(x, w_fc) + gate * (x @ v.T @ fast_b.T @ u.T)
        r = jnp.maximum(h, 0.0)
        return _bitlinear(r * r, w_proj)

    def _L1_attn_ref(x, W_in, conv_k, theta, decay_slopes, anchor_slopes, score_scale, W_re, W_im, norm_scale, W_out):
        import jax, jax.numpy as jnp
        from jax import lax
        import numpy as np
        D_MODEL = 256
        K = 32
        K_Q = 4
        N_ANCHOR = 4
        N_DECAY = K - N_ANCHOR
        M = 8
        KS = 4
        H = D_MODEL // K
        N_REP = K // K_Q
        DIM_K = D_MODEL
        DIM_DECAY = K
        DIM_Q = K_Q * H * M * 2
        TOTAL = DIM_K + DIM_DECAY + DIM_Q
        B, L = (2, 512)
        b, l, _ = x.shape
        z = x @ W_in
        z_mem = z[..., :DIM_K + DIM_DECAY]
        q_raw = z[..., DIM_K + DIM_DECAY:]
        zp = jnp.pad(z_mem, ((0, 0), (KS - 1, 0), (0, 0)))
        z_mem = lax.conv_general_dilated(zp, conv_k, window_strides=(1,), padding='VALID', dimension_numbers=('NWC', 'WIO', 'NWC'), feature_group_count=DIM_K + DIM_DECAY)
        k_val = z_mem[..., :DIM_K].reshape(b, l, K, H)
        s_raw = z_mem[..., -K:].reshape(b, l, K, 1)
        q = q_raw.reshape(b, l, K_Q, H, M, 2)
        q_re, q_im = (q[..., 0], q[..., 1])
        pos = jnp.arange(l, dtype=jnp.float32)
        slopes_d = jax.nn.softplus(decay_slopes).reshape(1, 1, N_DECAY, 1)
        dist = jnp.maximum(jnp.float32(l - 1) - pos, 0.0)
        lw_d = -slopes_d * dist[None, :, None, None]
        slopes_a = jax.nn.softplus(anchor_slopes).reshape(1, 1, N_ANCHOR, 1)
        lw_a = -slopes_a * pos[None, :, None, None]
        log_tw = jnp.concatenate([lw_d, lw_a], axis=2)
        log_p = jnp.clip(score_scale[None, None, :, None] * s_raw, -20.0, 20.0)
        p_w = jnp.exp(log_p + log_tw)
        phi = k_val[..., None] * theta
        re_k = jnp.cos(phi)
        im_k = jnp.sin(phi)
        den = jnp.cumsum(p_w[..., 0], axis=1)
        pwb = p_w[..., None]
        num_re = jnp.cumsum(pwb * re_k, axis=1)
        num_im = jnp.cumsum(pwb * im_k, axis=1)
        inv = lax.rsqrt(jnp.maximum(den, 0.0001))
        inv = (inv * inv)[..., None, None]
        s_re = (num_re * inv).reshape(b, l, K_Q, N_REP, H, M)
        s_im = (num_im * inv).reshape(b, l, K_Q, N_REP, H, M)
        qr = q_re.reshape(b, l, K_Q, 1, H, M)
        qi = q_im.reshape(b, l, K_Q, 1, H, M)
        out_re = jnp.sum(s_re * qr + s_im * qi, axis=-1).reshape(b, l, K, H)
        out_im = jnp.sum(s_im * qr - s_re * qi, axis=-1).reshape(b, l, K, H)
        y_re = out_re * norm_scale[:H] * jnp.diagonal(W_re)
        y_im = out_im * norm_scale[H:] * jnp.diagonal(W_im)
        y = jax.nn.silu((y_re + y_im).reshape(b, l, DIM_K))
        return y @ W_out

    def _L1_ffn_ref(hidden_states, W1, b1, W2, b2):
        import jax, jax.numpy as jnp
        import numpy as np
        HIDDEN = 256
        INTER = 1024
        h = jax.nn.relu(jnp.einsum('bsh,hi->bsi', hidden_states, W1) + b1)
        return jnp.einsum('bsi,ih->bsh', h, W2) + b2
    x = L0_attn_x
    x = x + _layernorm(_L0_attn_ref(_layernorm(x, axis=-1), L0_attn_W_kv_down, L0_attn_W_k_up, L0_attn_W_v_up, L0_attn_W_q, L0_attn_W_q_rope, L0_attn_W_k_rope, L0_attn_W_o), axis=-1)
    x = x + _layernorm(_L0_ffn_ref(_layernorm(x, axis=-1), L0_ffn_fast_b, L0_ffn_w_fc, L0_ffn_w_proj, L0_ffn_u, L0_ffn_v, L0_ffn_gate), axis=-1)
    x = x + _layernorm(_L1_attn_ref(_layernorm(x, axis=-1), L1_attn_W_in, L1_attn_conv_k, L1_attn_theta, L1_attn_decay_slopes, L1_attn_anchor_slopes, L1_attn_score_scale, L1_attn_W_re, L1_attn_W_im, L1_attn_norm_scale, L1_attn_W_out), axis=-1)
    x = x + _layernorm(_L1_ffn_ref(_layernorm(x, axis=-1), L1_ffn_W1, L1_ffn_b1, L1_ffn_W2, L1_ffn_b2), axis=-1)
    return x

_drawn_inputs = setup_inputs


def setup_inputs(seed=0):
    import zlib

    import numpy as np

    out = dict(_drawn_inputs(seed))
    spreads = {'L1_attn_score_scale': (1.0, 0.6), 'L1_attn_norm_scale': (1.0, 0.2)}
    factors = {'L0_ffn_fast_b': 3.583,
     'L0_ffn_u': 3.591,
     'L0_ffn_v': 3.609,
     'L1_attn_anchor_slopes': 47.864,
     'L1_ffn_b1': 6.199,
     'L1_ffn_b2': 4.457}
    for name, (base, spread) in spreads.items():
        noise = np.random.default_rng([zlib.crc32(name.encode()), seed]).standard_normal(out[name].shape)
        drawn = base * np.exp(spread * noise) if base else spread * noise
        out[name] = jnp.asarray(drawn.astype(out[name].dtype))
    for name, factor in factors.items():
        out[name] = (out[name] * factor).astype(out[name].dtype)
    return out
```

```python
from contextlib import ExitStack

import concourse.bass as bass
from concourse import mybir

ALU = mybir.AluOpType
ACT = mybir.ActivationFunctionType
AX = mybir.AxisListType
F32 = mybir.dt.float32

P = 128
B, T, D = 8, 512, 256
TT = T // P
DC = D // P
NH, HD, DR = 16, 16, 32
HID = 1024
HC = HID // P
RANK = 16
K, KQ, H, M = 32, 4, 8, 8
REP = K // KQ
ML = 4
MH = M // ML
RL = 4
RH = REP // RL
W = KQ * H
KS = 4
N_DECAY = 28
EPS = 1e-5
SCORE_SCALE = 1.0 / float(HD + DR) ** 0.5
MASKED = -1e30
ROUND = 12582912.0
TWO_PI = 6.283185
HALF_PI = 1.5707963
BIG = 3.0e38

HEADS = [(n // 16, n // 4 % 4, n % 4) for n in range(64)]
LAG_T, LAG_PV, LAG_OT = 2, 7, 20
SLOTS = 64 + 6


def attention_items():
    return [("norm", 0), ("xT", 0), ("proj", 0), ("proj", 1), ("base", 0)] + \
           [("slot", n) for n in range(SLOTS)] + [("attnT", 0), ("out", 0), ("sum", 0)]


def mixer_items():
    at, items = [0.5], []

    def put(name, n=0, step=1.0):
        items.append(((name, n), at[0]))
        at[0] += step

    put("norm", 0), put("xT", 0)
    for g in range(HC):
        put("fc", g, 0.9)
    for g in range(2):
        put("proj", g, 2.5)
    put("sum", 0), put("norm", 1), put("xT", 1)
    for g in range(4):
        put("z", g)
    put("weights", 0)
    for g in range(4):
        put("query", g, 0.7)
    put("turn", 0), put("turn", 1), put("wave", 0)
    for r in range(REP):
        if r + 1 < REP:
            put("wave", r + 1, 0.5)
        put("scan", r, 1.2)
        if r + 2 < REP:
            put("turn", r + 2, 0.8)
        put("gather", r, 0.5)
    put("gate", 0), put("out", 0), put("sum", 1), put("norm", 2), put("xT", 2)
    for g in range(HC):
        put("fc2", g, 0.9)
    for g in range(2):
        put("proj2", g, 2.5)
    put("sum", 2)
    return items


def weave():
    mixer, order = mixer_items(), []
    span = mixer[-1][1] + 1
    attention = attention_items()
    for i, item in enumerate(attention):
        order.append(("attention", item))
        while mixer and mixer[0][1] * len(attention) / span <= i + 1:
            order.append(("mixer", mixer.pop(0)[0]))
    return order + [("mixer", item) for item, _ in mixer]


ORDER = weave()


def plan_banks():
    place, count = {}, [0] * 8

    def use(name, bank):
        count[bank] += 1
        place[name] = (bank, count[bank])

    for n, name in enumerate(("xT0", "xT1", "ckv", "q0", "q1", "qr", "qs", "k0", "k1", "kr", "ks", "v0", "v1")):
        use(name, n % 5)
    for t in range(TT):
        use(f"base{t}", (13 + t) % 5)
    for n in range(SLOTS):
        if n < 64:
            use(f"S{n}", n % 3)
        if LAG_T <= n < 64 + LAG_T:
            use(f"T{n - LAG_T}", 3 + n % 2)
        if n >= LAG_OT and (n - LAG_OT) % 16 == 0:
            use(f"OT{(n - LAG_OT) // 16}", n % 3)
    use("aT0", 3), use("aT1", 4)
    use("y0", 0), use("y1", 1)

    def pair(name):
        use(name + "0", 6), use(name + "1", 7)

    pair("m_xTa")
    for i in range(HC):
        use(f"m_fc{i}", 6 + i % 2)
    pair("m_proj"), pair("m_xTb")
    for i in range(4):
        use(f"m_z{i}", 6 + i % 2)
    for i in range(4):
        use(f"m_q{i}", 6 + i % 2)
    pair("m_mem"), pair("m_out"), pair("m_xTc")
    for i in range(HC):
        use(f"m_fd{i}", 6 + i % 2)
    pair("m_prok")
    return place, count


class Signal:

    def __init__(self, sem, per_batch, step=1):
        self.sem, self.per_batch, self.step, self.given = sem, per_batch, step, 0

    @property
    def one(self):
        self.given += 1
        return self.sem, self.step

    def at(self, b, n):
        return self.sem, (b * self.per_batch + (self.per_batch + n)) * self.step

    def last(self, b):
        return self.at(b, (self.given - 1) % self.per_batch + 1)


def sandwich_kernel(nc, x, w_kv_down, w_k_up, w_v_up, w_q, w_q_rope, w_k_rope, w_o,
                    fast_b, w_fc, w_proj, u, v, gate,
                    w_in, conv_k, theta, decay_slopes, anchor_slopes, score_scale, w_re, w_im,
                    norm_scale, w_out, w1, b1, w2, b2,
                    c_ident, c_rope, c_mask, c_parity, c_dist, c_sel, out):
    place, bank_uses = plan_banks()
    with ExitStack() as ctx:
        def sb(name, shape):
            return ctx.enter_context(nc.sbuf_tensor(name, shape, F32))

        def sem(name):
            return ctx.enter_context(nc.semaphore(name))

        signals = {}

        def signal(name, per_batch, step=1):
            signals[name] = Signal(sem(name), per_batch, step)
            return signals[name]

        ident = sb("ident", [P, P])
        rope = sb("rope", [DR, 2, T])
        mask = sb("mask", [P, P])
        parity = sb("parity", [P, 2])
        sel = sb("sel", [P, W])
        wkv = sb("wkv", [P, DC, P])
        wku = sb("wku", [P, D])
        wvu = sb("wvu", [P, D])
        wq = sb("wq", [P, DC, D])
        wqr = sb("wqr", [P, DC, 2, DR])
        wkr = sb("wkr", [P, 2, DR])
        wo = sb("wo", [P, DC, D])
        wfc = sb("wfc", [P, DC, HID])
        wpr = sb("wpr", [P, HC, D])
        wz = sb("wz", [P, DC, 2, RH, P])
        wqc = sb("wqc", [P, DC, 2, MH, P])
        wout = sb("wout", [P, RH, D])
        wf1 = sb("wf1", [P, DC, HID])
        wf2 = sb("wf2", [P, HC, D])
        b1c = sb("b1c", [P, HC])
        b2r = sb("b2r", [P, D])
        turns = sb("turns", [P, REP, MH])
        taps = sb("taps", [P, 2, RH, KS])
        sscale = sb("sscale", [P, RH])
        logw = sb("logw", [P, RH, T])
        power = sb("power", [P, TT])
        half_pi = sb("half_pi", [P, 1])
        zero = sb("zero", [P, 1])

        x_in = sb("x_in", [P, TT, D])
        xa = sb("xa", [P, TT, D])
        xr = sb("xr", [P, TT, D])
        xna = sb("xna", [P, TT, D])
        xnr = sb("xnr", [P, TT, D])
        xTa = sb("xTa", [P, DC, T])
        xTr = sb("xTr", [P, DC, T])
        norms = sb("norms", [P, 2, TT, 11])

        pool_words = 30544
        work = sb("work", [P, pool_words])
        cut = [0]

        def part(*shape):
            n = 1
            for s in shape:
                n *= s
            ap = work[:, cut[0]:cut[0] + n]
            cut[0] += n
            assert cut[0] <= pool_words, (cut[0], pool_words)
            if len(shape) == 1:
                return ap
            names = "abcd"[:len(shape)]
            return ap.rearrange(f"p ({' '.join(names)}) -> p {' '.join(names)}", **dict(zip(names, shape)))

        qpar = part(2, DC, T)
        kT = part(DC, T)
        base = part(TT * (TT + 1) // 2 * P)
        vaug = part(TT, NH, 32)
        sc = part(2, T)
        pr = part(2, T)
        osb = part(T)
        nmax = part(64)
        rden = part(TT, 4)
        pt_at = cut[0]
        pt = part(6, T)
        cut[0] = pt_at
        ckv = part(T)
        qrope = part(T)
        krope = part(T)
        rtmp = part(2, T)
        cut[0] = pt_at + 6 * T
        zc = part(2, RH, T)
        kvr = part(RL, T)
        pwr = part(RL, T)
        qc = part(2 * MH, T)
        frac = part(2, MH, T)
        whole = part(MH, T)
        inv = part(RH, T)
        ring_at = cut[0]
        ring = part(3, 2 * MH, T)
        cut[0] = ring_at
        hid = part(HC, T)
        att = xna

        ps = ctx.enter_context(nc.psum_tensor("ps", [P, 8, 512], F32))

        filled = [signal(f"bank{i}_filled", n - (1 if i >= 6 else 0)) for i, n in enumerate(bank_uses)]
        drained = [signal(f"bank{i}_drained", n) for i, n in enumerate(bank_uses)]
        x_loaded = signal("x_loaded", 1, 16)
        a_stats = signal("a_stats", 2)
        a_rstd = signal("a_rstd", 2)
        a_shift = signal("a_shift", 1)
        a_scaled = signal("a_scaled", 1)
        a_xn = signal("a_xn", 1)
        a_xT = signal("a_xT", 2)
        a_sum = signal("a_sum", 1)
        ckv_ready = signal("ckv_ready", 1)
        q_ready = signal("q_ready", 2)
        rope_ready = signal("rope_ready", 2)
        k_ready = signal("k_ready", 2)
        v_ready = signal("v_ready", 2)
        scored = signal("scored", 64)
        exped = signal("exped", 64)
        pt_act = signal("pt_act", 32)
        pt_dve = signal("pt_dve", 32)
        pv_done = signal("pv_done", 16)
        o_copied = signal("o_copied", 4)
        attn_ready = signal("attn_ready", 4)
        attnT_ready = signal("attnT_ready", 2)
        a_step = signal("a_step", 12)
        m_stats = signal("m_stats", 6)
        m_rstd = signal("m_rstd", 6)
        m_shift = signal("m_shift", 3)
        m_scaled = signal("m_scaled", 3)
        m_xn = signal("m_xn", 3)
        m_xT = signal("m_xT", 6)
        m_sum = signal("m_sum", 3)
        hid_relu = signal("hid_relu", 2 * HC)
        hid_sq = signal("hid_sq", HC)
        last_tap = signal("last_tap", 4)
        conv_done = signal("conv_done", 4)
        logp_ready = signal("logp_ready", 1)
        pw_ready = signal("pw_ready", 1)
        kv_sent = [signal(f"kv{l}_sent", RH * ML, 16) for l in range(RL)]
        pw_sent = [signal(f"pw{l}_sent", RH * ML, 16) for l in range(RL)]
        qc_ready = signal("qc_ready", 4)
        turned = signal("turned", REP)
        folded = signal("folded", REP)
        waved = signal("waved", REP)
        weighed = signal("weighed", REP)
        mixed = signal("mixed", REP)
        gathered = signal("gathered", REP)
        y_raw = signal("y_raw", 1)
        y_tanh = signal("y_tanh", 1)
        y_ready = signal("y_ready", 1)
        b2_added = signal("b2_added", 1)
        stored = signal("stored", 1, 16)
        m_step = signal("m_step", 47)

        loaded = sem("loaded")
        zeroed = sem("zeroed")
        waits_taken = sem("waits_taken")
        prep_dve = sem("prep_dve")
        prep_pe = sem("prep_pe")
        prep_act = sem("prep_act")
        set_up = sem("set_up")

        cut[0] = 0
        raw_fc = part(HC, D)
        raw_pr = part(DC, HID)
        raw_in = part(DC, 800)
        tmp_a = part(2048)
        tmp_b = part(2048)
        raw_u = part(HC, RANK)
        raw_fb = part(RANK)
        raw_v = part(D)
        uT = part(HID)
        a1T = part(HID)
        gcol = part(1)
        rows = part(3, 16)
        fac = part(4, H)
        ab = part(2, H)
        slope = part(RH)
        soft = part(6, RH)
        dist = part(RH, T)
        theta_raw = part(REP, MH)

        def bank(name):
            return place[name][0]

        def out_of(name):
            return ps[:, bank(name), :]

        def may_fill(pe, b, name):
            i, n = place[name]
            pe.wait_ge(*drained[i].at(b, n - 1))

        def fills(name):
            return filled[bank(name)].one

        def drains(name):
            return drained[bank(name)].one

        def is_filled(eng, b, name):
            i, n = place[name]
            skipped = i >= 6 and n > place["m_mem0" if i == 6 else "m_mem1"][1]
            eng.wait_ge(*filled[i].at(b, n - skipped))

        def run(eng, attention, mixer):
            for chain, item in ORDER:
                if chain == "attention":
                    attention(0, *item)
            with eng.Fori(1, B) as b:
                for chain, item in ORDER:
                    if chain == "attention":
                        attention(b, *item)
                    else:
                        mixer(b - 1, *item)
            for chain, item in ORDER:
                if chain == "mixer":
                    mixer(B - 1, *item)

        def base_of(t):
            return base[:, t * (t + 1) // 2 * P:(t + 1) * (t + 2) // 2 * P]

        def slot_rows():
            for l in range(RL):
                for q in range(KQ):
                    for r in range(RH):
                        yield l * W + q * H, r, q * REP + r * RL + l

        block = ctx.enter_context(nc.Block())

        n_loads = [0]

        @block.sync
        def _(sp):
            def load(dst, src):
                sp.dma_start(dst, src, allow_slow_non_contiguous=True).then_inc(loaded, 16)
                n_loads[0] += 1

            load(raw_fc, w_fc.rearrange("(g p) i -> p g i", p=P))
            load(raw_pr, w_proj.rearrange("(g p) i -> p g i", p=P))
            load(raw_in, w_in.rearrange("(c p) n -> p c n", p=P))
            load(raw_u, u.rearrange("(g p) r -> p g r", p=P))
            load(raw_fb[0:RANK], fast_b)
            load(raw_v[0:RANK], v)
            load(gcol, gate.to_broadcast([P, 1]))
            load(ident[:], c_ident)
            load(rope[:], c_rope)
            load(mask[:], c_mask)
            load(parity[:], c_parity)
            load(sel[:], c_sel)
            load(dist, c_dist)
            load(wkv[:], w_kv_down.rearrange("(c p) n -> p c n", p=P))
            load(wku[:], w_k_up)
            load(wvu[:], w_v_up)
            load(wq[:], w_q.rearrange("(c p) n -> p c n", p=P))
            rq, hr = w_q_rope.rearrange("(c p) n -> p c n", p=P), DR // 2
            load(wqr[:, :, 0, :], rq)
            load(wqr[:, :, 1, 0:hr], rq[:, :, hr:DR])
            load(wqr[:, :, 1, hr:DR], rq[:, :, 0:hr])
            load(wkr[:, 0, :], w_k_rope)
            load(wkr[:, 1, 0:hr], w_k_rope[:, hr:DR])
            load(wkr[:, 1, hr:DR], w_k_rope[:, 0:hr])
            load(wo[:], w_o.rearrange("(c p) n -> p c n", p=P))
            load(wf1[:], w1.rearrange("(c p) n -> p c n", p=P))
            load(wf2[:], w2.rearrange("(c p) n -> p c n", p=P))
            load(b1c[:], b1.rearrange("(g p) -> p g", p=P))
            load(b2r[:], b2.rearrange("(o d) -> o d", o=1).to_broadcast([P, D]))
            load(fac[:, 0, :], norm_scale.rearrange("(o h) -> o h", o=2)[0:1, :].to_broadcast([P, H]))
            load(fac[:, 1, :], norm_scale.rearrange("(o h) -> o h", o=2)[1:2, :].to_broadcast([P, H]))
            for i, w in ((2, w_re), (3, w_im)):
                for h in range(H):
                    load(fac[:, i, h:h + 1], w[h:h + 1, h:h + 1].to_broadcast([P, 1]))
            column = "(k o) -> k o"
            for p0, r, k in slot_rows():
                load(wout[p0:p0 + H, r, :], w_out[k * H:(k + 1) * H, :])
                load(taps[p0:p0 + H, 0, r, :], conv_k[:, 0, k * H:(k + 1) * H].rearrange("s h -> h s"))
                load(taps[p0:p0 + H, 1, r, :], conv_k[:, 0, D + k:D + k + 1].rearrange("s o -> o s").to_broadcast([H, KS]))
                load(sscale[p0:p0 + H, r:r + 1], score_scale.rearrange(column, o=1)[k:k + 1].to_broadcast([H, 1]))
                s = decay_slopes if k < N_DECAY else anchor_slopes
                k0 = k if k < N_DECAY else k - N_DECAY
                load(slope[p0:p0 + H, r:r + 1], s.rearrange(column, o=1)[k0:k0 + 1].to_broadcast([H, 1]))
            for l in range(ML):
                for q in range(KQ):
                    p0 = l * W + q * H
                    for i in range(MH):
                        load(theta_raw[p0:p0 + H, :, i],
                             theta[0, 0, q * REP:(q + 1) * REP, :, i * ML + l].rearrange("k h -> h k"))
            for s in [x_loaded, stored] + kv_sent + pw_sent:
                sp.sem_inc(s.sem, s.per_batch * s.step)
            sp.wait_ge(set_up, 4)

            def load_x(b):
                sp.dma_start(x_in[:], x[bass.ds(b, 1)].rearrange("o (t p) d -> p (o t) d", p=P)
                             ).then_inc(*x_loaded.one)

            load_x(0)

            def attention(b, item, n):
                if item == "norm" and not isinstance(b, int):
                    sp.wait_ge(*a_sum.at(b, 0))
                    load_x(b)

            def send(kind, dst, sent):
                for l in range(RL):
                    for m in range(ML):
                        sp.dma_start(dst[m * W:(m + 1) * W, l, :], zc[l * W:(l + 1) * W, kind, 0, :]
                                     ).then_inc(*sent[l].one)

            def mixer(b, item, n):
                if item == "query" and n == 0:
                    sp.wait_ge(*conv_done.at(b, 4))
                    send(0, kvr, kv_sent)
                    sp.wait_ge(*pw_ready.at(b, 1))
                    send(1, pwr, pw_sent)
                if item == "scan" and n < RL:
                    l = n
                    for kind, dst, sent, used in ((0, kvr, kv_sent, turned), (1, pwr, pw_sent, weighed)):
                        sp.wait_ge(*used.at(b, l + 1))
                        for m in range(ML):
                            sp.dma_start(dst[m * W:(m + 1) * W, l, :], zc[l * W:(l + 1) * W, kind, 1, :]
                                         ).then_inc(*sent[l].one)
                if item == "sum" and n == 2:
                    sp.wait_ge(*m_sum.at(b, 3))
                    sp.dma_start(out[bass.ds(b, 1)].rearrange("o (t p) d -> p (o t) d", p=P), xr[:]
                                 ).then_inc(*stored.one)

            run(sp, attention, mixer)
            sp.wait_ge(*stored.at(B - 1, 1))

        @block.gpsimd
        def _(pool):
            g = nc.gpsimd
            g.memset(power[:], -0.5).then_inc(zeroed, 1)
            g.memset(half_pi[:], HALF_PI).then_inc(zeroed, 1)
            g.memset(zero[:], 0.0).then_inc(zeroed, 1)
            pool.wait_ge(zeroed, 3)
            for s in (a_rstd, a_sum, m_rstd, m_sum, hid_sq, weighed):
                pool.sem_inc(s.sem, s.per_batch)
            pool.sem_inc(set_up, 1)

            def rsqrt(b, chain, stats, rstd, n):
                pool.wait_ge(*stats.at(b, n))
                g.tensor_tensor(norms[:, chain, :, 9], norms[:, chain, :, 8], power[:], ALU.pow).then_inc(*rstd.one)

            def attention(b, item, n):
                if item == "norm":
                    rsqrt(b, 0, a_stats, a_rstd, 1)
                if item == "sum":
                    rsqrt(b, 0, a_stats, a_rstd, 2)
                    pool.wait_ge(*a_scaled.at(b, 1))
                    pool.wait_ge(*m_sum.at(b, -2))
                    g.tensor_tensor(xa[:], x_in[:], xna[:], ALU.add).then_inc(*a_sum.one)

            def mixer(b, item, n):
                if item == "norm":
                    rsqrt(b, 1, m_stats, m_rstd, 2 * n + 1)
                if item == "fc":
                    pool.wait_ge(*hid_relu.at(b, n + 1))
                    g.tensor_tensor(hid[:, n, :], hid[:, n, :], hid[:, n, :], ALU.mult).then_inc(*hid_sq.one)
                if item == "wave":
                    r, slot = n, n % 3
                    pool.wait_ge(*waved.at(b, r + 1))
                    pool.wait_ge(*pw_sent[r % RL].at(b, (r // RL + 1) * ML))
                    g.tensor_tensor(ring[:, slot], ring[:, slot],
                                    pwr[:, r % RL, None, :].to_broadcast([P, 2 * MH, T]), ALU.mult
                                    ).then_inc(*weighed.one)
                if item == "sum":
                    rsqrt(b, 1, m_stats, m_rstd, 2 * n + 2)
                    pool.wait_ge(*m_scaled.at(b, n + 1))
                    if n == 0:
                        pool.wait_ge(*stored.at(b, 0))
                    g.tensor_tensor(xr[:], (xa if n == 0 else xr)[:], xnr[:], ALU.add).then_inc(*m_sum.one)

            run(pool, attention, mixer)

        @block.tensor
        def _(pe):
            pe.wait_ge(loaded, 16 * n_loads[0])
            mm, tr = nc.tensor.matmul, nc.tensor.transpose
            for g in range(HC):
                i = tr(ps[0:RANK, g // 4, g % 4 * P:(g % 4 + 1) * P], raw_u[:, g, :], ident[:])
            i.then_inc(prep_pe, 1)
            pe.wait_ge(prep_act, 1)
            for g in range(2):
                i = mm(ps[0:RANK, 2 + g, :], raw_fb[0:RANK, :], uT[0:RANK, g * 512:(g + 1) * 512],
                       start=True, stop=True)
            i.then_inc(prep_pe, 1)
            pe.wait_ge(prep_act, 2)
            for g in range(HC):
                i = mm(ps[:, 4 + g // 2, g % 2 * D:(g % 2 + 1) * D], a1T[0:RANK, g * P:(g + 1) * P],
                       raw_v[0:RANK, :], start=True, stop=True)
            i.then_inc(prep_pe, 1)
            pe.wait_ge(prep_dve, DVE_ROWS)
            for c in range(DC):
                for g in range(HC):
                    i = tr(ps[:, 2 * c + g // 4, g % 4 * P:(g % 4 + 1) * P], raw_fc[:, g, c * P:(c + 1) * P],
                           ident[:])
            i.then_inc(prep_pe, 1)
            for h in range(HC):
                for g in range(DC):
                    i = tr(ps[:, 4 + h // 2, h % 2 * D + g * P:h % 2 * D + (g + 1) * P],
                           raw_pr[:, g, h * P:(h + 1) * P], ident[:])
            i.then_inc(prep_pe, 1)
            for s in [f for f in filled if f.per_batch] + [pv_done, gathered]:
                pe.sem_inc(s.sem, s.per_batch)
            pe.sem_inc(set_up, 1)
            pe.wait_ge(set_up, 4)

            def transposes(b, tag, src):
                for c in range(DC):
                    name = f"{tag}{c}"
                    may_fill(pe, b, name)
                    for t in range(TT):
                        i = tr(ps[:, bank(name), t * P:(t + 1) * P], src[:, t, c * P:(c + 1) * P], ident[:])
                    i.then_inc(*fills(name))

            def product(b, name, dst, pairs):
                may_fill(pe, b, name)
                for j, (l, r) in enumerate(pairs):
                    i = mm(dst, l, r, start=j == 0, stop=j == len(pairs) - 1)
                i.then_inc(*fills(name))

            def tokens_out(b, tag, half, lhs, rhs, n_k):
                name = f"{tag}{half}"
                may_fill(pe, b, name)
                for t in range(2):
                    tt = 2 * half + t
                    for j in range(n_k):
                        i = mm(ps[:, bank(name), t * D:(t + 1) * D], lhs[:, j, tt * P:(tt + 1) * P],
                               rhs[:, j, :], start=j == 0, stop=j == n_k - 1)
                i.then_inc(*fills(name))

            xa_c = [xTa[:, c, :] for c in range(DC)]
            xm_c = [xTr[:, c, :] for c in range(DC)]

            def turn_out(b, g):
                name = f"OT{g}"
                may_fill(pe, b, name)
                pe.wait_ge(*o_copied.at(b, g + 1))
                for t in range(TT):
                    i = tr(ps[:, bank(name), t * P:(t + 1) * P], osb[:, t * P:(t + 1) * P], ident[:])
                i.then_inc(*fills(name))

            def attention(b, item, n):
                if item == "xT":
                    pe.wait_ge(*a_xn.at(b, 1))
                    transposes(b, "xT", xna)
                if item == "proj" and n == 0:
                    pe.wait_ge(*a_xT.at(b, 2))
                    product(b, "ckv", out_of("ckv"), [(wkv[:, c, :], xa_c[c]) for c in range(DC)])
                    for g in range(DC):
                        product(b, f"q{g}", out_of(f"q{g}"),
                                [(wq[:, c, g * P:(g + 1) * P], xa_c[c]) for c in range(DC)])
                    for s, name in enumerate(("qr", "qs")):
                        product(b, name, out_of(name)[0:DR], [(wqr[:, c, s, :], xa_c[c]) for c in range(DC)])
                if item == "proj" and n == 1:
                    pe.wait_ge(*ckv_ready.at(b, 1))
                    for g in range(DC):
                        product(b, f"k{g}", out_of(f"k{g}"), [(wku[:, g * P:(g + 1) * P], ckv)])
                    for s, name in enumerate(("kr", "ks")):
                        product(b, name, out_of(name)[0:DR], [(wkr[:, s, :], ckv)])
                    for g in range(2):
                        name = f"v{g}"
                        may_fill(pe, b, name)
                        for t in range(2):
                            i = mm(ps[:, bank(name), t * D:(t + 1) * D],
                                   ckv[:, (2 * g + t) * P:(2 * g + t + 1) * P], wvu[:], start=True, stop=True)
                        i.then_inc(*fills(name))
                if item == "base":
                    pe.wait_ge(*rope_ready.at(b, 2))
                    for t in range(TT):
                        product(b, f"base{t}", out_of(f"base{t}")[:, 0:(t + 1) * P],
                                [(qrope[0:DR, t * P:(t + 1) * P], krope[0:DR, 0:(t + 1) * P])])
                    pe.wait_ge(*q_ready.at(b, 2))
                    pe.wait_ge(*k_ready.at(b, 2))
                    pe.wait_ge(*v_ready.at(b, 2))
                if item == "slot":
                    if n < 64:
                        hg, qt, j = HEADS[n]
                        i8, nk = hg % 2 * 4 + j, (qt + 1) * P
                        p0 = 32 * (i8 // 2)
                        product(b, f"S{n}", out_of(f"S{n}")[:, 0:nk],
                                [(qpar[p0:p0 + 32, i8 % 2, hg // 2, qt * P:(qt + 1) * P],
                                  kT[p0:p0 + 32, hg // 2, 0:nk])])
                    if LAG_T <= n < 64 + LAG_T:
                        m = n - LAG_T
                        name = f"T{m}"
                        may_fill(pe, b, name)
                        pe.wait_ge(*exped.at(b, m + 1))
                        for t in range(HEADS[m][1] + 1):
                            i = tr(ps[:, bank(name), t * P:(t + 1) * P], pr[:, m % 2, t * P:(t + 1) * P], ident[:])
                        i.then_inc(*fills(name))
                    m = n - LAG_PV + 1
                    if m >= 0 and m % 4 == 0 and m < 64:
                        hg, qt, _ = HEADS[m]
                        if qt == 0:
                            pe.wait_ge(*o_copied.at(b, hg))
                        pe.wait_ge(*pt_act.at(b, m // 2 + 2))
                        pe.wait_ge(*pt_dve.at(b, m // 2 + 2))
                        for t in range(qt + 1):
                            for j in range(4):
                                i = mm(ps[32 * j:32 * j + 32, 5, qt * P:(qt + 1) * P],
                                       vaug[:, t, hg * 4 + j, :], pt[:, (m + j) % 6, t * P:(t + 1) * P],
                                       start=t == 0, stop=t == qt)
                        i.then_inc(*pv_done.one)
                    if n >= LAG_OT and (n - LAG_OT) % 16 == 0:
                        turn_out(b, (n - LAG_OT) // 16)
                if item == "attnT":
                    pe.wait_ge(*attn_ready.at(b, 4))
                    transposes(b, "aT", att)
                if item == "out":
                    pe.wait_ge(*attnT_ready.at(b, 2))
                    tokens_out(b, "y", 0, xTa, wo, DC)
                    tokens_out(b, "y", 1, xTa, wo, DC)

            def mixer(b, item, n):
                if item == "xT":
                    pe.wait_ge(*m_xn.at(b, n + 1))
                    transposes(b, ("m_xTa", "m_xTb", "m_xTc")[n], xnr)
                if item in ("fc", "fc2"):
                    tag, w, k = ("m_fc", wfc, 2) if item == "fc" else ("m_fd", wf1, 6)
                    if n == 0:
                        pe.wait_ge(*m_xT.at(b, k))
                    product(b, f"{tag}{n}", out_of(f"{tag}{n}"),
                            [(w[:, c, n * P:(n + 1) * P], xm_c[c]) for c in range(DC)])
                if item == "proj":
                    pe.wait_ge(*hid_sq.at(b, HC))
                    tokens_out(b, "m_proj", n, hid, wpr, HC)
                if item == "proj2":
                    pe.wait_ge(*hid_relu.at(b, 2 * HC))
                    tokens_out(b, "m_prok", n, hid, wf2, HC)
                if item == "z":
                    if n == 0:
                        pe.wait_ge(*m_xT.at(b, 4))
                    product(b, f"m_z{n}", out_of(f"m_z{n}"),
                            [(wz[:, c, n % 2, n // 2, :], xm_c[c]) for c in range(DC)])
                if item == "query":
                    product(b, f"m_q{n}", out_of(f"m_q{n}"),
                            [(wqc[:, c, n // MH, n % MH, :], xm_c[c]) for c in range(DC)])
                if item == "gather":
                    name = f"m_mem{n // RL}"
                    if n % RL == 0:
                        may_fill(pe, b, name)
                    pe.wait_ge(*mixed.at(b, n + 1))
                    for j in range(2 * MH):
                        i = mm(ps[n % RL * W:(n % RL + 1) * W, bank(name), :], sel[:], ring[:, n % 3, j, :],
                               start=j == 0, stop=j == 2 * MH - 1)
                    i.then_inc(*gathered.one)
                if item == "out":
                    pe.wait_ge(*y_ready.at(b, 1))
                    tokens_out(b, "m_out", 0, inv, wout, RH)
                    tokens_out(b, "m_out", 1, inv, wout, RH)

            run(pe, attention, mixer)

        @block.scalar
        def _(act):
            s_ = nc.scalar
            act.wait_ge(prep_pe, 1)
            s_.copy(uT[0:RANK], ps[0:RANK, 0:2, :].rearrange("p a b -> p (a b)")).then_inc(prep_act, 1)
            act.wait_ge(prep_pe, 2)
            s_.copy(a1T[0:RANK], ps[0:RANK, 2:4, :].rearrange("p a b -> p (a b)")).then_inc(prep_act, 1)
            act.wait_ge(prep_dve, DVE_ABS)
            s_.activation(soft[:, 1, :], soft[:, 0, :], ACT.Exp).then_inc(prep_act, 1)
            act.wait_ge(prep_act, 3)
            s_.activation(soft[:, 2, :], soft[:, 1, :], ACT.Ln, bias=1.0).then_inc(prep_act, 1)
            act.wait_ge(prep_pe, 4)
            for c in range(DC):
                s_.copy(wfc[:, c, :], ps[:, 2 * c:2 * c + 2, :].rearrange("p a b -> p (a b)")).then_inc(prep_act, 1)
            act.wait_ge(prep_pe, 5)
            s_.copy(wpr[:].rearrange("p a b -> p (a b)"), ps[:, 4:8, :].rearrange("p a b -> p (a b)")
                    ).then_inc(prep_act, 1)
            act.wait_ge(prep_act, 7)
            act.wait_ge(zeroed, 3)
            for s in (a_scaled, a_xT, q_ready, v_ready, exped, pt_act, o_copied, attnT_ready, m_scaled, m_xT,
                      hid_relu, last_tap, pw_ready, qc_ready, folded, waved, y_tanh):
                act.sem_inc(s.sem, s.per_batch)
            act.sem_inc(set_up, 1)
            act.wait_ge(set_up, 4)

            def copy_T(b, tag, dst, ready):
                for c in range(DC):
                    name = f"{tag}{c}"
                    is_filled(act, b, name)
                    s_.copy(dst[:, c, :], out_of(name)).then_inc(*ready.one)
                    act.sem_inc(*drains(name))

            def scaled(b, tag, chain, src, dst, shift, n, done):
                act.wait_ge(*shift.at(b, n))
                for t in range(TT):
                    i = s_.activation(dst[:, t, :], src(t), ACT.Identity, scale=norms[:, chain, t, 9:10],
                                      bias=norms[:, chain, t, 10:11])
                i.then_inc(*done.one)

            def pair_of(tag):
                return lambda t: ps[:, bank(f"{tag}{t // 2}"), t % 2 * D:(t % 2 + 1) * D]

            def attention(b, item, n):
                if item == "xT":
                    copy_T(b, "xT", xTa, a_xT)
                if item == "proj" and n == 0:
                    for g in range(DC):
                        name = f"q{g}"
                        is_filled(act, b, name)
                        s_.activation(qpar[:, 0, g, :], out_of(name), ACT.Copy, scale=parity[:, 0:1])
                        s_.activation(qpar[:, 1, g, :], out_of(name), ACT.Copy, scale=parity[:, 1:2]
                                      ).then_inc(*q_ready.one)
                        act.wait_ge(*q_ready.last(b))
                        act.sem_inc(*drains(name))
                if item == "proj" and n == 1:
                    for g in range(2):
                        name = f"v{g}"
                        is_filled(act, b, name)
                        s_.copy(vaug[:, 2 * g:2 * g + 2, :, 0:HD],
                                out_of(name).rearrange("p (t h d) -> p t h d", t=2, h=NH)).then_inc(*v_ready.one)
                        act.wait_ge(*v_ready.last(b))
                        act.sem_inc(*drains(name))
                if item == "slot":
                    if n < 64:
                        nk = (HEADS[n][1] + 1) * P
                        act.wait_ge(*scored.at(b, n + 1))
                        if n >= 2:
                            is_filled(act, b, f"T{n - 2}")
                        s_.activation(pr[:, n % 2, 0:nk], sc[:, n % 2, 0:nk], ACT.Exp, scale=-1.0,
                                      bias=nmax[:, n:n + 1]).then_inc(*exped.one)
                    m = n - LAG_T
                    if 0 <= m < 64 and m % 2 == 0:
                        name, nk = f"T{m}", (HEADS[m][1] + 1) * P
                        is_filled(act, b, name)
                        if m >= 6:
                            act.wait_ge(*pv_done.at(b, (m - 6) // 4 + 1))
                        s_.copy(pt[:, m % 6, 0:nk], out_of(name)[:, 0:nk]).then_inc(*pt_act.one)
                        act.wait_ge(*pt_act.last(b))
                        act.sem_inc(*drains(name))
                    m = n - LAG_PV + 1
                    if m >= 0 and m % 16 == 12:
                        act.wait_ge(*pv_done.at(b, m // 4 + 1))
                        if m // 16:
                            is_filled(act, b, f"OT{m // 16 - 1}")
                        s_.copy(osb, ps[:, 5, :]).then_inc(*o_copied.one)
                if item == "attnT":
                    copy_T(b, "aT", xTa, attnT_ready)
                if item == "sum":
                    scaled(b, "y", 0, pair_of("y"), xna, a_shift, 1, a_scaled)
                    act.wait_ge(*a_scaled.last(b))
                    act.sem_inc(*drains("y0"))
                    act.sem_inc(*drains("y1"))

            def mixer(b, item, n):
                if item == "xT":
                    copy_T(b, ("m_xTa", "m_xTb", "m_xTc")[n], xTr, m_xT)
                if item in ("fc", "fc2"):
                    name = f"m_fc{n}" if item == "fc" else f"m_fd{n}"
                    is_filled(act, b, name)
                    s_.activation(hid[:, n, :], out_of(name), ACT.Relu,
                                  bias=zero[:, 0:1] if item == "fc" else b1c[:, n:n + 1]).then_inc(*hid_relu.one)
                    act.wait_ge(*hid_relu.last(b))
                    act.sem_inc(*drains(name))
                if item == "sum":
                    tag = ("m_proj", "m_out", None)[n]
                    if tag:
                        scaled(b, tag, 1, pair_of(tag), xnr, m_shift, n + 1, m_scaled)
                        act.wait_ge(*m_scaled.last(b))
                        act.sem_inc(*drains(f"{tag}0"))
                        act.sem_inc(*drains(f"{tag}1"))
                    else:
                        scaled(b, tag, 1, lambda t: xnr[:, t, :], xnr, m_shift, n + 1, m_scaled)
                if item == "z":
                    name = f"m_z{n}"
                    is_filled(act, b, name)
                    s_.activation(zc[:, n % 2, n // 2, :], out_of(name), ACT.Copy,
                                  scale=taps[:, n % 2, n // 2, KS - 1:KS]).then_inc(*last_tap.one)
                if item == "weights":
                    act.wait_ge(*logp_ready.at(b, 1))
                    s_.activation(zc[:, 1], zc[:, 1], ACT.Exp).then_inc(*pw_ready.one)
                if item == "query":
                    name = f"m_q{n}"
                    is_filled(act, b, name)
                    s_.copy(qc[:, n, :], out_of(name)).then_inc(*qc_ready.one)
                    act.wait_ge(*qc_ready.last(b))
                    act.sem_inc(*drains(name))
                if item == "wave":
                    r, slot = n, n % 3
                    act.wait_ge(*turned.at(b, r + 1))
                    if r >= 3:
                        act.wait_ge(*gathered.at(b, r - 2))
                    s_.activation(ring[:, slot, 0:MH], frac[:, r % 2], ACT.Abs).then_inc(*folded.one)
                    s_.activation(ring[:, slot, MH:2 * MH], frac[:, r % 2], ACT.Sin, scale=TWO_PI)
                    act.wait_ge(*folded.at(b, r + 1))
                    s_.activation(ring[:, slot, 0:MH], ring[:, slot, 0:MH], ACT.Sin, scale=-TWO_PI,
                                  bias=half_pi[:, 0:1]).then_inc(*waved.one)
                if item == "gate":
                    act.wait_ge(*y_raw.at(b, 1))
                    s_.activation(frac[:, 0], inv, ACT.Tanh, scale=0.5).then_inc(*y_tanh.one)

            run(act, attention, mixer)

        @block.vector
        def _(dve):
            v_ = nc.vector
            dve.wait_ge(loaded, 16 * n_loads[0])
            count = [0]

            def prep(instruction):
                count[0] += 1
                instruction.then_inc(prep_dve, 1)
                dve.wait_ge(prep_dve, count[0])

            prep(v_.tensor_scalar(soft[:, 0, :], slope, -1.0, None, ALU.mult))
            prep(v_.tensor_tensor(soft[:, 0, :], soft[:, 0, :], slope, ALU.min))
            assert count[0] == DVE_ABS
            for raw, n_row, n_col in ((raw_fc, HC, D), (raw_pr, DC, HID)):
                mag = tmp_a.rearrange("p (g i) -> p g i", g=n_row)
                low = tmp_b.rearrange("p (g i) -> p g i", g=n_row)
                scale, hi, lo = (rows[:, i, 0:n_row] for i in range(3))
                prep(v_.tensor_scalar(mag, raw, -1.0, None, ALU.mult))
                prep(v_.tensor_tensor(mag, mag, raw, ALU.max))
                prep(v_.tensor_reduce(scale, mag, AX.X, ALU.add))
                prep(v_.tensor_scalar(scale, scale, 1.0 / n_col, 1e-5, ALU.mult, ALU.max))
                prep(v_.tensor_scalar(hi, scale, 0.5, None, ALU.mult))
                prep(v_.tensor_scalar(lo, scale, -0.5, None, ALU.mult))
                for g in range(n_row):
                    v_.tensor_scalar(mag[:, g, :], raw[:, g, :], hi[:, g:g + 1], scale[:, g:g + 1], ALU.is_gt, ALU.mult)
                    prep(v_.tensor_scalar(low[:, g, :], raw[:, g, :], lo[:, g:g + 1], scale[:, g:g + 1],
                                          ALU.is_lt, ALU.mult))
                prep(v_.tensor_tensor(raw, mag, low, ALU.subtract))
            dve.wait_ge(prep_pe, 3)
            for g in range(HC):
                low_rank = ps[:, 4 + g // 2, g % 2 * D:(g % 2 + 1) * D]
                prep(v_.scalar_tensor_tensor(raw_fc[:, g, :], low_rank, gcol[:, 0:1], raw_fc[:, g, :],
                                             ALU.mult, ALU.add))
            assert count[0] == DVE_ROWS, count[0]
            for c in range(DC):
                for r in range(RH):
                    vals = raw_in[:, c, 0:D].rearrange("p (q r l h) -> p r l q h", q=KQ, r=RH, l=RL)[:, r]
                    v_.tensor_copy(wz[:, c, 0, r, :].rearrange("p (l q h) -> p l q h", l=RL, q=KQ), vals)
                    slots = raw_in[:, c, D:D + K].rearrange("p (q r l) -> p r l q", q=KQ, r=RH)[:, r]
                    prep(v_.tensor_copy(wz[:, c, 1, r, :].rearrange("p (l q h) -> p l q h", l=RL, q=KQ),
                                        slots[:, :, :, None].to_broadcast([P, RL, KQ, H])))
            v_.tensor_tensor(ab[:, 0, :], fac[:, 0, :], fac[:, 2, :], ALU.mult)
            prep(v_.tensor_tensor(ab[:, 1, :], fac[:, 1, :], fac[:, 3, :], ALU.mult))
            half = P * MH
            for c in range(DC):
                wide = raw_in[:, c, D + K:].rearrange("p (q h n l z) -> p z n l q h", q=KQ, h=H, n=MH, l=ML)
                for n in range(MH):
                    for l in range(ML):
                        re, im = wide[:, 0, n, l], wide[:, 1, n, l]
                        t = [tmp_a[:, i * W:(i + 1) * W].rearrange("p (q h) -> p q h", q=KQ) for i in range(4)]
                        fa, fb = (ab[:, i, None, :].to_broadcast([P, KQ, H]) for i in range(2))
                        v_.tensor_tensor(t[0], re, fa, ALU.mult)
                        v_.tensor_tensor(t[1], im, fb, ALU.mult)
                        v_.tensor_tensor(t[2], im, fa, ALU.mult)
                        prep(v_.tensor_tensor(t[3], re, fb, ALU.mult))
                        cols = [wqc[:, c, i, n, l * W:(l + 1) * W].rearrange("p (q h) -> p q h", q=KQ)
                                for i in range(2)]
                        v_.tensor_tensor(cols[0], t[0], t[1], ALU.subtract)
                        prep(v_.tensor_tensor(cols[1], t[2], t[3], ALU.add))
            prep(v_.tensor_scalar(wout[:], wout[:], 0.5, None, ALU.mult))
            prep(v_.tensor_scalar(turns[:], theta_raw, 1.0 / TWO_PI_EXACT, None, ALU.mult))
            dve.wait_ge(prep_act, 4)
            e, ln, d, one = soft[:, 1, :], soft[:, 2, :], soft[:, 3, :], soft[:, 4, :]
            prep(v_.tensor_scalar(d, e, 1.0, 1.0, ALU.add, ALU.subtract))
            prep(v_.tensor_scalar(one, d, 0.0, None, ALU.is_equal))
            prep(v_.tensor_tensor(d, d, one, ALU.add))
            prep(v_.reciprocal(d, d))
            prep(v_.tensor_tensor(ln, ln, d, ALU.mult))
            prep(v_.tensor_tensor(ln, ln, one, ALU.add))
            prep(v_.tensor_tensor(ln, ln, e, ALU.mult))
            prep(v_.tensor_scalar(one, slope, 0.0, None, ALU.max))
            prep(v_.tensor_tensor(ln, ln, one, ALU.add))
            for r in range(RH):
                prep(v_.tensor_scalar(logw[:, r, :], dist[:, r, :], ln[:, r:r + 1], None, ALU.mult))
            dve.wait_ge(prep_act, 7)
            prep(v_.memset(vaug, 0.0))
            prep(v_.memset(vaug[:, :, :, HD:HD + 1], 1.0))
            for s in (a_stats, a_shift, a_xn, ckv_ready, rope_ready, k_ready, scored, pt_dve, attn_ready, a_step,
                      m_stats, m_shift, m_xn, conv_done, logp_ready, turned, mixed, y_raw, y_ready, b2_added,
                      m_step) + tuple(d for d in drained if d.per_batch):
                dve.sem_inc(s.sem, s.per_batch)
            dve.sem_inc(set_up, 1)
            dve.wait_ge(set_up, 4)

            def step(b, own, instruction):
                instruction.then_inc(*own.one)
                dve.wait_ge(*own.last(b))

            def take_wait():
                dve.sem_inc(waits_taken, 1)

            def statistics(b, chain, own, src, stats):
                for t in range(TT):
                    i = v_.bn_stats(norms[:, chain, t, 0:6], src(t))
                i.then_inc(*own.one)
                dve.wait_ge(*own.last(b))
                take_wait()
                for t in range(TT):
                    i = v_.bn_aggr(norms[:, chain, t, 6:8], norms[:, chain, t, 0:6])
                step(b, own, i)
                v_.tensor_scalar(norms[:, chain, :, 8], norms[:, chain, :, 7], EPS, None, ALU.add
                                 ).then_inc(*stats.one)

            def normed(b, chain, src, dst, rstd, n, done):
                dve.wait_ge(*rstd.at(b, n))
                for t in range(TT):
                    i = v_.tensor_scalar(dst[:, t, :], src[:, t, :], norms[:, chain, t, 6:7],
                                         norms[:, chain, t, 9:10], ALU.subtract, ALU.mult)
                i.then_inc(*done.one)

            def shift(b, chain, rstd, n, done):
                dve.wait_ge(*rstd.at(b, n))
                v_.scalar_tensor_tensor(norms[:, chain, :, 10], norms[:, chain, :, 6], -1.0, norms[:, chain, :, 9],
                                        ALU.mult, ALU.mult).then_inc(*done.one)

            def pair_of(tag):
                return lambda t: ps[:, bank(f"{tag}{t // 2}"), t % 2 * D:(t % 2 + 1) * D]

            def rotate(b, plain, swapped, dst):
                is_filled(dve, b, plain)
                v_.tensor_tensor(rtmp[0:DR, 0, :], out_of(plain)[0:DR], rope[:, 0, :], ALU.mult
                                 ).then_inc(*drains(plain))
                is_filled(dve, b, swapped)
                v_.tensor_tensor(rtmp[0:DR, 1, :], out_of(swapped)[0:DR], rope[:, 1, :], ALU.mult
                                 ).then_inc(*drains(swapped))
                dve.wait_ge(*drained[bank(plain)].at(b, place[plain][1]))
                dve.wait_ge(*drained[bank(swapped)].at(b, place[swapped][1]))
                v_.tensor_tensor(dst[0:DR], rtmp[0:DR, 0, :], rtmp[0:DR, 1, :], ALU.add).then_inc(*rope_ready.one)
                dve.wait_ge(*rope_ready.last(b))

            def copied(b, name, dst, src, ready):
                is_filled(dve, b, name)
                v_.tensor_copy(dst, src).then_inc(*ready.one)
                dve.wait_ge(*ready.last(b))
                dve.sem_inc(*drains(name))

            def attn_out(b, g):
                name = f"OT{g}"
                o = out_of(name).rearrange("p (t j e) -> p t j e", t=TT, j=4)
                is_filled(dve, b, name)
                step(b, a_step, v_.reciprocal(rden, o[:, :, :, HD]))
                v_.tensor_tensor(att[:].rearrange("p t (g j e) -> p t g j e", g=4, j=4)[:, :, g], o[:, :, :, 0:HD],
                                 rden[:, :, :, None].to_broadcast([P, TT, 4, HD]), ALU.mult).then_inc(*attn_ready.one)
                dve.wait_ge(*attn_ready.last(b))
                dve.sem_inc(*drains(name))

            def attention(b, item, n):
                if item == "norm":
                    dve.wait_ge(*x_loaded.at(b, 1))
                    statistics(b, 0, a_step, lambda t: x_in[:, t, :], a_stats)
                    normed(b, 0, x_in, xna, a_rstd, 1, a_xn)
                if item == "proj" and n == 0:
                    copied(b, "ckv", ckv, out_of("ckv"), ckv_ready)
                    rotate(b, "qr", "qs", qrope)
                if item == "proj" and n == 1:
                    for g in range(DC):
                        copied(b, f"k{g}", kT[:, g, :], out_of(f"k{g}"), k_ready)
                    rotate(b, "kr", "ks", krope)
                if item == "base":
                    for t in range(TT):
                        name, at = f"base{t}", t * P
                        is_filled(dve, b, name)
                        if t:
                            v_.tensor_copy(base_of(t)[:, 0:at], out_of(name)[:, 0:at])
                        step(b, a_step, v_.tensor_tensor(base_of(t)[:, at:at + P], out_of(name)[:, at:at + P], mask[:],
                                                         ALU.add))
                        dve.sem_inc(*drains(name))
                if item == "slot":
                    if n < 64:
                        qt = HEADS[n][1]
                        nk, name = (qt + 1) * P, f"S{n}"
                        is_filled(dve, b, name)
                        if n >= 2:
                            dve.wait_ge(*exped.at(b, n - 1))
                        take_wait()
                        v_.tensor_tensor_reduce(sc[:, n % 2, 0:nk], out_of(name)[:, 0:nk], base_of(qt), -SCORE_SCALE,
                                                BIG, ALU.add, ALU.min, nmax[:, n:n + 1]).then_inc(*scored.one)
                        dve.wait_ge(*scored.last(b))
                        dve.sem_inc(*drains(name))
                    m = n - LAG_T
                    if 0 <= m < 64 and m % 2 == 1:
                        nk = (HEADS[m][1] + 1) * P
                        if m >= 6:
                            dve.wait_ge(*pv_done.at(b, (m - 6) // 4 + 1))
                        copied(b, f"T{m}", pt[:, m % 6, 0:nk], out_of(f"T{m}")[:, 0:nk], pt_dve)
                    if n >= LAG_OT and (n - LAG_OT) % 16 == 0:
                        attn_out(b, (n - LAG_OT) // 16)
                if item == "sum":
                    is_filled(dve, b, "y0")
                    is_filled(dve, b, "y1")
                    statistics(b, 0, a_step, pair_of("y"), a_stats)
                    shift(b, 0, a_rstd, 2, a_shift)

            def mixer(b, item, n):
                if item == "norm":
                    src = (xa, xr, xr)[n]
                    dve.wait_ge(*(a_sum.at(b, 1) if n == 0 else m_sum.at(b, n)))
                    statistics(b, 1, m_step, lambda t: src[:, t, :], m_stats)
                    normed(b, 1, src, xnr, m_rstd, 2 * n + 1, m_xn)
                if item == "sum":
                    tag = ("m_proj", "m_out", "m_prok")[n]
                    for h in range(2):
                        is_filled(dve, b, f"{tag}{h}")
                    if n < 2:
                        statistics(b, 1, m_step, pair_of(tag), m_stats)
                    else:
                        y = ps[:, 6:8, :].rearrange("p a (t d) -> p (a t) d", t=2)
                        v_.tensor_tensor(xnr[:], y, b2r[:, None, :].to_broadcast([P, TT, D]), ALU.add
                                         ).then_inc(*b2_added.one)
                        dve.wait_ge(*b2_added.last(b))
                        dve.sem_inc(*drains(f"{tag}0"))
                        dve.sem_inc(*drains(f"{tag}1"))
                        statistics(b, 1, m_step, lambda t: xnr[:, t, :], m_stats)
                    shift(b, 1, m_rstd, 2 * n + 2, m_shift)
                if item == "z":
                    name, kind, r = f"m_z{n}", n % 2, n // 2
                    dve.wait_ge(*last_tap.at(b, n + 1))
                    for j in range(KS - 2, -1, -1):
                        s = KS - 1 - j
                        i = v_.scalar_tensor_tensor(zc[:, kind, r, s:T], out_of(name)[:, 0:T - s],
                                                    taps[:, kind, r, j:j + 1], zc[:, kind, r, s:T], ALU.mult, ALU.add)
                        if j:
                            step(b, m_step, i)
                    i.then_inc(*conv_done.one)
                    dve.wait_ge(*conv_done.last(b))
                    dve.sem_inc(*drains(name))
                if item == "weights":
                    for r in range(RH):
                        i = v_.tensor_scalar(zc[:, 1, r, :], zc[:, 1, r, :], sscale[:, r:r + 1], 20.0, ALU.mult, ALU.min)
                    step(b, m_step, i)
                    v_.scalar_tensor_tensor(zc[:, 1], zc[:, 1], -20.0, logw[:], ALU.max, ALU.add
                                            ).then_inc(*logp_ready.one)
                if item == "query" and n == 3:
                    dve.wait_ge(*pw_ready.at(b, 1))
                    for r in range(RH):
                        i = v_.tensor_tensor_scan(inv[:, r, :], zero[:, 0:1].to_broadcast([P, T]), zc[:, 1, r, :], 0.0,
                                                  ALU.add, ALU.add)
                    step(b, m_step, i)
                    step(b, m_step, v_.tensor_scalar(inv, inv, 1e-4, None, ALU.max))
                    v_.reciprocal(inv, inv)
                if item == "turn":
                    r = n
                    dve.wait_ge(*kv_sent[r % RL].at(b, (r // RL + 1) * ML))
                    if r >= 2:
                        dve.wait_ge(*waved.at(b, r - 1))
                    vals = kvr[:, r % RL, :]
                    for m in range(MH):
                        i = v_.tensor_scalar(whole[:, m, :], vals, turns[:, r, m:m + 1], ROUND, ALU.mult, ALU.add)
                    step(b, m_step, i)
                    step(b, m_step, v_.tensor_scalar(whole, whole, ROUND, None, ALU.subtract))
                    for m in range(MH):
                        i = v_.scalar_tensor_tensor(frac[:, r % 2, m, :], vals, turns[:, r, m:m + 1], whole[:, m, :],
                                                    ALU.mult, ALU.subtract)
                    i.then_inc(*turned.one)
                    dve.wait_ge(*turned.last(b))
                if item == "scan":
                    r, slot = n, n % 3
                    dve.wait_ge(*weighed.at(b, r + 1))
                    if r == 0:
                        dve.wait_ge(*qc_ready.at(b, 4))
                    for j in range(2 * MH):
                        i = v_.tensor_tensor_scan(ring[:, slot, j, :], zero[:, 0:1].to_broadcast([P, T]),
                                                  ring[:, slot, j, :], 0.0, ALU.add, ALU.add)
                    step(b, m_step, i)
                    v_.tensor_tensor(ring[:, slot], ring[:, slot], qc, ALU.mult).then_inc(*mixed.one)
                if item == "gate":
                    dve.wait_ge(*gathered.at(b, REP))
                    v_.tensor_tensor(inv, ps[:, 6:8, :], inv, ALU.mult).then_inc(*y_raw.one)
                    dve.wait_ge(*y_raw.last(b))
                    dve.sem_inc(*drains("m_mem0"))
                    dve.sem_inc(*drains("m_mem1"))
                    dve.wait_ge(*y_tanh.at(b, 1))
                    v_.scalar_tensor_tensor(inv, frac[:, 0], 1.0, inv, ALU.add, ALU.mult).then_inc(*y_ready.one)

            run(dve, attention, mixer)

        for name, s in signals.items():
            assert s.given == 2 * s.per_batch, (name, s.given / 2, s.per_batch)


DVE_ABS = 2
DVE_ROWS = 2 + 7 + HC + 7 + DC + HC
TWO_PI_EXACT = 6.283185307179586

_INS = ["L0_attn_x", "L0_attn_W_kv_down", "L0_attn_W_k_up", "L0_attn_W_v_up", "L0_attn_W_q", "L0_attn_W_q_rope",
        "L0_attn_W_k_rope", "L0_attn_W_o", "L0_ffn_fast_b", "L0_ffn_w_fc", "L0_ffn_w_proj", "L0_ffn_u", "L0_ffn_v",
        "L0_ffn_gate", "L1_attn_W_in", "L1_attn_conv_k", "L1_attn_theta", "L1_attn_decay_slopes",
        "L1_attn_anchor_slopes", "L1_attn_score_scale", "L1_attn_W_re", "L1_attn_W_im", "L1_attn_norm_scale",
        "L1_attn_W_out", "L1_ffn_W1", "L1_ffn_b1", "L1_ffn_W2", "L1_ffn_b2"]


def tables(np):
    f32 = np.float32
    inv_freq = f32(1.0) / np.power(f32(10000.0), np.arange(0, DR, 2, dtype=f32) / f32(DR)).astype(f32)
    freqs = np.outer(np.arange(T, dtype=f32), inv_freq).astype(f32)
    cos, sin = np.cos(freqs).T, np.sin(freqs).T
    rope = np.stack([np.concatenate([cos, cos]), np.concatenate([-sin, sin])], axis=1).astype(f32)
    p = np.arange(P)
    mask = np.where(p[None, :] > p[:, None], f32(MASKED), f32(0.0)).astype(f32)
    parity = np.stack([(p // HD) % 2 == 0, (p // HD) % 2 == 1], axis=1).astype(f32)
    slot = (p[:, None] % W // H) * REP + np.arange(RH)[None, :] * RL + p[:, None] // W
    pos = np.arange(T, dtype=f32)[None, None, :]
    dist = np.where(slot[:, :, None] < N_DECAY, -(f32(T - 1) - pos), -pos).astype(f32)
    sel = (p[:, None] % W == np.arange(W)[None, :]).astype(f32)
    return {"ident": np.eye(P, dtype=f32), "rope": rope, "mask": mask, "parity": parity, "dist": dist, "sel": sel}


def kernel(**inputs):
    import numpy as np
    import concourse.bacc as bacc
    from concourse.bass_utils import run_bass_kernel_spmd

    nc = bacc.Bacc("TRN2", target_bir_lowering=False, num_devices=1)
    arrays, args = {}, []
    for name in _INS:
        a = np.ascontiguousarray(inputs[name])
        if a.ndim == 0:
            a = a.reshape(1, 1)
        arrays[f"in_{name}"] = a
    for name, a in tables(np).items():
        arrays[f"table_{name}"] = a
    for name, a in arrays.items():
        args.append(nc.dram_tensor(name, a.shape, mybir.dt.from_np(a.dtype), kind="ExternalInput").ap())
    args.append(nc.dram_tensor("out", (B, T, D), F32, kind="ExternalOutput").ap())
    sandwich_kernel(nc, *args)
    r = run_bass_kernel_spmd(nc, [arrays], core_ids=[0])
    return r.results[0]["out"]
```

```python
from contextlib import ExitStack

import concourse.bass as bass
from concourse import mybir

ALU = mybir.AluOpType
ACT = mybir.ActivationFunctionType
AX = mybir.AxisListType
F32 = mybir.dt.float32

P = 128
B, T, D = 8, 512, 256
TT = T // P
DC = D // P
NH, HD, DR = 16, 16, 32
HID = 1024
HC = HID // P
RANK = 16
K, KQ, H, M = 32, 4, 8, 8
REP = K // KQ
ML = 4
MH = M // ML
RL = 4
RH = REP // RL
W = KQ * H
KS = 4
N_DECAY = 28
EPS = 1e-5
SCORE_SCALE = 1.0 / float(HD + DR) ** 0.5
MASKED = -1e30
ROUND = 12582912.0
TWO_PI = 6.283185
HALF_PI = 1.5707963
BIG = 3.0e38

HEADS = [(n // 16, n // 4 % 4, n % 4) for n in range(64)]
LAG_T, LAG_PV, LAG_OT = 2, 7, 20
SLOTS = 64 + 6
HEAD = [("norm", 0), ("xT", 0), ("proj", 0), ("proj", 1), ("base", 0)]
BODY = [("slot", n) for n in range(SLOTS)] + [("attnT", 0), ("out", 0), ("sum", 0)]
MIXER = [(("norm", 0), 0), (("xT", 0), 4)] + [(("fc", g), 5 + g) for g in range(HC)] + \
        [(("proj", 0), 14), (("proj", 1), 16), (("sum", 0), 18), (("norm", 1), 20), (("xT", 1), 24)] + \
        [(("z", g), 25 + g) for g in range(4)] + [(("weights", 0), 30)] + \
        [(("query", g), 30 + g) for g in range(4)] + \
        [(("turn", 0), 34), (("turn", 1), 35), (("wave", 0), 35), (("inv", 0), 36)]
for _r in range(REP):
    _at = 37 + 2 * _r
    MIXER += [(("wave", _r + 1), _at)] * (_r + 1 < REP) + [(("scan", _r), _at)] + \
             [(("turn", _r + 2), _at + 1)] * (_r + 2 < REP) + [(("gather", _r), _at + 1)]
MIXER += [(("gate", 0), 53), (("out", 0), 55), (("sum", 1), 57), (("norm", 2), 59), (("xT", 2), 63)] + \
         [(("fc2", g), 64 + g) for g in range(HC)] + [(("proj2", 0), 73), (("proj2", 1), 75), (("sum", 2), 78)]
PREPARE = [(("ternary", g), 2 + 4 * g) for g in range(4)] + [(("prep", k), 20 + 3 * k) for k in range(16)] + \
          [(("tables", 0), 60)]


def weave(attention, other):
    order, other = [], list(other)
    for n, item in enumerate(attention):
        while other and other[0][1] <= n:
            order.append(("other", other.pop(0)[0]))
        order.append(("attention", item))
    return order + [("other", item) for item, _ in other]


def plan_banks():
    place, count = {}, [0] * 8

    def use(name, bank):
        count[bank] += 1
        place[name] = (bank, count[bank])

    for n, name in enumerate(("xT0", "xT1", "ckv", "q0", "q1", "qr", "qs", "k0", "k1", "kr", "ks", "v0", "v1")):
        use(name, n % 5)
    for t in range(TT):
        use(f"base{t}", (13 + t) % 5)
    for n in range(SLOTS):
        if n < 64:
            use(f"S{n}", n % 3)
        if LAG_T <= n < 64 + LAG_T:
            use(f"T{n - LAG_T}", 3 + n % 2)
        if n >= LAG_OT and (n - LAG_OT) % 16 == 0:
            use(f"OT{(n - LAG_OT) // 16}", n % 3)
    use("aT0", 3), use("aT1", 4)
    use("y0", 0), use("y1", 1)

    def pair(name):
        use(name + "0", 6), use(name + "1", 7)

    pair("m_xTa")
    for i in range(HC):
        use(f"m_fc{i}", 6 + i % 2)
    pair("m_proj"), pair("m_xTb")
    for i in range(4):
        use(f"m_z{i}", 6 + i % 2)
    for i in range(4):
        use(f"m_q{i}", 6 + i % 2)
    pair("m_mem"), pair("m_out"), pair("m_xTc")
    for i in range(HC):
        use(f"m_fd{i}", 6 + i % 2)
    pair("m_prok")
    return place, count


class Signal:

    def __init__(self, sem, per_batch, step=1):
        self.sem, self.per_batch, self.step, self.given = sem, per_batch, step, 0

    @property
    def one(self):
        self.given += 1
        return self.sem, self.step

    def at(self, b, n):
        return self.sem, (b * self.per_batch + (self.per_batch + n)) * self.step

    def last(self, b):
        return self.at(b, (self.given - 1) % self.per_batch + 1)


def sandwich_kernel(nc, x, w_kv_down, w_k_up, w_v_up, w_q, w_q_rope, w_k_rope, w_o, fast_b, w_fc, w_proj, u, v,
                    w_in_slots, w_in_re, w_in_im, w_out, w1, w2, small, factors, b2,
                    c_ident, c_rope, c_mask, c_dist, c_sel, out):
    place, bank_uses = plan_banks()
    with ExitStack() as ctx:
        def sb(name, shape):
            return ctx.enter_context(nc.sbuf_tensor(name, shape, F32))

        def sem(name):
            return ctx.enter_context(nc.semaphore(name))

        signals = {}

        def signal(name, per_batch, step=1):
            signals[name] = Signal(sem(name), per_batch, step)
            return signals[name]

        ident = sb("ident", [P, P])
        rope = sb("rope", [DR, 2, T])
        mask = sb("mask", [P, P])
        sel = sb("sel", [P, W])
        wkv = sb("wkv", [P, DC, P])
        wku = sb("wku", [P, D])
        wvu = sb("wvu", [P, D])
        wq = sb("wq", [P, DC, D])
        wqr = sb("wqr", [P, DC, 2, DR])
        wkr = sb("wkr", [P, 2, DR])
        wo = sb("wo", [P, DC, D])
        wfc = sb("wfc", [P, DC, HID])
        wpr = sb("wpr", [P, HC, D])
        wz = sb("wz", [P, DC, 2, RH, P])
        wqc = sb("wqc", [P, 2, DC, MH, P])
        wout = sb("wout", [P, RH, D])
        wf1 = sb("wf1", [P, DC, HID])
        wf2 = sb("wf2", [P, HC, D])
        b2r = sb("b2r", [P, D])
        logw = sb("logw", [P, RH, T])
        smalls = sb("smalls", [P, SMALL])
        at = [0]

        def column(*shape):
            n = 1
            for k in shape:
                n *= k
            ap = smalls[:, at[0]:at[0] + n]
            at[0] += n
            if len(shape) == 1:
                return ap
            names = "abcd"[:len(shape)]
            return ap.rearrange(f"p ({' '.join(names)}) -> p {' '.join(names)}", **dict(zip(names, shape)))

        b1c = column(HC)
        turns = column(REP, MH)
        taps = column(2, RH, KS)
        sscale = column(RH)
        slope = column(RH)
        parity = column(2)
        gcol = column(1)
        assert at[0] == SMALL, at[0]
        power = sb("power", [P, TT])
        half_pi = sb("half_pi", [P, 1])
        zero = sb("zero", [P, 1])

        x_in = sb("x_in", [P, TT, D])
        xa = sb("xa", [P, TT, D])
        xr = sb("xr", [P, TT, D])
        xna = sb("xna", [P, TT, D])
        xnr = sb("xnr", [P, TT, D])
        xTa = sb("xTa", [P, DC, T])
        xTr = sb("xTr", [P, DC, T])
        norms = sb("norms", [P, 2, TT, 11])

        words = 30544
        work = sb("work", [P, words])
        cut = [0]

        def part(*shape):
            n = 1
            for k in shape:
                n *= k
            ap = work[:, cut[0]:cut[0] + n]
            cut[0] += n
            assert cut[0] <= words, (cut[0], words)
            if len(shape) == 1:
                return ap
            names = "abcd"[:len(shape)]
            return ap.rearrange(f"p ({' '.join(names)}) -> p {' '.join(names)}", **dict(zip(names, shape)))

        qpar = part(2, DC, T)
        kT = part(DC, T)
        base = part(TT * (TT + 1) // 2 * P)
        vaug = part(TT, NH, 32)
        sc = part(2, T)
        pr = part(2, T)
        osb = part(T)
        nmax = part(64)
        rden = part(TT, 4)
        pt_at = cut[0]
        pt = part(6, T)
        cut[0] = pt_at
        ckv = part(T)
        qrope = part(T)
        krope = part(T)
        rtmp = part(2, T)
        cut[0] = mixer_at = pt_at + 6 * T
        zc = part(2, RH, T)
        kvr = part(RL, T)
        pwr = part(RL, T)
        qc = part(2 * MH, T)
        frac = part(2, MH, T)
        whole = part(MH, T)
        inv = part(RH, T)
        ring_at = cut[0]
        ring = part(3, 2 * MH, T)
        cut[0] = ring_at
        hid = part(HC, T)
        att = xna

        ps = ctx.enter_context(nc.psum_tensor("ps", [P, 8, 512], F32))

        filled = [signal(f"bank{i}_filled", n - (1 if i >= 6 else 0)) for i, n in enumerate(bank_uses)]
        drained = [signal(f"bank{i}_drained", n) for i, n in enumerate(bank_uses)]
        x_loaded = signal("x_loaded", 1, 16)
        a_stats = signal("a_stats", 2)
        a_rstd = signal("a_rstd", 2)
        a_shift = signal("a_shift", 1)
        a_xn = signal("a_xn", 1)
        a_sum = signal("a_sum", 1)
        rope_ready = signal("rope_ready", 2)
        exped = signal("exped", 64)
        pv_done = signal("pv_done", 16)
        o_copied = signal("o_copied", 4)
        a_step = signal("a_step", 8)
        m_stats = signal("m_stats", 6)
        m_rstd = signal("m_rstd", 6)
        m_shift = signal("m_shift", 3)
        m_scaled = signal("m_scaled", 1)
        m_xn = signal("m_xn", 3)
        m_sum = signal("m_sum", 3)
        hid_sq = signal("hid_sq", HC)
        last_tap = signal("last_tap", 4)
        logp_ready = signal("logp_ready", 1)
        pw_ready = signal("pw_ready", 1)
        kv_sent = [signal(f"kv{l}_sent", RH * ML, 16) for l in range(RL)]
        pw_sent = [signal(f"pw{l}_sent", RH * ML, 16) for l in range(RL)]
        turned = signal("turned", REP)
        folded = signal("folded", REP)
        waved = signal("waved", REP)
        weighed = signal("weighed", REP)
        mixed = signal("mixed", REP)
        gathered = signal("gathered", REP)
        inv_ready = signal("inv_ready", 1)
        y_tanh = signal("y_tanh", 1)
        y_ready = signal("y_ready", 1)
        stored = signal("stored", 1, 16)
        m_step = signal("m_step", 47)

        loaded_first = sem("loaded_first")
        loaded = sem("loaded")
        constants = sem("constants")
        values_blank = sem("values_blank")
        prep_step = sem("prep_step")
        prep_filled = [sem(f"prep_filled{i}") for i in range(2)]
        prep_drained = [sem(f"prep_drained{i}") for i in range(2)]
        prep_soft = sem("prep_soft")
        waits_taken = sem("waits_taken")

        cut[0] = mixer_at
        raw_fc = part(HC, D)
        raw_pr = part(DC, HID)
        tmp_a = part(2048)
        tmp_b = part(2048)
        raw_re = part(DC, MH, P)
        raw_im = part(DC, MH, P)
        raw_u = part(HC, RANK)
        raw_fb = part(RANK)
        raw_v = part(D)
        uT = part(2, 512)
        a1T = part(2, 512)
        rows = part(2, 3, 16)
        fac = part(4, P)
        soft = part(6, RH)
        dist = part(RH, T)

        def bank(name):
            return place[name][0]

        def out_of(name):
            return ps[:, bank(name), :]

        def may_fill(pe, b, name):
            i, n = place[name]
            pe.wait_ge(*drained[i].at(b, n - 1))

        def fills(name):
            return filled[bank(name)].one

        def drains(name):
            return drained[bank(name)].one

        def is_filled(eng, b, name):
            i, n = place[name]
            skipped = i >= 6 and n > place["m_mem0" if i == 6 else "m_mem1"][1]
            eng.wait_ge(*filled[i].at(b, n - skipped))

        def is_drained(eng, b, name):
            i, n = place[name]
            eng.wait_ge(*drained[i].at(b, n))

        def run(eng, attention, mixer, prepare, between):
            def both(b, order):
                for chain, (item, n) in order:
                    if chain == "other":
                        mixer(b - 1, item, n)
                    elif (item, n) in HEAD:
                        attention(b + 1, item, n)
                    else:
                        attention(b, item, n)

            for item, n in HEAD:
                attention(0, item, n)
            for chain, (item, n) in weave(BODY + HEAD, PREPARE):
                if chain == "other":
                    prepare(item, n)
                else:
                    attention(1 if (item, n) in HEAD else 0, item, n)
            between()
            with eng.Fori(1, B - 1) as b:
                both(b, weave(BODY + HEAD, MIXER))
            both(B - 1, weave(BODY, MIXER))
            for item, _ in MIXER:
                mixer(B - 1, *item)

        def base_of(t):
            return base[:, t * (t + 1) // 2 * P:(t + 1) * (t + 2) // 2 * P]

        n_first, n_rest = [0], [0]

        block = ctx.enter_context(nc.Block())

        @block.sync
        def _(sp):
            def load(dst, src, sem=loaded, count=n_rest):
                sp.dma_start(dst, src).then_inc(sem, 16)
                count[0] += 1

            def first(dst, src):
                load(dst, src, loaded_first, n_first)

            def load_x(b):
                sp.dma_start(x_in[:], x[bass.ds(b, 1)].rearrange("o (t p) d -> p (o t) d", p=P)
                             ).then_inc(*x_loaded.one)

            for s in [x_loaded, stored] + kv_sent + pw_sent:
                sp.sem_inc(s.sem, s.per_batch * s.step)
            load_x(0)
            first(ident[:], c_ident)
            first(smalls[:], small)
            first(wkv[:], w_kv_down.rearrange("(c p) n -> p c n", p=P))
            first(wq[:], w_q.rearrange("(c p) n -> p c n", p=P))
            rq, hr = w_q_rope.rearrange("(c p) n -> p c n", p=P), DR // 2
            first(wqr[:, :, 0, :], rq)
            first(wqr[:, :, 1, 0:hr], rq[:, :, hr:DR])
            first(wqr[:, :, 1, hr:DR], rq[:, :, 0:hr])
            first(wku[:], w_k_up)
            first(wkr[:, 0, :], w_k_rope)
            first(wkr[:, 1, 0:hr], w_k_rope[:, hr:DR])
            first(wkr[:, 1, hr:DR], w_k_rope[:, 0:hr])
            first(wvu[:], w_v_up)
            first(rope[:], c_rope)
            first(mask[:], c_mask)
            first(wo[:], w_o.rearrange("(c p) n -> p c n", p=P))
            load(raw_fc, w_fc.rearrange("(g p) i -> p g i", p=P))
            load(raw_pr, w_proj.rearrange("(g p) i -> p g i", p=P))
            load(raw_u, u.rearrange("(g p) r -> p g r", p=P))
            load(raw_fb[0:RANK], fast_b)
            load(raw_v[0:RANK], v)
            load(raw_re, w_in_re)
            load(raw_im, w_in_im)
            load(fac, factors)
            load(dist, c_dist)
            load(sel[:], c_sel)
            load(wz[:], w_in_slots)
            load(wout[:], w_out)
            load(wf1[:], w1.rearrange("(c p) n -> p c n", p=P))
            load(wf2[:], w2.rearrange("(c p) n -> p c n", p=P))
            load(b2r[:], b2)

            def attention(b, item, n):
                if item == "norm" and not isinstance(b, int) or item == "norm" and b > 0:
                    sp.wait_ge(*a_sum.at(b, 0))
                    load_x(b)

            def send(kind, l, r, dst, sent):
                for m in range(ML):
                    sp.dma_start(dst[m * W:(m + 1) * W, l, :], zc[l * W:(l + 1) * W, kind, r, :]
                                 ).then_inc(*sent[l].one)

            def mixer(b, item, n):
                if item == "query" and n == 0:
                    is_drained(sp, b, "m_z2")
                    send(0, 0, 0, kvr, kv_sent)
                    send(0, 1, 0, kvr, kv_sent)
                    sp.wait_ge(*pw_ready.at(b, 1))
                    for l in range(RL):
                        send(1, l, 0, pwr, pw_sent)
                        if l >= 2:
                            send(0, l, 0, kvr, kv_sent)
                if item == "scan" and n < RL:
                    sp.wait_ge(*turned.at(b, n + 1))
                    send(0, n, 1, kvr, kv_sent)
                    sp.wait_ge(*weighed.at(b, n + 1))
                    send(1, n, 1, pwr, pw_sent)
                if item == "sum" and n == 2:
                    sp.wait_ge(*m_sum.at(b, 3))
                    sp.dma_start(out[bass.ds(b, 1)].rearrange("o (t p) d -> p (o t) d", p=P), xr[:]
                                 ).then_inc(*stored.one)

            run(sp, attention, mixer, lambda item, n: None, lambda: None)
            sp.wait_ge(*stored.at(B - 1, 1))

        @block.gpsimd
        def _(pool):
            g = nc.gpsimd
            g.memset(power[:], -0.5).then_inc(constants, 1)
            g.memset(half_pi[:], HALF_PI).then_inc(constants, 1)
            g.memset(zero[:], 0.0).then_inc(constants, 1)
            pool.wait_ge(constants, 3)
            for s in (a_rstd, a_sum, m_rstd, m_sum, hid_sq, weighed):
                pool.sem_inc(s.sem, s.per_batch)

            def rsqrt(b, chain, stats, rstd, n):
                pool.wait_ge(*stats.at(b, n))
                g.tensor_tensor(norms[:, chain, :, 9], norms[:, chain, :, 8], power[:], ALU.pow).then_inc(*rstd.one)

            def attention(b, item, n):
                if item == "norm":
                    rsqrt(b, 0, a_stats, a_rstd, 1)
                if item == "sum":
                    rsqrt(b, 0, a_stats, a_rstd, 2)
                    is_drained(pool, b, "y0")
                    is_drained(pool, b, "y1")
                    pool.wait_ge(*m_sum.at(b, -2))
                    g.tensor_tensor(xa[:], x_in[:], xna[:], ALU.add).then_inc(*a_sum.one)

            def mixer(b, item, n):
                if item == "norm":
                    rsqrt(b, 1, m_stats, m_rstd, 2 * n + 1)
                if item == "fc":
                    is_drained(pool, b, f"m_fc{n}")
                    g.tensor_tensor(hid[:, n, :], hid[:, n, :], hid[:, n, :], ALU.mult).then_inc(*hid_sq.one)
                if item == "wave":
                    r, slot = n, n % 3
                    pool.wait_ge(*waved.at(b, r + 1))
                    pool.wait_ge(*pw_sent[r % RL].at(b, (r // RL + 1) * ML))
                    g.tensor_tensor(ring[:, slot], ring[:, slot],
                                    pwr[:, r % RL, None, :].to_broadcast([P, 2 * MH, T]), ALU.mult
                                    ).then_inc(*weighed.one)
                if item == "sum":
                    rsqrt(b, 1, m_stats, m_rstd, 2 * n + 2)
                    if n < 2:
                        tag = ("m_proj", "m_out")[n]
                        is_drained(pool, b, f"{tag}0")
                        is_drained(pool, b, f"{tag}1")
                    else:
                        pool.wait_ge(*m_scaled.at(b, 1))
                    if n == 0:
                        pool.wait_ge(*stored.at(b, 0))
                    g.tensor_tensor(xr[:], (xa if n == 0 else xr)[:], xnr[:], ALU.add).then_inc(*m_sum.one)

            run(pool, attention, mixer, lambda item, n: None, lambda: None)

        @block.tensor
        def _(pe):
            mm, tr = nc.tensor.matmul, nc.tensor.transpose
            for s in filled + drained + [pv_done, gathered]:
                if s.per_batch:
                    pe.sem_inc(s.sem, s.per_batch)
            pe.wait_ge(loaded_first, 16 * n_first[0])

            def transposes(b, tag, src):
                for c in range(DC):
                    name = f"{tag}{c}"
                    may_fill(pe, b, name)
                    for t in range(TT):
                        i = tr(ps[:, bank(name), t * P:(t + 1) * P], src[:, t, c * P:(c + 1) * P], ident[:])
                    i.then_inc(*fills(name))

            def product(b, name, dst, pairs):
                may_fill(pe, b, name)
                for j, (l, r) in enumerate(pairs):
                    i = mm(dst, l, r, start=j == 0, stop=j == len(pairs) - 1)
                i.then_inc(*fills(name))

            def tokens_out(b, tag, half, lhs, rhs, n_k):
                name = f"{tag}{half}"
                may_fill(pe, b, name)
                for t in range(2):
                    tt = 2 * half + t
                    for j in range(n_k):
                        i = mm(ps[:, bank(name), t * D:(t + 1) * D], lhs[:, j, tt * P:(tt + 1) * P],
                               rhs[:, j, :], start=j == 0, stop=j == n_k - 1)
                i.then_inc(*fills(name))

            xa_c = [xTa[:, c, :] for c in range(DC)]
            xm_c = [xTr[:, c, :] for c in range(DC)]

            def attention(b, item, n):
                if item == "xT":
                    pe.wait_ge(*a_xn.at(b, 1))
                    transposes(b, "xT", xna)
                if item == "proj" and n == 0:
                    is_drained(pe, b, "xT0")
                    is_drained(pe, b, "xT1")
                    product(b, "ckv", out_of("ckv"), [(wkv[:, c, :], xa_c[c]) for c in range(DC)])
                    for g in range(DC):
                        product(b, f"q{g}", out_of(f"q{g}"),
                                [(wq[:, c, g * P:(g + 1) * P], xa_c[c]) for c in range(DC)])
                    for s, name in enumerate(("qr", "qs")):
                        product(b, name, out_of(name)[0:DR], [(wqr[:, c, s, :], xa_c[c]) for c in range(DC)])
                if item == "proj" and n == 1:
                    is_drained(pe, b, "ckv")
                    for g in range(DC):
                        product(b, f"k{g}", out_of(f"k{g}"), [(wku[:, g * P:(g + 1) * P], ckv)])
                    for s, name in enumerate(("kr", "ks")):
                        product(b, name, out_of(name)[0:DR], [(wkr[:, s, :], ckv)])
                    for g in range(2):
                        name = f"v{g}"
                        may_fill(pe, b, name)
                        for t in range(2):
                            i = mm(ps[:, bank(name), t * D:(t + 1) * D],
                                   ckv[:, (2 * g + t) * P:(2 * g + t + 1) * P], wvu[:], start=True, stop=True)
                        i.then_inc(*fills(name))
                if item == "base":
                    pe.wait_ge(*rope_ready.at(b, 2))
                    for t in range(TT):
                        product(b, f"base{t}", out_of(f"base{t}")[:, 0:(t + 1) * P],
                                [(qrope[0:DR, t * P:(t + 1) * P], krope[0:DR, 0:(t + 1) * P])])
                    for name in ("q0", "q1", "k0", "k1", "v0", "v1"):
                        is_drained(pe, b, name)
                if item == "slot":
                    if n < 64:
                        hg, qt, j = HEADS[n]
                        i8, nk = hg % 2 * 4 + j, (qt + 1) * P
                        p0 = 32 * (i8 // 2)
                        product(b, f"S{n}", out_of(f"S{n}")[:, 0:nk],
                                [(qpar[p0:p0 + 32, i8 % 2, hg // 2, qt * P:(qt + 1) * P],
                                  kT[p0:p0 + 32, hg // 2, 0:nk])])
                    if LAG_T <= n < 64 + LAG_T:
                        m = n - LAG_T
                        name = f"T{m}"
                        may_fill(pe, b, name)
                        pe.wait_ge(*exped.at(b, m + 1))
                        for t in range(HEADS[m][1] + 1):
                            i = tr(ps[:, bank(name), t * P:(t + 1) * P], pr[:, m % 2, t * P:(t + 1) * P], ident[:])
                        i.then_inc(*fills(name))
                    m = n - LAG_PV + 1
                    if m >= 0 and m % 4 == 0 and m < 64:
                        hg, qt, _ = HEADS[m]
                        if qt == 0:
                            pe.wait_ge(*o_copied.at(b, hg))
                        is_drained(pe, b, f"T{m + 2}")
                        is_drained(pe, b, f"T{m + 3}")
                        for t in range(qt + 1):
                            for j in range(4):
                                i = mm(ps[32 * j:32 * j + 32, 5, qt * P:(qt + 1) * P],
                                       vaug[:, t, hg * 4 + j, :], pt[:, (m + j) % 6, t * P:(t + 1) * P],
                                       start=t == 0, stop=t == qt)
                        i.then_inc(*pv_done.one)
                    if n >= LAG_OT and (n - LAG_OT) % 16 == 0:
                        g = (n - LAG_OT) // 16
                        name = f"OT{g}"
                        may_fill(pe, b, name)
                        pe.wait_ge(*o_copied.at(b, g + 1))
                        for t in range(TT):
                            i = tr(ps[:, bank(name), t * P:(t + 1) * P], osb[:, t * P:(t + 1) * P], ident[:])
                        i.then_inc(*fills(name))
                if item == "attnT":
                    for g in range(4):
                        is_drained(pe, b, f"OT{g}")
                    transposes(b, "aT", att)
                if item == "out":
                    is_drained(pe, b, "aT0")
                    is_drained(pe, b, "aT1")
                    tokens_out(b, "y", 0, xTa, wo, DC)
                    tokens_out(b, "y", 1, xTa, wo, DC)

            def mixer(b, item, n):
                if item == "xT":
                    pe.wait_ge(*m_xn.at(b, n + 1))
                    transposes(b, ("m_xTa", "m_xTb", "m_xTc")[n], xnr)
                if item in ("fc", "fc2"):
                    tag, w, t = ("m_fc", wfc, "m_xTa") if item == "fc" else ("m_fd", wf1, "m_xTc")
                    if n == 0:
                        is_drained(pe, b, t + "0")
                        is_drained(pe, b, t + "1")
                    product(b, f"{tag}{n}", out_of(f"{tag}{n}"),
                            [(w[:, c, n * P:(n + 1) * P], xm_c[c]) for c in range(DC)])
                if item == "proj":
                    pe.wait_ge(*hid_sq.at(b, HC))
                    tokens_out(b, "m_proj", n, hid, wpr, HC)
                if item == "proj2":
                    is_drained(pe, b, "m_fd6")
                    is_drained(pe, b, "m_fd7")
                    tokens_out(b, "m_prok", n, hid, wf2, HC)
                if item == "z":
                    if n == 0:
                        is_drained(pe, b, "m_xTb0")
                        is_drained(pe, b, "m_xTb1")
                    product(b, f"m_z{n}", out_of(f"m_z{n}"),
                            [(wz[:, c, n % 2, n // 2, :], xm_c[c]) for c in range(DC)])
                if item == "query":
                    product(b, f"m_q{n}", out_of(f"m_q{n}"),
                            [(wqc[:, n // MH, c, n % MH, :], xm_c[c]) for c in range(DC)])
                if item == "gather":
                    name = f"m_mem{n // RL}"
                    if n % RL == 0:
                        may_fill(pe, b, name)
                    pe.wait_ge(*mixed.at(b, n + 1))
                    for j in range(2 * MH):
                        i = mm(ps[n % RL * W:(n % RL + 1) * W, bank(name), :], sel[:], ring[:, n % 3, j, :],
                               start=j == 0, stop=j == 2 * MH - 1)
                    i.then_inc(*gathered.one)
                if item == "out":
                    pe.wait_ge(*y_ready.at(b, 1))
                    tokens_out(b, "m_out", 0, inv, wout, RH)
                    tokens_out(b, "m_out", 1, inv, wout, RH)

            def prepare(item, n):
                if item != "prep":
                    return
                i, o = n % 2, ps[:, 6 + n % 2, :]
                if n == 0:
                    pe.wait_ge(loaded, 16 * n_rest[0])
                if n >= 2:
                    pe.wait_ge(prep_drained[i], n // 2)
                if n < 2:
                    for g in range(4):
                        k = tr(o[0:RANK, g * P:(g + 1) * P], raw_u[:, 4 * n + g, :], ident[:])
                elif n < 4:
                    k = mm(o[0:RANK], raw_fb[0:RANK, :], uT[0:RANK, n - 2, :], start=True, stop=True)
                elif n < 8:
                    if n == 4:
                        pe.wait_ge(prep_drained[1], 2)
                    for g in range(2):
                        c = (n - 4) * 2 + g
                        k = mm(o[:, g * D:(g + 1) * D], a1T[0:RANK, c // 4, c % 4 * P:(c % 4 + 1) * P],
                               raw_v[0:RANK, :], start=True, stop=True)
                elif n < 12:
                    pe.wait_ge(prep_drained[1], 4)
                    pe.wait_ge(prep_drained[0], 4)
                    c, half = (n - 8) // 2, n % 2
                    for g in range(4):
                        k = tr(o[:, g * P:(g + 1) * P], raw_fc[:, 4 * half + g, c * P:(c + 1) * P], ident[:])
                else:
                    for h in range(2):
                        for g in range(DC):
                            c = 2 * (n - 12) + h
                            k = tr(o[:, h * D + g * P:h * D + (g + 1) * P], raw_pr[:, g, c * P:(c + 1) * P], ident[:])
                k.then_inc(prep_filled[i], 1)

            def between():
                pe.wait_ge(prep_drained[0], 8)
                pe.wait_ge(prep_drained[1], 8)
                pe.wait_ge(prep_step, N_PREP)

            run(pe, attention, mixer, prepare, between)

        @block.scalar
        def _(act):
            s_ = nc.scalar
            for s in (exped, o_copied, m_scaled, last_tap, pw_ready, folded, waved, y_tanh):
                act.sem_inc(s.sem, s.per_batch)
            act.wait_ge(constants, 3)
            act.wait_ge(values_blank, 2)
            act.wait_ge(loaded_first, 16 * n_first[0])

            def copy_T(b, tag, dst):
                for c in range(DC):
                    name = f"{tag}{c}"
                    is_filled(act, b, name)
                    s_.copy(dst[:, c, :], out_of(name)).then_inc(*drains(name))

            def scaled(b, tag, chain, dst, shift, n):
                act.wait_ge(*shift.at(b, n))
                for t in range(TT):
                    name = f"{tag}{t // 2}"
                    i = s_.activation(dst[:, t, :], ps[:, bank(name), t % 2 * D:(t % 2 + 1) * D], ACT.Identity,
                                      scale=norms[:, chain, t, 9:10], bias=norms[:, chain, t, 10:11])
                    if t % 2:
                        i.then_inc(*drains(name))

            def attention(b, item, n):
                if item == "xT":
                    copy_T(b, "xT", xTa)
                if item == "proj" and n == 0:
                    for g in range(DC):
                        name = f"q{g}"
                        is_filled(act, b, name)
                        s_.activation(qpar[:, 0, g, :], out_of(name), ACT.Copy, scale=parity[:, 0:1])
                        s_.activation(qpar[:, 1, g, :], out_of(name), ACT.Copy, scale=parity[:, 1:2]
                                      ).then_inc(*drains(name))
                if item == "proj" and n == 1:
                    for g in range(2):
                        name = f"v{g}"
                        is_filled(act, b, name)
                        s_.copy(vaug[:, 2 * g:2 * g + 2, :, 0:HD],
                                out_of(name).rearrange("p (t h d) -> p t h d", t=2, h=NH)).then_inc(*drains(name))
                if item == "slot":
                    if n < 64:
                        nk = (HEADS[n][1] + 1) * P
                        is_drained(act, b, f"S{n}")
                        if n >= 2:
                            is_filled(act, b, f"T{n - 2}")
                        s_.activation(pr[:, n % 2, 0:nk], sc[:, n % 2, 0:nk], ACT.Exp, scale=-1.0,
                                      bias=nmax[:, n:n + 1]).then_inc(*exped.one)
                    m = n - LAG_T
                    if 0 <= m < 64 and m % 2 == 0:
                        name, nk = f"T{m}", (HEADS[m][1] + 1) * P
                        is_filled(act, b, name)
                        if m >= 6:
                            act.wait_ge(*pv_done.at(b, (m - 6) // 4 + 1))
                        s_.copy(pt[:, m % 6, 0:nk], out_of(name)[:, 0:nk]).then_inc(*drains(name))
                    m = n - LAG_PV + 1
                    if m >= 0 and m % 16 == 12:
                        act.wait_ge(*pv_done.at(b, m // 4 + 1))
                        if m // 16:
                            is_filled(act, b, f"OT{m // 16 - 1}")
                        s_.copy(osb, ps[:, 5, :]).then_inc(*o_copied.one)
                if item == "attnT":
                    copy_T(b, "aT", xTa)
                if item == "sum":
                    scaled(b, "y", 0, xna, a_shift, 1)

            def mixer(b, item, n):
                if item == "xT":
                    copy_T(b, ("m_xTa", "m_xTb", "m_xTc")[n], xTr)
                if item in ("fc", "fc2"):
                    name = f"m_fc{n}" if item == "fc" else f"m_fd{n}"
                    is_filled(act, b, name)
                    s_.activation(hid[:, n, :], out_of(name), ACT.Relu,
                                  bias=zero[:, 0:1] if item == "fc" else b1c[:, n:n + 1]).then_inc(*drains(name))
                if item == "sum" and n < 2:
                    scaled(b, ("m_proj", "m_out")[n], 1, xnr, m_shift, n + 1)
                if item == "sum" and n == 2:
                    act.wait_ge(*m_shift.at(b, 3))
                    for t in range(TT):
                        i = s_.activation(xnr[:, t, :], xnr[:, t, :], ACT.Identity, scale=norms[:, 1, t, 9:10],
                                          bias=norms[:, 1, t, 10:11])
                    i.then_inc(*m_scaled.one)
                if item == "z":
                    name = f"m_z{n}"
                    is_filled(act, b, name)
                    s_.activation(zc[:, n % 2, n // 2, :], out_of(name), ACT.Copy,
                                  scale=taps[:, n % 2, n // 2, KS - 1:KS]).then_inc(*last_tap.one)
                if item == "weights":
                    act.wait_ge(*logp_ready.at(b, 1))
                    s_.activation(zc[:, 1], zc[:, 1], ACT.Exp).then_inc(*pw_ready.one)
                if item == "query":
                    name = f"m_q{n}"
                    is_filled(act, b, name)
                    s_.copy(qc[:, n, :], out_of(name)).then_inc(*drains(name))
                if item == "wave":
                    r, slot = n, n % 3
                    act.wait_ge(*turned.at(b, r + 1))
                    if r >= 3:
                        act.wait_ge(*gathered.at(b, r - 2))
                    s_.activation(ring[:, slot, 0:MH], frac[:, r % 2], ACT.Abs).then_inc(*folded.one)
                    s_.activation(ring[:, slot, MH:2 * MH], frac[:, r % 2], ACT.Sin, scale=TWO_PI)
                    act.wait_ge(*folded.at(b, r + 1))
                    s_.activation(ring[:, slot, 0:MH], ring[:, slot, 0:MH], ACT.Sin, scale=-TWO_PI,
                                  bias=half_pi[:, 0:1]).then_inc(*waved.one)
                if item == "gate":
                    for h in range(RH):
                        is_drained(act, b, f"m_mem{h}")
                    s_.activation(frac[:, 0], inv, ACT.Tanh, scale=0.5).then_inc(*y_tanh.one)

            def prepare(item, n):
                if item == "ternary" and n == 0:
                    act.wait_ge(prep_step, 2)
                    s_.activation(soft[:, 1, :], soft[:, 0, :], ACT.Exp).then_inc(prep_soft, 1)
                    act.wait_ge(prep_soft, 1)
                    s_.activation(soft[:, 2, :], soft[:, 1, :], ACT.Ln, bias=1.0).then_inc(prep_soft, 1)
                if item == "prep" and not 4 <= n < 8:
                    i, o = n % 2, ps[:, 6 + n % 2, :]
                    act.wait_ge(prep_filled[i], n // 2 + 1)
                    if n < 2:
                        k = s_.copy(uT[0:RANK, n, :], o[0:RANK])
                    elif n < 4:
                        k = s_.copy(a1T[0:RANK, n - 2, :], o[0:RANK])
                    elif n < 12:
                        c, half = (n - 8) // 2, n % 2
                        k = s_.copy(wfc[:, c, half * 512:(half + 1) * 512], o)
                    else:
                        c = 2 * (n - 12)
                        k = s_.copy(wpr[:, c:c + 2, :].rearrange("p a b -> p (a b)"), o)
                    k.then_inc(prep_drained[i], 1)

            def between():
                act.wait_ge(loaded, 16 * n_rest[0])
                act.wait_ge(prep_step, N_PREP)
                act.wait_ge(prep_drained[0], 8)
                act.wait_ge(prep_drained[1], 8)

            run(act, attention, mixer, prepare, between)

        @block.vector
        def _(dve):
            v_ = nc.vector
            v_.memset(vaug, 0.0).then_inc(values_blank, 1)
            dve.wait_ge(values_blank, 1)
            v_.memset(vaug[:, :, :, HD:HD + 1], 1.0).then_inc(values_blank, 1)
            for s in (a_stats, a_shift, a_xn, rope_ready, a_step, m_stats, m_shift, m_xn, logp_ready, turned, mixed,
                      inv_ready, y_ready, m_step):
                dve.sem_inc(s.sem, s.per_batch)
            dve.wait_ge(values_blank, 2)

            def take_wait():
                dve.sem_inc(waits_taken, 1)

            def step(b, own, instruction):
                instruction.then_inc(*own.one)
                dve.wait_ge(*own.last(b))

            def statistics(b, chain, own, src, stats):
                for t in range(TT):
                    i = v_.bn_stats(norms[:, chain, t, 0:6], src(t))
                i.then_inc(*own.one)
                dve.wait_ge(*own.last(b))
                take_wait()
                for t in range(TT):
                    i = v_.bn_aggr(norms[:, chain, t, 6:8], norms[:, chain, t, 0:6])
                step(b, own, i)
                v_.tensor_scalar(norms[:, chain, :, 8], norms[:, chain, :, 7], EPS, None, ALU.add
                                 ).then_inc(*stats.one)

            def normed(b, chain, src, dst, rstd, n, done):
                dve.wait_ge(*rstd.at(b, n))
                for t in range(TT):
                    i = v_.tensor_scalar(dst[:, t, :], src[:, t, :], norms[:, chain, t, 6:7],
                                         norms[:, chain, t, 9:10], ALU.subtract, ALU.mult)
                i.then_inc(*done.one)

            def shift(b, chain, rstd, n, done):
                dve.wait_ge(*rstd.at(b, n))
                v_.scalar_tensor_tensor(norms[:, chain, :, 10], norms[:, chain, :, 6], -1.0, norms[:, chain, :, 9],
                                        ALU.mult, ALU.mult).then_inc(*done.one)

            def pair_of(tag):
                return lambda t: ps[:, bank(f"{tag}{t // 2}"), t % 2 * D:(t % 2 + 1) * D]

            def rotate(b, plain, swapped, dst):
                is_filled(dve, b, plain)
                v_.tensor_tensor(rtmp[0:DR, 0, :], out_of(plain)[0:DR], rope[:, 0, :], ALU.mult
                                 ).then_inc(*drains(plain))
                is_filled(dve, b, swapped)
                v_.tensor_tensor(rtmp[0:DR, 1, :], out_of(swapped)[0:DR], rope[:, 1, :], ALU.mult
                                 ).then_inc(*drains(swapped))
                is_drained(dve, b, plain)
                is_drained(dve, b, swapped)
                v_.tensor_tensor(dst[0:DR], rtmp[0:DR, 0, :], rtmp[0:DR, 1, :], ALU.add).then_inc(*rope_ready.one)
                dve.wait_ge(*rope_ready.last(b))

            def copied(b, name, dst, src):
                is_filled(dve, b, name)
                v_.tensor_copy(dst, src).then_inc(*drains(name))

            def attention(b, item, n):
                if item == "norm":
                    dve.wait_ge(*x_loaded.at(b, 1))
                    statistics(b, 0, a_step, lambda t: x_in[:, t, :], a_stats)
                    normed(b, 0, x_in, xna, a_rstd, 1, a_xn)
                if item == "proj" and n == 0:
                    if isinstance(b, int) and b == 0:
                        dve.wait_ge(loaded_first, 16 * n_first[0])
                    copied(b, "ckv", ckv, out_of("ckv"))
                    rotate(b, "qr", "qs", qrope)
                if item == "proj" and n == 1:
                    for g in range(DC):
                        copied(b, f"k{g}", kT[:, g, :], out_of(f"k{g}"))
                    rotate(b, "kr", "ks", krope)
                if item == "base":
                    for t in range(TT):
                        name, at = f"base{t}", t * P
                        is_filled(dve, b, name)
                        if t:
                            v_.tensor_copy(base_of(t)[:, 0:at], out_of(name)[:, 0:at])
                        v_.tensor_tensor(base_of(t)[:, at:at + P], out_of(name)[:, at:at + P], mask[:],
                                         ALU.add).then_inc(*drains(name))
                    for t in range(TT):
                        is_drained(dve, b, f"base{t}")
                if item == "slot":
                    if n < 64:
                        qt = HEADS[n][1]
                        nk, name = (qt + 1) * P, f"S{n}"
                        is_filled(dve, b, name)
                        if n >= 2:
                            dve.wait_ge(*exped.at(b, n - 1))
                        take_wait()
                        v_.tensor_tensor_reduce(sc[:, n % 2, 0:nk], out_of(name)[:, 0:nk], base_of(qt), -SCORE_SCALE,
                                                BIG, ALU.add, ALU.min, nmax[:, n:n + 1]).then_inc(*drains(name))
                    m = n - LAG_T
                    if 0 <= m < 64 and m % 2 == 1:
                        nk = (HEADS[m][1] + 1) * P
                        if m >= 6:
                            dve.wait_ge(*pv_done.at(b, (m - 6) // 4 + 1))
                        copied(b, f"T{m}", pt[:, m % 6, 0:nk], out_of(f"T{m}")[:, 0:nk])
                    if n >= LAG_OT and (n - LAG_OT) % 16 == 0:
                        g = (n - LAG_OT) // 16
                        name = f"OT{g}"
                        o = out_of(name).rearrange("p (t j e) -> p t j e", t=TT, j=4)
                        is_filled(dve, b, name)
                        step(b, a_step, v_.reciprocal(rden, o[:, :, :, HD]))
                        v_.tensor_tensor(att[:].rearrange("p t (g j e) -> p t g j e", g=4, j=4)[:, :, g],
                                         o[:, :, :, 0:HD], rden[:, :, :, None].to_broadcast([P, TT, 4, HD]), ALU.mult
                                         ).then_inc(*drains(name))
                if item == "sum":
                    is_filled(dve, b, "y0")
                    is_filled(dve, b, "y1")
                    statistics(b, 0, a_step, pair_of("y"), a_stats)
                    shift(b, 0, a_rstd, 2, a_shift)

            def mixer(b, item, n):
                if item == "norm":
                    src = (xa, xr, xr)[n]
                    dve.wait_ge(*(a_sum.at(b, 1) if n == 0 else m_sum.at(b, n)))
                    statistics(b, 1, m_step, lambda t: src[:, t, :], m_stats)
                    normed(b, 1, src, xnr, m_rstd, 2 * n + 1, m_xn)
                if item == "sum":
                    tag = ("m_proj", "m_out", "m_prok")[n]
                    for h in range(2):
                        is_filled(dve, b, f"{tag}{h}")
                    if n < 2:
                        statistics(b, 1, m_step, pair_of(tag), m_stats)
                    else:
                        for h in range(2):
                            name = f"{tag}{h}"
                            v_.tensor_tensor(xnr[:, 2 * h:2 * h + 2, :], out_of(name).rearrange("p (t d) -> p t d", t=2),
                                             b2r[:, None, :].to_broadcast([P, 2, D]), ALU.add).then_inc(*drains(name))
                        for h in range(2):
                            is_drained(dve, b, f"{tag}{h}")
                        statistics(b, 1, m_step, lambda t: xnr[:, t, :], m_stats)
                    shift(b, 1, m_rstd, 2 * n + 2, m_shift)
                if item == "z":
                    name, kind, r = f"m_z{n}", n % 2, n // 2
                    dve.wait_ge(*last_tap.at(b, n + 1))
                    for j in range(KS - 2, -1, -1):
                        s = KS - 1 - j
                        i = v_.scalar_tensor_tensor(zc[:, kind, r, s:T], out_of(name)[:, 0:T - s],
                                                    taps[:, kind, r, j:j + 1], zc[:, kind, r, s:T], ALU.mult, ALU.add)
                        if j:
                            step(b, m_step, i)
                    i.then_inc(*drains(name))
                if item == "weights":
                    is_drained(dve, b, "m_z1")
                    is_drained(dve, b, "m_z3")
                    for r in range(RH):
                        i = v_.tensor_scalar(zc[:, 1, r, :], zc[:, 1, r, :], sscale[:, r:r + 1], 20.0, ALU.mult, ALU.min)
                    step(b, m_step, i)
                    v_.scalar_tensor_tensor(zc[:, 1], zc[:, 1], -20.0, logw[:], ALU.max, ALU.add
                                            ).then_inc(*logp_ready.one)
                if item == "inv":
                    dve.wait_ge(*pw_ready.at(b, 1))
                    for r in range(RH):
                        i = v_.tensor_tensor_scan(inv[:, r, :], zero[:, 0:1].to_broadcast([P, T]), zc[:, 1, r, :], 0.0,
                                                  ALU.add, ALU.add)
                    step(b, m_step, i)
                    step(b, m_step, v_.tensor_scalar(inv, inv, 1e-4, None, ALU.max))
                    v_.reciprocal(inv, inv).then_inc(*inv_ready.one)
                if item == "turn":
                    r = n
                    dve.wait_ge(*kv_sent[r % RL].at(b, (r // RL + 1) * ML))
                    if r >= 1:
                        dve.wait_ge(*turned.at(b, r))
                    if r >= 2:
                        dve.wait_ge(*waved.at(b, r - 1))
                    vals = kvr[:, r % RL, :]
                    for m in range(MH):
                        i = v_.tensor_scalar(whole[:, m, :], vals, turns[:, r, m:m + 1], ROUND, ALU.mult, ALU.add)
                    step(b, m_step, i)
                    step(b, m_step, v_.tensor_scalar(whole, whole, ROUND, None, ALU.subtract))
                    for m in range(MH):
                        i = v_.scalar_tensor_tensor(frac[:, r % 2, m, :], vals, turns[:, r, m:m + 1], whole[:, m, :],
                                                    ALU.mult, ALU.subtract)
                    i.then_inc(*turned.one)
                if item == "scan":
                    r, slot = n, n % 3
                    dve.wait_ge(*weighed.at(b, r + 1))
                    if r == 0:
                        is_drained(dve, b, "m_q2")
                        is_drained(dve, b, "m_q3")
                    for j in range(2 * MH):
                        i = v_.tensor_tensor_scan(ring[:, slot, j, :], zero[:, 0:1].to_broadcast([P, T]),
                                                  ring[:, slot, j, :], 0.0, ALU.add, ALU.add)
                    step(b, m_step, i)
                    v_.tensor_tensor(ring[:, slot], ring[:, slot], qc, ALU.mult).then_inc(*mixed.one)
                if item == "gate":
                    dve.wait_ge(*inv_ready.at(b, 1))
                    for h in range(RH):
                        dve.wait_ge(*gathered.at(b, (h + 1) * RL))
                        v_.tensor_tensor(inv[:, h, :], out_of(f"m_mem{h}"), inv[:, h, :], ALU.mult
                                         ).then_inc(*drains(f"m_mem{h}"))
                    dve.wait_ge(*y_tanh.at(b, 1))
                    v_.scalar_tensor_tensor(inv, frac[:, 0], 1.0, inv, ALU.add, ALU.mult).then_inc(*y_ready.one)

            count = [0]

            def prep(instruction):
                count[0] += 1
                instruction.then_inc(prep_step, 1)
                dve.wait_ge(prep_step, count[0])

            def magnitudes(raw, k, n_row, n_col):
                mag = tmp_a.rearrange("p (g i) -> p g i", g=n_row)
                scale, hi, lo = (rows[:, k, i, 0:n_row] for i in range(3))
                prep(v_.tensor_scalar(mag, raw, -1.0, None, ALU.mult))
                prep(v_.tensor_tensor(mag, mag, raw, ALU.max))
                prep(v_.tensor_reduce(scale, mag, AX.X, ALU.add))
                prep(v_.tensor_scalar(scale, scale, 1.0 / n_col, 1e-5, ALU.mult, ALU.max))
                prep(v_.tensor_scalar(hi, scale, 0.5, None, ALU.mult))
                prep(v_.tensor_scalar(lo, scale, -0.5, None, ALU.mult))

            def ternary(raw, k, n_row):
                mag = tmp_a.rearrange("p (g i) -> p g i", g=n_row)
                low = tmp_b.rearrange("p (g i) -> p g i", g=n_row)
                scale, hi, lo = (rows[:, k, i, 0:n_row] for i in range(3))
                for g in range(n_row):
                    v_.tensor_scalar(mag[:, g, :], raw[:, g, :], hi[:, g:g + 1], scale[:, g:g + 1], ALU.is_gt, ALU.mult)
                    i = v_.tensor_scalar(low[:, g, :], raw[:, g, :], lo[:, g:g + 1], scale[:, g:g + 1],
                                         ALU.is_lt, ALU.mult)
                prep(i)
                prep(v_.tensor_tensor(raw, mag, low, ALU.subtract))

            def prepare(item, n):
                if item == "ternary" and n == 0:
                    dve.wait_ge(loaded, 16 * n_rest[0])
                    prep(v_.tensor_scalar(soft[:, 0, :], slope, -1.0, None, ALU.mult))
                    prep(v_.tensor_tensor(soft[:, 0, :], soft[:, 0, :], slope, ALU.min))
                    magnitudes(raw_fc, 0, HC, D)
                if item == "ternary" and n == 1:
                    ternary(raw_fc, 0, HC)
                if item == "ternary" and n == 2:
                    magnitudes(raw_pr, 1, DC, HID)
                if item == "ternary" and n == 3:
                    ternary(raw_pr, 1, DC)
                if item == "prep" and 4 <= n < 8:
                    i = n % 2
                    dve.wait_ge(prep_filled[i], n // 2 + 1)
                    for g in range(2):
                        c = (n - 4) * 2 + g
                        k = v_.scalar_tensor_tensor(raw_fc[:, c, :], ps[:, 6 + i, g * D:(g + 1) * D], gcol[:, 0:1],
                                                    raw_fc[:, c, :], ALU.mult, ALU.add)
                    k.then_inc(prep_drained[i], 1)
                if item == "tables":
                    v_.tensor_tensor(fac[:, 0, :], fac[:, 0, :], fac[:, 2, :], ALU.mult)
                    prep(v_.tensor_tensor(fac[:, 1, :], fac[:, 1, :], fac[:, 3, :], ALU.mult))
                    fa, fb = (fac[:, i, None, :].to_broadcast([P, DC * MH, P]) for i in range(2))
                    flat = [a.rearrange("p c m n -> p (c m) n") for a in (raw_re, raw_im, wqc[:, 0], wqc[:, 1])]
                    t0 = tmp_a[:, 0:DC * MH * P].rearrange("p (a n) -> p a n", n=P)
                    t1 = tmp_b[:, 0:DC * MH * P].rearrange("p (a n) -> p a n", n=P)
                    v_.tensor_tensor(t0, flat[0], fa, ALU.mult)
                    prep(v_.tensor_tensor(t1, flat[1], fb, ALU.mult))
                    prep(v_.tensor_tensor(flat[2], t0, t1, ALU.subtract))
                    v_.tensor_tensor(t0, flat[1], fa, ALU.mult)
                    prep(v_.tensor_tensor(t1, flat[0], fb, ALU.mult))
                    prep(v_.tensor_tensor(flat[3], t0, t1, ALU.add))
                    prep(v_.tensor_scalar(wout[:], wout[:], 0.5, None, ALU.mult))
                    prep(v_.tensor_scalar(turns, turns, 1.0 / TWO_PI_EXACT, None, ALU.mult))
                    dve.wait_ge(prep_soft, 2)
                    e, ln, d, one = soft[:, 1, :], soft[:, 2, :], soft[:, 3, :], soft[:, 4, :]
                    prep(v_.tensor_scalar(d, e, 1.0, 1.0, ALU.add, ALU.subtract))
                    prep(v_.tensor_scalar(one, d, 0.0, None, ALU.is_equal))
                    prep(v_.tensor_tensor(d, d, one, ALU.add))
                    prep(v_.reciprocal(d, d))
                    prep(v_.tensor_tensor(ln, ln, d, ALU.mult))
                    prep(v_.tensor_tensor(ln, ln, one, ALU.add))
                    prep(v_.tensor_tensor(ln, ln, e, ALU.mult))
                    prep(v_.tensor_scalar(one, slope, 0.0, None, ALU.max))
                    prep(v_.tensor_tensor(ln, ln, one, ALU.add))
                    for r in range(RH):
                        prep(v_.tensor_scalar(logw[:, r, :], dist[:, r, :], ln[:, r:r + 1], None, ALU.mult))
                    assert count[0] == N_PREP, count[0]

            def between():
                dve.wait_ge(prep_drained[0], 8)
                dve.wait_ge(prep_drained[1], 8)

            run(dve, attention, mixer, prepare, between)

        for name, s in signals.items():
            assert s.given == 3 * s.per_batch, (name, s.given / 3, s.per_batch)


N_PREP = 36
SMALL = HC + REP * MH + 2 * RH * KS + RH + RH + 2 + 1
TWO_PI_EXACT = 6.283185307179586


def tables(np):
    f32 = np.float32
    inv_freq = f32(1.0) / np.power(f32(10000.0), np.arange(0, DR, 2, dtype=f32) / f32(DR)).astype(f32)
    freqs = np.outer(np.arange(T, dtype=f32), inv_freq).astype(f32)
    cos, sin = np.cos(freqs).T, np.sin(freqs).T
    rope = np.stack([np.concatenate([cos, cos]), np.concatenate([-sin, sin])], axis=1).astype(f32)
    p = np.arange(P)
    mask = np.where(p[None, :] > p[:, None], f32(MASKED), f32(0.0)).astype(f32)
    parity = np.stack([(p // HD) % 2 == 0, (p // HD) % 2 == 1], axis=1).astype(f32)
    pos = np.arange(T, dtype=f32)[None, None, :]
    dist = np.where(slots(np)[:, :, None] < N_DECAY, -(f32(T - 1) - pos), -pos).astype(f32)
    sel = (p[:, None] % W == np.arange(W)[None, :]).astype(f32)
    return {"ident": np.eye(P, dtype=f32), "rope": rope, "mask": mask, "dist": dist, "sel": sel}, parity


def slots(np):
    p = np.arange(P)
    return (p[:, None] % W // H) * REP + np.arange(RH)[None, :] * RL + p[:, None] // W


def layout(np, a):
    p = np.arange(P)
    slot = slots(np)
    chan = slot * H + p[:, None] % H
    w_in = a["L1_attn_W_in"].reshape(DC, P, -1)
    by_slot = np.stack([w_in[:, :, chan.T], w_in[:, :, D + slot.T]], axis=2)
    kq, h, ml = p % W // H, p % H, p // W
    m = np.arange(MH)[None, :] * ML + ml[:, None]
    q0 = D + K + ((kq[:, None] * H + h[:, None]) * M + m) * 2
    conv = a["L1_attn_conv_k"][:, 0, :]
    slopes = np.concatenate([a["L1_attn_decay_slopes"], a["L1_attn_anchor_slopes"]])
    theta = a["L1_attn_theta"][0, 0]
    rep = np.arange(REP)
    turns = theta[kq[:, None, None] * REP + rep[None, :, None], h[:, None, None], m[:, None, :]]
    small = [a["L1_ffn_b1"].reshape(HC, P).T, turns.reshape(P, -1),
             np.stack([conv[:, chan], conv[:, D + slot]]).transpose(2, 0, 3, 1).reshape(P, -1),
             a["L1_attn_score_scale"][slot], slopes[slot], tables(np)[1],
             np.broadcast_to(a["L0_ffn_gate"].reshape(1, 1), (P, 1))]
    ns = a["L1_attn_norm_scale"]
    factors = np.stack([ns[h], ns[H + h], a["L1_attn_W_re"][h, h], a["L1_attn_W_im"][h, h]])
    return {
        "x": a["L0_attn_x"], "w_kv_down": a["L0_attn_W_kv_down"], "w_k_up": a["L0_attn_W_k_up"],
        "w_v_up": a["L0_attn_W_v_up"], "w_q": a["L0_attn_W_q"], "w_q_rope": a["L0_attn_W_q_rope"],
        "w_k_rope": a["L0_attn_W_k_rope"], "w_o": a["L0_attn_W_o"], "fast_b": a["L0_ffn_fast_b"],
        "w_fc": a["L0_ffn_w_fc"], "w_proj": a["L0_ffn_w_proj"], "u": a["L0_ffn_u"], "v": a["L0_ffn_v"],
        "w_in_slots": by_slot.transpose(1, 0, 2, 3, 4),
        "w_in_re": w_in[:, :, q0.T].transpose(1, 0, 2, 3),
        "w_in_im": w_in[:, :, q0.T + 1].transpose(1, 0, 2, 3),
        "w_out": a["L1_attn_W_out"][chan], "w1": a["L1_ffn_W1"], "w2": a["L1_ffn_W2"],
        "small": np.concatenate(small, axis=1), "factors": np.broadcast_to(factors[None], (P, 4, P)),
        "b2": np.broadcast_to(a["L1_ffn_b2"][None], (P, D)),
    }


def kernel(**inputs):
    import numpy as np
    import concourse.bacc as bacc
    from concourse.bass_utils import run_bass_kernel_spmd

    arrays = layout(np, {name: np.asarray(a) for name, a in inputs.items()})
    for name, a in tables(np)[0].items():
        arrays[f"table_{name}"] = a
    arrays = {name: np.ascontiguousarray(a) for name, a in arrays.items()}
    nc = bacc.Bacc("TRN2", target_bir_lowering=False, num_devices=1)
    args = [nc.dram_tensor(name, a.shape, mybir.dt.from_np(a.dtype), kind="ExternalInput").ap()
            for name, a in arrays.items()]
    args.append(nc.dram_tensor("out", (B, T, D), F32, kind="ExternalOutput").ap())
    sandwich_kernel(nc, *args)
    r = run_bass_kernel_spmd(nc, [arrays], core_ids=[0])
    return r.results[0]["out"]
```

```python
from contextlib import ExitStack

import concourse.bass as bass
from concourse import mybir

ALU = mybir.AluOpType
ACT = mybir.ActivationFunctionType
AX = mybir.AxisListType
F32 = mybir.dt.float32
BF16 = mybir.dt.bfloat16

P = 128
B, T, D = 8, 512, 256
TT = T // P
DC = D // P
NH, HD, DR = 16, 16, 32
HID = 1024
HC = HID // P
RANK = 16
K, KQ, H, M = 32, 4, 8, 8
REP = K // KQ
ML = 4
MH = M // ML
RL = 4
RH = REP // RL
W = KQ * H
KS = 4
N_DECAY = 28
EPS = 1e-5
SCORE_SCALE = 1.0 / float(HD + DR) ** 0.5
MASKED = -1e30
ROUND = 12582912.0
TWO_PI = 6.283185
HALF_PI = 1.5707963
BIG = 3.0e38

RUNS = (((0, 3), (0, 3)), ((0, 2), (1, 2)), ((0, 1), (2, 1)))
SROWS = 6 * HD

HEADS = [(n // 16, n // 4 % 4, n % 4) for n in range(64)]
LAG_T, LAG_PV, LAG_OT = 3, 8, 21
SLOTS = 64 + 6
HEAD = [("stats", 0), ("norm", 0), ("xT", 0), ("proj", 0), ("proj", 1), ("base", 0)]
ATTEND = [("slot", n) for n in range(SLOTS)] + [("attnT", 0), ("out", 0), ("ystats", 0), ("sum", 0)]
SQUARED = [("fstats", 0), ("fnorm", 0), ("fxT", 0)] + [("fc", g) for g in range(HC)] + \
          [("fproj", 0), ("fproj", 1), ("fystats", 0), ("fsum", 0)]
BODY = ATTEND + SQUARED
MIXER = [((item, n), ahead) for item, n, ahead in (
    ("stats", 1, 0), ("norm", 1, 0), ("xT", 1, 0), ("z", 0, 0), ("z", 1, 0), ("z", 2, 0), ("z", 3, 0),
    ("weights", 0, 0), ("query", 0, 0), ("query", 1, 2), ("query", 2, 2), ("query", 3, 2), ("turn", 0, 2),
    ("whole", 0, 2), ("frac", 0, 2), ("turn", 1, 2), ("whole", 1, 2), ("frac", 1, 2), ("wave", 0, 6),
    ("wave", 1, 12), ("scan", 0, 12), ("scan", 1, 12), ("mix", 0, 12), ("scan", 2, 12), ("scan", 3, 12),
    ("mix", 1, 12), ("turn", 2, 12), ("whole", 2, 12), ("frac", 2, 12), ("gather", 0, 13), ("wave", 2, 13),
    ("scan", 4, 14), ("scan", 5, 14), ("mix", 2, 14), ("scan", 6, 14), ("scan", 7, 15), ("mix", 3, 16),
    ("turn", 3, 16), ("whole", 3, 16), ("frac", 3, 16), ("gather", 1, 16), ("inv", 0, 16), ("wave", 3, 16),
    ("scan", 8, 16), ("scan", 9, 16), ("mix", 4, 17), ("scan", 10, 19), ("scan", 11, 19), ("mix", 5, 20),
    ("turn", 4, 20), ("whole", 4, 22), ("frac", 4, 23), ("gather", 2, 23), ("inv", 1, 23), ("wave", 4, 23),
    ("scan", 12, 24), ("scan", 13, 27), ("mix", 6, 28), ("scan", 14, 28), ("scan", 15, 28), ("mix", 7, 30),
    ("turn", 5, 30), ("whole", 5, 30), ("frac", 5, 30), ("gather", 3, 30), ("wave", 5, 31), ("scan", 16, 31),
    ("scan", 17, 32), ("mix", 8, 32), ("scan", 18, 32), ("scan", 19, 33), ("mix", 9, 34), ("turn", 6, 34),
    ("whole", 6, 34), ("frac", 6, 34), ("gather", 4, 34), ("wave", 6, 34), ("scan", 20, 34), ("scan", 21, 34),
    ("mix", 10, 35), ("scan", 22, 35), ("scan", 23, 35), ("mix", 11, 35), ("turn", 7, 35), ("whole", 7, 35),
    ("frac", 7, 36), ("gather", 5, 38), ("wave", 7, 38), ("scan", 24, 38), ("scan", 25, 38), ("mix", 12, 41),
    ("scan", 26, 41), ("scan", 27, 43), ("mix", 13, 44), ("gather", 6, 45), ("scan", 28, 45), ("scan", 29, 45),
    ("mix", 14, 46), ("scan", 30, 47), ("scan", 31, 47), ("mix", 15, 52), ("gather", 7, 53), ("gate", 0, 59),
    ("out", 0, 67), ("ystats", 1, 67), ("sum", 1, 70), ("stats", 2, 70), ("norm", 2, 70), ("xT", 2, 72),
    ("fc2", 0, 74), ("fc2", 1, 74), ("fc2", 2, 74), ("fc2", 3, 74), ("fc2", 4, 76), ("fc2", 5, 76), ("fc2", 6, 77),
    ("fc2", 7, 85), ("proj2", 0, 88), ("proj2", 1, 88), ("ystats", 2, 91), ("sum", 2, 94))]
PREPARE = [((item, n), ahead) for item, n, ahead in (
    ("ternary", 0, 0), ("ternary", 1, 0), ("ternary", 2, 0), ("ternary", 3, 0), ("prep", 0, 0), ("prep", 1, 0),
    ("prep", 2, 0), ("prep", 3, 0), ("prep", 4, 0), ("prep", 5, 0), ("prep", 6, 0), ("prep", 7, 0), ("prep", 8, 5),
    ("prep", 9, 8), ("prep", 10, 8), ("prep", 11, 8), ("prep", 12, 8), ("prep", 13, 8), ("prep", 14, 13),
    ("prep", 15, 28), ("tables", 0, 28))]


def weave(attention, other):
    order, other = [], list(other)
    for n, item in enumerate(attention):
        while other and other[0][1] <= n:
            order.append(("other", other.pop(0)[0]))
        order.append(("attention", item))
    return order + [("other", item) for item, _ in other]


def plan_banks():
    place, count = {}, [0] * 8

    def use(name, bank):
        count[bank] += 1
        place[name] = (bank, count[bank])

    for n, name in enumerate(("xT0", "xT1", "ckv", "q0", "q1", "qr", "qs", "k0", "k1", "kr", "ks", "v0", "v1")):
        use(name, n % 5)
    for t in range(TT):
        use(f"base{t}", (13 + t) % 5)
    for n in range(SLOTS):
        if n < 64:
            use(f"S{n}", n % 2)
        if LAG_T <= n < 64 + LAG_T:
            use(f"T{n - LAG_T}", 2 + n % 3)
        if n >= LAG_OT and (n - LAG_OT) % 16 == 0:
            use(f"OT{(n - LAG_OT) // 16}", n % 2)
    use("aT0", 3), use("aT1", 4)
    use("y0", 0), use("y1", 1)
    for n, name in enumerate(["fxT0", "fxT1"] + [f"fc{g}" for g in range(HC)] + ["fproj0", "fproj1"]):
        use(name, (n + 2) % 5)

    def pair(name):
        use(name + "0", 6), use(name + "1", 7)

    pair("m_xTb")
    for i in range(4):
        use(f"m_z{i}", 6 + i % 2)
    for i in range(4):
        use(f"m_q{i}", 6 + i % 2)
    pair("m_mem"), pair("m_out"), pair("m_xTc")
    for i in range(HC):
        use(f"m_fd{i}", 6 + i % 2)
    pair("m_prok")
    return place, count


class Signal:

    def __init__(self, sem, per_batch, step=1):
        self.sem, self.per_batch, self.step, self.given = sem, per_batch, step, 0

    @property
    def one(self):
        self.given += 1
        return self.sem, self.step

    def at(self, b, n):
        return self.sem, (b * self.per_batch + (self.per_batch + n)) * self.step

    def last(self, b):
        return self.at(b, (self.given - 1) % self.per_batch + 1)


def sandwich_kernel(nc, x, w_kv_down, w_k_up, w_v_up, w_q, w_q_rope, w_k_rope, w_o, fast_b, w_fc, w_proj, u, v,
                    w_in_slots, w_in_re, w_in_im, w_out, w1, w2, small, factors, b2,
                    c_ident, c_rope, c_mask, c_dist, c_sel, out, scratch):
    place, bank_uses = plan_banks()
    with ExitStack() as ctx:
        def sb(name, shape):
            return ctx.enter_context(nc.sbuf_tensor(name, shape, F32))

        def sem(name):
            return ctx.enter_context(nc.semaphore(name))

        signals = {}

        def signal(name, per_batch, step=1):
            signals[name] = Signal(sem(name), per_batch, step)
            return signals[name]

        ident = sb("ident", [P, P])
        rope = sb("rope", [DR, 2, T])
        mask = sb("mask", [P, P])
        sel = sb("sel", [P, W])
        wkv = sb("wkv", [P, DC, P])
        wku = sb("wku", [P, D])
        wvu = sb("wvu", [P, D])
        wq = sb("wq", [P, DC, D])
        wqr = sb("wqr", [P, DC, 2, DR])
        wkr = sb("wkr", [P, 2, DR])
        wo = sb("wo", [P, DC, D])
        wfc = sb("wfc", [P, DC, HID])
        wpr = sb("wpr", [P, HC, D])
        wz = sb("wz", [P, DC, 2, RH, P])
        wqc = sb("wqc", [P, 2, DC, MH, P])
        wout = sb("wout", [P, RH, D])
        wf1 = sb("wf1", [P, DC, HID])
        wf2 = sb("wf2", [P, HC, D])
        b2r = sb("b2r", [P, D])
        logw = sb("logw", [P, RH, T])
        smalls = sb("smalls", [P, SMALL])
        at = [0]

        def column(*shape):
            n = 1
            for k in shape:
                n *= k
            ap = smalls[:, at[0]:at[0] + n]
            at[0] += n
            if len(shape) == 1:
                return ap
            names = "abcd"[:len(shape)]
            return ap.rearrange(f"p ({' '.join(names)}) -> p {' '.join(names)}", **dict(zip(names, shape)))

        b1c = column(HC)
        turns = column(REP, MH)
        taps = column(2, RH, KS)
        sscale = column(RH)
        slope = column(RH)
        gcol = column(1)
        assert at[0] == SMALL, at[0]
        power = sb("power", [P, TT])
        half_pi = sb("half_pi", [P, 1])
        zero = sb("zero", [P, 1])

        x_in = sb("x_in", [P, TT, D])
        xa = sb("xa", [P, TT, D])
        xr = sb("xr", [P, TT, D])
        xna = sb("xna", [P, TT, D])
        xnr = sb("xnr", [P, TT, D])
        xTa = sb("xTa", [P, DC, T])
        xTr = sb("xTr", [P, DC, T])
        norms = sb("norms", [P, 2, TT, 11])

        words = 30544
        work = sb("work", [P, words])
        cut = [0]

        def part(*shape):
            n = 1
            for k in shape:
                n *= k
            ap = work[:, cut[0]:cut[0] + n]
            cut[0] += n
            assert cut[0] <= words, (cut[0], words)
            if len(shape) == 1:
                return ap
            names = "abcd"[:len(shape)]
            return ap.rearrange(f"p ({' '.join(names)}) -> p {' '.join(names)}", **dict(zip(names, shape)))

        stack_at = cut[0]
        stack = part(2 * 2 * 4 * T // 2).bitcast(BF16).rearrange("p (i k j t) -> p i k j t", i=2, k=2, j=4)
        cut[0] = stack_at + 2 * 4 * T // 2
        q_pieces = part(3 * DC * T // 2).bitcast(BF16).rearrange("p (c s t) -> p c s t", s=3, c=DC)
        cut[0] = stack_at + 2 * 2 * 4 * T // 2
        base = part(TT * (TT + 1) // 2 * P)
        vaug = part(TT, NH, 32)
        osb = part(T)
        nmax = part(64)
        rden = part(TT, 4)
        scores_at = cut[0]
        k_pieces = part(3 * DC * T // 2).bitcast(BF16).rearrange("p (c s t) -> p c s t", s=3, c=DC)
        cut[0] = scores_at
        sc = part(4, T)
        pt_at = cut[0]
        pt = part(6, T)
        cut[0] = scores_at
        squared = part(HC, T)
        cut[0] = pt_at
        ckv = part(T)
        qrope = part(T)
        krope = part(T)
        rtmp = part(2, T)
        cut[0] = mixer_at = pt_at + 6 * T
        zc = part(2, RH, T)
        kvr = part(RL, T)
        pwr = part(RL, T)
        qc = part(2 * MH, T)
        frac = part(2, MH, T)
        inv = part(RH, T)
        ring_at = cut[0]
        ring = part(3, 2 * MH, T)
        cut[0] = ring_at
        hid = part(HC, T)
        att = xna
        rest = xna[:].rearrange("p t d -> p (t d)").rearrange("p (c t) -> p c t", c=DC)

        ps = ctx.enter_context(nc.psum_tensor("ps", [P, 8, 512], F32))

        filled = [signal(f"bank{i}_filled", n - (1 if i >= 6 else 0)) for i, n in enumerate(bank_uses)]
        drained = [signal(f"bank{i}_drained", n) for i, n in enumerate(bank_uses)]
        x_loaded = signal("x_loaded", 1, 16)
        a_stats = signal("a_stats", 4)
        a_rstd = signal("a_rstd", 4)
        a_shift = signal("a_shift", 2)
        a_xn = signal("a_xn", 2)
        a_sum = signal("a_sum", 2)
        rope_ready = signal("rope_ready", 2)
        first_piece = signal("first_piece", 2 * DC)
        second_piece = signal("second_piece", 2 * DC)
        third_piece = signal("third_piece", 2 * DC)
        pieces_sent = signal("pieces_sent", 4, 16)
        stacked = [signal(f"stack{i}_loaded", 2 * 2 * len(RUNS), 16) for i in range(2)]
        exped = signal("exped", 64)
        pv_done = signal("pv_done", 16)
        o_copied = signal("o_copied", 4)
        a_step = signal("a_step", 12)
        m_stats = signal("m_stats", 4)
        m_rstd = signal("m_rstd", 4)
        m_shift = signal("m_shift", 2)
        m_scaled = signal("m_scaled", 1)
        m_xn = signal("m_xn", 2)
        m_sum = signal("m_sum", 2)
        hid_sq = signal("hid_sq", HC)
        last_tap = signal("last_tap", 4)
        logp_ready = signal("logp_ready", 1)
        pw_ready = signal("pw_ready", 1)
        kv_sent = [signal(f"kv{l}_sent", RH * ML, 16) for l in range(RL)]
        pw_sent = [signal(f"pw{l}_sent", RH * ML, 16) for l in range(RL)]
        turned = signal("turned", REP)
        folded = signal("folded", REP)
        waved = signal("waved", REP)
        weighed = signal("weighed", REP)
        mixed = signal("mixed", 2 * REP)
        gathered = signal("gathered", REP)
        inv_ready = signal("inv_ready", RH)
        y_tanh = signal("y_tanh", 1)
        y_ready = signal("y_ready", 1)
        stored = signal("stored", 1, 16)
        m_step = signal("m_step", 69)

        loaded_first = sem("loaded_first")
        loaded = sem("loaded")
        constants = sem("constants")
        values_blank = sem("values_blank")
        prep_step = sem("prep_step")
        prep_filled = [sem(f"prep_filled{i}") for i in range(2)]
        prep_drained = [sem(f"prep_drained{i}") for i in range(2)]
        prep_soft = sem("prep_soft")
        waits_taken = sem("waits_taken")

        cut[0] = mixer_at
        raw_fc = part(HC, D)
        raw_pr = part(DC, HID)
        tmp_a = part(2048)
        tmp_b = part(2048)
        raw_re = part(DC, MH, P)
        raw_im = part(DC, MH, P)
        raw_u = part(HC, RANK)
        raw_fb = part(RANK)
        raw_v = part(D)
        uT = part(2, 512)
        a1T = part(2, 512)
        rows = part(2, 3, 16)
        fac = part(4, P)
        soft = part(6, RH)
        dist = part(RH, T)

        def bank(name):
            return place[name][0]

        def out_of(name):
            return ps[:, bank(name), :]

        def may_fill(pe, b, name):
            i, n = place[name]
            pe.wait_ge(*drained[i].at(b, n - 1))

        def fills(name):
            return filled[bank(name)].one

        def drains(name):
            return drained[bank(name)].one

        def is_filled(eng, b, name):
            i, n = place[name]
            skipped = i >= 6 and n > place["m_mem0" if i == 6 else "m_mem1"][1]
            eng.wait_ge(*filled[i].at(b, n - skipped))

        def is_drained(eng, b, name):
            i, n = place[name]
            eng.wait_ge(*drained[i].at(b, n))

        def run(eng, attention, mixer, prepare, between):
            def both(b, order):
                for chain, (item, n) in order:
                    if chain == "other":
                        mixer(b - 1, item, n)
                    elif (item, n) in HEAD:
                        attention(b + 1, item, n)
                    else:
                        attention(b, item, n)

            for item, n in HEAD:
                attention(0, item, n)
            for chain, (item, n) in weave(ATTEND, PREPARE):
                if chain == "other":
                    prepare(item, n)
                else:
                    attention(0, item, n)
            between()
            for item, n in SQUARED:
                attention(0, item, n)
            for item, n in HEAD:
                attention(1, item, n)
            with eng.Fori(1, B - 1) as b:
                both(b, weave(BODY + HEAD, MIXER))
            both(B - 1, weave(BODY, MIXER))
            for item, _ in MIXER:
                mixer(B - 1, *item)

        def base_of(t):
            return base[:, t * (t + 1) // 2 * P:(t + 1) * (t + 2) // 2 * P]

        n_first, n_rest = [0], [0]

        block = ctx.enter_context(nc.Block())

        @block.sync
        def _(sp):
            def load(dst, src, sem=loaded, count=n_rest):
                sp.dma_start(dst, src).then_inc(sem, 16)
                count[0] += 1

            def first(dst, src):
                load(dst, src, loaded_first, n_first)

            def load_x(b):
                sp.dma_start(x_in[:], x[bass.ds(b, 1)].rearrange("o (t p) d -> p (o t) d", p=P)
                             ).then_inc(*x_loaded.one)

            def load_group(b, hg):
                i, at = hg % 2, 0
                for run in RUNS:
                    for kind in range(2):
                        s0, k = run[kind]
                        sp.dma_start(stack[at:at + k * HD, i, kind].rearrange("p j t -> p (j t)"),
                                     scratch[bass.ds(b, 1), kind, hg % 2, hg // 2, s0:s0 + k]
                                     .rearrange("o s (d j) t -> (o s d) (j t)", j=4)).then_inc(*stacked[i].one)
                    at += k * HD

            for s in [x_loaded, stored, pieces_sent] + stacked + kv_sent + pw_sent:
                sp.sem_inc(s.sem, s.per_batch * s.step)
            load_x(0)
            first(ident[:], c_ident)
            first(smalls[:], small)
            first(wkv[:], w_kv_down.rearrange("(c p) n -> p c n", p=P))
            first(wq[:], w_q.rearrange("(c p) n -> p c n", p=P))
            rq, hr = w_q_rope.rearrange("(c p) n -> p c n", p=P), DR // 2
            first(wqr[:, :, 0, :], rq)
            first(wqr[:, :, 1, 0:hr], rq[:, :, hr:DR])
            first(wqr[:, :, 1, hr:DR], rq[:, :, 0:hr])
            first(wku[:], w_k_up)
            first(wkr[:, 0, :], w_k_rope)
            first(wkr[:, 1, 0:hr], w_k_rope[:, hr:DR])
            first(wkr[:, 1, hr:DR], w_k_rope[:, 0:hr])
            first(wvu[:], w_v_up)
            first(rope[:], c_rope)
            first(mask[:], c_mask)
            first(wo[:], w_o.rearrange("(c p) n -> p c n", p=P))
            load(raw_fc, w_fc.rearrange("(g p) i -> p g i", p=P))
            load(raw_pr, w_proj.rearrange("(g p) i -> p g i", p=P))
            load(raw_u, u.rearrange("(g p) r -> p g r", p=P))
            load(raw_fb[0:RANK], fast_b)
            load(raw_v[0:RANK], v)
            load(raw_re, w_in_re)
            load(raw_im, w_in_im)
            load(fac, factors)
            load(dist, c_dist)
            load(sel[:], c_sel)
            load(wz[:], w_in_slots)
            load(wout[:], w_out)
            load(wf1[:], w1.rearrange("(c p) n -> p c n", p=P))
            load(wf2[:], w2.rearrange("(c p) n -> p c n", p=P))
            load(b2r[:], b2)

            def attention(b, item, n):
                if item == "stats" and not isinstance(b, int) or item == "stats" and b > 0:
                    sp.wait_ge(*a_sum.at(b, -1))
                    load_x(b)
                if item == "base":
                    sp.wait_ge(*third_piece.at(b, 2 * DC))
                    for kind, pieces in enumerate((q_pieces, k_pieces)):
                        for half in range(2):
                            r = half * 64
                            sp.dma_start(scratch[bass.ds(b, 1), kind, half].rearrange("o c s r t -> r (o c s) t"),
                                         pieces[r:r + 64].rearrange("p c s t -> p (c s) t")).then_inc(*pieces_sent.one)
                    sp.wait_ge(*pieces_sent.at(b, 4))
                    load_group(b, 0)
                    load_group(b, 1)
                if item == "slot" and n in (17, 33):
                    is_filled(sp, b, f"S{n - 2}")
                    load_group(b, n // 16 + 1)

            def send(kind, l, r, dst, sent):
                for m in range(ML):
                    sp.dma_start(dst[m * W:(m + 1) * W, l, :], zc[l * W:(l + 1) * W, kind, r, :]
                                 ).then_inc(*sent[l].one)

            def mixer(b, item, n):
                if item == "query" and n == 0:
                    is_drained(sp, b, "m_z2")
                    send(0, 0, 0, kvr, kv_sent)
                    send(0, 1, 0, kvr, kv_sent)
                    sp.wait_ge(*pw_ready.at(b, 1))
                    for l in range(RL):
                        send(1, l, 0, pwr, pw_sent)
                        if l >= 2:
                            send(0, l, 0, kvr, kv_sent)
                if item == "mix" and n % 2 and n < 2 * RL:
                    r = n // 2
                    sp.wait_ge(*turned.at(b, r + 1))
                    send(0, r, 1, kvr, kv_sent)
                    sp.wait_ge(*weighed.at(b, r + 1))
                    send(1, r, 1, pwr, pw_sent)
                if item == "sum" and n == 2:
                    sp.wait_ge(*m_sum.at(b, 2))
                    sp.dma_start(out[bass.ds(b, 1)].rearrange("o (t p) d -> p (o t) d", p=P), xr[:]
                                 ).then_inc(*stored.one)

            run(sp, attention, mixer, lambda item, n: None, lambda: None)
            sp.wait_ge(*stored.at(B - 1, 1))

        @block.gpsimd
        def _(pool):
            g_ = nc.gpsimd
            g_.memset(power[:], -0.5).then_inc(constants, 1)
            g_.memset(half_pi[:], HALF_PI).then_inc(constants, 1)
            g_.memset(zero[:], 0.0).then_inc(constants, 1)
            pool.wait_ge(constants, 3)
            for s in (a_rstd, a_sum, m_rstd, m_sum, hid_sq, weighed, second_piece, third_piece):
                pool.sem_inc(s.sem, s.per_batch)

            def rsqrt(b, chain, stats, rstd, n):
                pool.wait_ge(*stats.at(b, n))
                g_.tensor_tensor(norms[:, chain, :, 9], norms[:, chain, :, 8], power[:], ALU.pow).then_inc(*rstd.one)

            def attention(b, item, n):
                if item == "stats":
                    rsqrt(b, 0, a_stats, a_rstd, 1)
                if item == "proj":
                    for g in range(DC):
                        pieces, pick = (q_pieces, (1, 2)) if n == 0 else (k_pieces, (1, 0))
                        is_drained(pool, b, f"{'qk'[n]}{g}")
                        pool.sem_inc(waits_taken, 1)
                        g_.tensor_copy(pieces[:, g, pick[0], :], rest[:, g, :]).then_inc(*second_piece.one)
                        pool.wait_ge(*second_piece.last(b))
                        g_.tensor_tensor(pieces[:, g, pick[1], :], rest[:, g, :], pieces[:, g, pick[0], :],
                                         ALU.subtract).then_inc(*third_piece.one)
                if item == "ystats":
                    rsqrt(b, 0, a_stats, a_rstd, 2)
                if item == "sum":
                    is_drained(pool, b, "y0")
                    is_drained(pool, b, "y1")
                    pool.wait_ge(*m_sum.at(b, -1))
                    g_.tensor_tensor(xa[:], x_in[:], xna[:], ALU.add).then_inc(*a_sum.one)
                if item == "fstats":
                    rsqrt(b, 0, a_stats, a_rstd, 3)
                if item == "fc":
                    is_drained(pool, b, f"fc{n}")
                    g_.tensor_tensor(squared[:, n, :], squared[:, n, :], squared[:, n, :], ALU.mult
                                     ).then_inc(*hid_sq.one)
                if item == "fystats":
                    rsqrt(b, 0, a_stats, a_rstd, 4)
                if item == "fsum":
                    is_drained(pool, b, "fproj0")
                    is_drained(pool, b, "fproj1")
                    g_.tensor_tensor(xa[:], xa[:], xna[:], ALU.add).then_inc(*a_sum.one)

            def mixer(b, item, n):
                if item == "stats":
                    rsqrt(b, 1, m_stats, m_rstd, 2 * n - 1)
                if item == "ystats":
                    rsqrt(b, 1, m_stats, m_rstd, 2 * n)
                if item == "wave":
                    r, slot = n, n % 3
                    pool.wait_ge(*waved.at(b, r + 1))
                    pool.wait_ge(*pw_sent[r % RL].at(b, (r // RL + 1) * ML))
                    g_.tensor_tensor(ring[:, slot], ring[:, slot],
                                    pwr[:, r % RL, None, :].to_broadcast([P, 2 * MH, T]), ALU.mult
                                    ).then_inc(*weighed.one)
                if item == "sum":
                    if n == 1:
                        is_drained(pool, b, "m_out0")
                        is_drained(pool, b, "m_out1")
                        pool.wait_ge(*stored.at(b, 0))
                    else:
                        pool.wait_ge(*m_scaled.at(b, 1))
                    g_.tensor_tensor(xr[:], (xa if n == 1 else xr)[:], xnr[:], ALU.add).then_inc(*m_sum.one)

            run(pool, attention, mixer, lambda item, n: None, lambda: None)

        @block.tensor
        def _(pe):
            mm, tr = nc.tensor.matmul, nc.tensor.transpose
            for s in filled + drained + [pv_done, gathered]:
                if s.per_batch:
                    pe.sem_inc(s.sem, s.per_batch)
            pe.wait_ge(loaded_first, 16 * n_first[0])

            def transposes(b, tag, src):
                for c in range(DC):
                    name = f"{tag}{c}"
                    may_fill(pe, b, name)
                    for t in range(TT):
                        i = tr(ps[:, bank(name), t * P:(t + 1) * P], src[:, t, c * P:(c + 1) * P], ident[:])
                    i.then_inc(*fills(name))

            def product(b, name, dst, pairs):
                may_fill(pe, b, name)
                for j, (l, r) in enumerate(pairs):
                    i = mm(dst, l, r, start=j == 0, stop=j == len(pairs) - 1)
                i.then_inc(*fills(name))

            def tokens_out(b, tag, half, lhs, rhs, n_k):
                name = f"{tag}{half}"
                may_fill(pe, b, name)
                for t in range(2):
                    tt = 2 * half + t
                    for j in range(n_k):
                        i = mm(ps[:, bank(name), t * D:(t + 1) * D], lhs[:, j, tt * P:(tt + 1) * P],
                               rhs[:, j, :], start=j == 0, stop=j == n_k - 1)
                i.then_inc(*fills(name))

            xa_c = [xTa[:, c, :] for c in range(DC)]
            xm_c = [xTr[:, c, :] for c in range(DC)]

            def attention(b, item, n):
                if item == "xT":
                    pe.wait_ge(*a_xn.at(b, 1))
                    transposes(b, "xT", xna)
                if item == "proj" and n == 0:
                    is_drained(pe, b, "xT0")
                    is_drained(pe, b, "xT1")
                    product(b, "ckv", out_of("ckv"), [(wkv[:, c, :], xa_c[c]) for c in range(DC)])
                    for g in range(DC):
                        product(b, f"q{g}", out_of(f"q{g}"),
                                [(wq[:, c, g * P:(g + 1) * P], xa_c[c]) for c in range(DC)])
                    for s, name in enumerate(("qr", "qs")):
                        product(b, name, out_of(name)[0:DR], [(wqr[:, c, s, :], xa_c[c]) for c in range(DC)])
                if item == "proj" and n == 1:
                    is_drained(pe, b, "ckv")
                    for g in range(DC):
                        product(b, f"k{g}", out_of(f"k{g}"), [(wku[:, g * P:(g + 1) * P], ckv)])
                    for s, name in enumerate(("kr", "ks")):
                        product(b, name, out_of(name)[0:DR], [(wkr[:, s, :], ckv)])
                    for g in range(2):
                        name = f"v{g}"
                        may_fill(pe, b, name)
                        for t in range(2):
                            i = mm(ps[:, bank(name), t * D:(t + 1) * D],
                                   ckv[:, (2 * g + t) * P:(2 * g + t + 1) * P], wvu[:], start=True, stop=True)
                        i.then_inc(*fills(name))
                if item == "base":
                    pe.wait_ge(*rope_ready.at(b, 2))
                    for t in range(TT):
                        product(b, f"base{t}", out_of(f"base{t}")[:, 0:(t + 1) * P],
                                [(qrope[0:DR, t * P:(t + 1) * P], krope[0:DR, 0:(t + 1) * P])])
                    for name in ("v0", "v1"):
                        is_drained(pe, b, name)
                if item == "slot":
                    if n < 64:
                        hg, qt, j = HEADS[n]
                        if n % 16 == 0:
                            pe.wait_ge(*stacked[hg % 2].at(b, (hg // 2 + 1) * 2 * len(RUNS)))
                        nk = (qt + 1) * P
                        product(b, f"S{n}", out_of(f"S{n}")[:, 0:nk],
                                [(stack[0:SROWS, hg % 2, 0, j, qt * P:(qt + 1) * P],
                                  stack[0:SROWS, hg % 2, 1, j, 0:nk])])
                    if LAG_T <= n < 64 + LAG_T:
                        m = n - LAG_T
                        name = f"T{m}"
                        may_fill(pe, b, name)
                        pe.wait_ge(*exped.at(b, m + 1))
                        for t in range(HEADS[m][1] + 1):
                            i = tr(ps[:, bank(name), t * P:(t + 1) * P], sc[:, m % 4, t * P:(t + 1) * P], ident[:])
                        i.then_inc(*fills(name))
                    m = n - LAG_PV + 1
                    if m >= 0 and m % 4 == 0 and m < 64:
                        hg, qt, _ = HEADS[m]
                        if qt == 0:
                            pe.wait_ge(*o_copied.at(b, hg))
                        is_drained(pe, b, f"T{m + 2}")
                        is_drained(pe, b, f"T{m + 3}")
                        for t in range(qt + 1):
                            for j in range(4):
                                i = mm(ps[32 * j:32 * j + 32, 5, qt * P:(qt + 1) * P],
                                       vaug[:, t, hg * 4 + j, :], pt[:, (m + j) % 6, t * P:(t + 1) * P],
                                       start=t == 0, stop=t == qt)
                        i.then_inc(*pv_done.one)
                    if n >= LAG_OT and (n - LAG_OT) % 16 == 0:
                        g = (n - LAG_OT) // 16
                        name = f"OT{g}"
                        may_fill(pe, b, name)
                        pe.wait_ge(*o_copied.at(b, g + 1))
                        for t in range(TT):
                            i = tr(ps[:, bank(name), t * P:(t + 1) * P], osb[:, t * P:(t + 1) * P], ident[:])
                        i.then_inc(*fills(name))
                if item == "attnT":
                    is_drained(pe, b, "OT3")
                    transposes(b, "aT", att)
                if item == "out":
                    is_drained(pe, b, "aT0")
                    is_drained(pe, b, "aT1")
                    tokens_out(b, "y", 0, xTa, wo, DC)
                    tokens_out(b, "y", 1, xTa, wo, DC)
                if item == "fxT":
                    pe.wait_ge(*a_xn.at(b, 2))
                    transposes(b, "fxT", xna)
                if item == "fc":
                    if n == 0:
                        is_drained(pe, b, "fxT0")
                        is_drained(pe, b, "fxT1")
                    product(b, f"fc{n}", out_of(f"fc{n}"),
                            [(wfc[:, c, n * P:(n + 1) * P], xa_c[c]) for c in range(DC)])
                if item == "fproj":
                    pe.wait_ge(*hid_sq.at(b, HC))
                    tokens_out(b, "fproj", n, squared, wpr, HC)

            def mixer(b, item, n):
                if item == "xT":
                    pe.wait_ge(*m_xn.at(b, n))
                    transposes(b, ("m_xTb", "m_xTc")[n - 1], xnr)
                if item == "fc2":
                    if n == 0:
                        is_drained(pe, b, "m_xTc0")
                        is_drained(pe, b, "m_xTc1")
                    product(b, f"m_fd{n}", out_of(f"m_fd{n}"),
                            [(wf1[:, c, n * P:(n + 1) * P], xm_c[c]) for c in range(DC)])
                if item == "proj2":
                    is_drained(pe, b, "m_fd6")
                    is_drained(pe, b, "m_fd7")
                    tokens_out(b, "m_prok", n, hid, wf2, HC)
                if item == "z":
                    if n == 0:
                        is_drained(pe, b, "m_xTb0")
                        is_drained(pe, b, "m_xTb1")
                    product(b, f"m_z{n}", out_of(f"m_z{n}"),
                            [(wz[:, c, n % 2, n // 2, :], xm_c[c]) for c in range(DC)])
                if item == "query":
                    product(b, f"m_q{n}", out_of(f"m_q{n}"),
                            [(wqc[:, n // MH, c, n % MH, :], xm_c[c]) for c in range(DC)])
                if item == "gather":
                    name = f"m_mem{n // RL}"
                    if n % RL == 0:
                        may_fill(pe, b, name)
                    for j in range(2 * MH):
                        if j % MH == 0:
                            pe.wait_ge(*mixed.at(b, 2 * n + j // MH + 1))
                        i = mm(ps[n % RL * W:(n % RL + 1) * W, bank(name), :], sel[:], ring[:, n % 3, j, :],
                               start=j == 0, stop=j == 2 * MH - 1)
                    i.then_inc(*gathered.one)
                if item == "out":
                    pe.wait_ge(*y_ready.at(b, 1))
                    tokens_out(b, "m_out", 0, inv, wout, RH)
                    tokens_out(b, "m_out", 1, inv, wout, RH)

            def prepare(item, n):
                if item != "prep":
                    return
                i, o = n % 2, ps[:, 6 + n % 2, :]
                if n == 0:
                    pe.wait_ge(loaded, 16 * n_rest[0])
                if n >= 2:
                    pe.wait_ge(prep_drained[i], n // 2)
                if n < 2:
                    for g in range(4):
                        k = tr(o[0:RANK, g * P:(g + 1) * P], raw_u[:, 4 * n + g, :], ident[:])
                elif n < 4:
                    k = mm(o[0:RANK], raw_fb[0:RANK, :], uT[0:RANK, n - 2, :], start=True, stop=True)
                elif n < 8:
                    if n == 4:
                        pe.wait_ge(prep_drained[1], 2)
                    for g in range(2):
                        c = (n - 4) * 2 + g
                        k = mm(o[:, g * D:(g + 1) * D], a1T[0:RANK, c // 4, c % 4 * P:(c % 4 + 1) * P],
                               raw_v[0:RANK, :], start=True, stop=True)
                elif n < 12:
                    pe.wait_ge(prep_drained[1], 4)
                    pe.wait_ge(prep_drained[0], 4)
                    c, half = (n - 8) // 2, n % 2
                    for g in range(4):
                        k = tr(o[:, g * P:(g + 1) * P], raw_fc[:, 4 * half + g, c * P:(c + 1) * P], ident[:])
                else:
                    for h in range(2):
                        for g in range(DC):
                            c = 2 * (n - 12) + h
                            k = tr(o[:, h * D + g * P:h * D + (g + 1) * P], raw_pr[:, g, c * P:(c + 1) * P], ident[:])
                k.then_inc(prep_filled[i], 1)

            def between():
                pe.wait_ge(prep_drained[0], 8)
                pe.wait_ge(prep_drained[1], 8)
                pe.wait_ge(prep_step, N_PREP)

            run(pe, attention, mixer, prepare, between)

        @block.scalar
        def _(act):
            s_ = nc.scalar
            for s in (first_piece, exped, o_copied, m_scaled, last_tap, pw_ready, folded, waved, y_tanh):
                act.sem_inc(s.sem, s.per_batch)
            act.wait_ge(constants, 3)
            act.wait_ge(values_blank, 2)
            act.wait_ge(loaded_first, 16 * n_first[0])

            def copy_T(b, tag, dst):
                for c in range(DC):
                    name = f"{tag}{c}"
                    is_filled(act, b, name)
                    s_.copy(dst[:, c, :], out_of(name)).then_inc(*drains(name))

            def scaled(b, tag, chain, dst, shift, n):
                act.wait_ge(*shift.at(b, n))
                for t in range(TT):
                    name = f"{tag}{t // 2}"
                    i = s_.activation(dst[:, t, :], ps[:, bank(name), t % 2 * D:(t % 2 + 1) * D], ACT.Identity,
                                      scale=norms[:, chain, t, 9:10], bias=norms[:, chain, t, 10:11])
                    if t % 2:
                        i.then_inc(*drains(name))

            def attention(b, item, n):
                if item == "xT":
                    copy_T(b, "xT", xTa)
                if item == "proj" and n == 0:
                    for g in range(DC):
                        name = f"q{g}"
                        is_filled(act, b, name)
                        s_.copy(q_pieces[:, g, 0, :], out_of(name)).then_inc(*first_piece.one)
                if item == "proj" and n == 1:
                    for g in range(DC):
                        name = f"k{g}"
                        is_filled(act, b, name)
                        s_.copy(k_pieces[:, g, 2, :], out_of(name)).then_inc(*first_piece.one)
                    for g in range(2):
                        name = f"v{g}"
                        is_filled(act, b, name)
                        s_.copy(vaug[:, 2 * g:2 * g + 2, :, 0:HD],
                                out_of(name).rearrange("p (t h d) -> p t h d", t=2, h=NH)).then_inc(*drains(name))
                if item == "slot":
                    if n < 64:
                        nk = (HEADS[n][1] + 1) * P
                        is_drained(act, b, f"S{n}")
                        s_.activation(sc[:, n % 4, 0:nk], sc[:, n % 4, 0:nk], ACT.Exp, scale=-1.0,
                                      bias=nmax[:, n:n + 1]).then_inc(*exped.one)
                    m = n - LAG_T
                    if 0 <= m < 64 and m % 2 == 0:
                        name, nk = f"T{m}", (HEADS[m][1] + 1) * P
                        is_filled(act, b, name)
                        if m >= 6:
                            act.wait_ge(*pv_done.at(b, (m - 6) // 4 + 1))
                        s_.copy(pt[:, m % 6, 0:nk], out_of(name)[:, 0:nk]).then_inc(*drains(name))
                    m = n - LAG_PV + 1
                    if m >= 0 and m % 16 == 12:
                        act.wait_ge(*pv_done.at(b, m // 4 + 1))
                        if m // 16:
                            is_filled(act, b, f"OT{m // 16 - 1}")
                        s_.copy(osb, ps[:, 5, :]).then_inc(*o_copied.one)
                if item == "attnT":
                    copy_T(b, "aT", xTa)
                if item == "sum":
                    scaled(b, "y", 0, xna, a_shift, 1)
                if item == "fxT":
                    copy_T(b, "fxT", xTa)
                if item == "fc":
                    is_filled(act, b, f"fc{n}")
                    s_.activation(squared[:, n, :], out_of(f"fc{n}"), ACT.Relu, bias=zero[:, 0:1]
                                  ).then_inc(*drains(f"fc{n}"))
                if item == "fsum":
                    scaled(b, "fproj", 0, xna, a_shift, 2)

            def mixer(b, item, n):
                if item == "xT":
                    copy_T(b, ("m_xTb", "m_xTc")[n - 1], xTr)
                if item == "fc2":
                    name = f"m_fd{n}"
                    is_filled(act, b, name)
                    s_.activation(hid[:, n, :], out_of(name), ACT.Relu, bias=b1c[:, n:n + 1]).then_inc(*drains(name))
                if item == "sum" and n == 1:
                    scaled(b, "m_out", 1, xnr, m_shift, 1)
                if item == "sum" and n == 2:
                    act.wait_ge(*m_shift.at(b, 2))
                    for t in range(TT):
                        i = s_.activation(xnr[:, t, :], xnr[:, t, :], ACT.Identity, scale=norms[:, 1, t, 9:10],
                                          bias=norms[:, 1, t, 10:11])
                    i.then_inc(*m_scaled.one)
                if item == "z":
                    name = f"m_z{n}"
                    is_filled(act, b, name)
                    s_.activation(zc[:, n % 2, n // 2, :], out_of(name), ACT.Copy,
                                  scale=taps[:, n % 2, n // 2, KS - 1:KS]).then_inc(*last_tap.one)
                if item == "weights":
                    act.wait_ge(*logp_ready.at(b, 1))
                    s_.activation(zc[:, 1], zc[:, 1], ACT.Exp).then_inc(*pw_ready.one)
                if item == "query":
                    name = f"m_q{n}"
                    is_filled(act, b, name)
                    s_.copy(qc[:, n, :], out_of(name)).then_inc(*drains(name))
                if item == "wave":
                    r, slot = n, n % 3
                    act.wait_ge(*turned.at(b, r + 1))
                    if r >= 3:
                        act.wait_ge(*gathered.at(b, r - 2))
                    s_.activation(ring[:, slot, 0:MH], frac[:, r % 2], ACT.Abs).then_inc(*folded.one)
                    s_.activation(ring[:, slot, MH:2 * MH], frac[:, r % 2], ACT.Sin, scale=TWO_PI)
                    act.wait_ge(*folded.at(b, r + 1))
                    s_.activation(ring[:, slot, 0:MH], ring[:, slot, 0:MH], ACT.Sin, scale=-TWO_PI,
                                  bias=half_pi[:, 0:1]).then_inc(*waved.one)
                if item == "gate":
                    for h in range(RH):
                        is_drained(act, b, f"m_mem{h}")
                    s_.activation(frac[:, 0], inv, ACT.Tanh, scale=0.5).then_inc(*y_tanh.one)

            def prepare(item, n):
                if item == "ternary" and n == 0:
                    act.wait_ge(prep_step, 2)
                    s_.activation(soft[:, 1, :], soft[:, 0, :], ACT.Exp).then_inc(prep_soft, 1)
                    act.wait_ge(prep_soft, 1)
                    s_.activation(soft[:, 2, :], soft[:, 1, :], ACT.Ln, bias=1.0).then_inc(prep_soft, 1)
                if item == "prep" and not 4 <= n < 8:
                    i, o = n % 2, ps[:, 6 + n % 2, :]
                    act.wait_ge(prep_filled[i], n // 2 + 1)
                    if n < 2:
                        k = s_.copy(uT[0:RANK, n, :], o[0:RANK])
                    elif n < 4:
                        k = s_.copy(a1T[0:RANK, n - 2, :], o[0:RANK])
                    elif n < 12:
                        c, half = (n - 8) // 2, n % 2
                        k = s_.copy(wfc[:, c, half * 512:(half + 1) * 512], o)
                    else:
                        c = 2 * (n - 12)
                        k = s_.copy(wpr[:, c:c + 2, :].rearrange("p a b -> p (a b)"), o)
                    k.then_inc(prep_drained[i], 1)

            def between():
                act.wait_ge(loaded, 16 * n_rest[0])
                act.wait_ge(prep_step, N_PREP)
                act.wait_ge(prep_drained[0], 8)
                act.wait_ge(prep_drained[1], 8)

            run(act, attention, mixer, prepare, between)

        @block.vector
        def _(dve):
            v_ = nc.vector
            v_.memset(vaug, 0.0).then_inc(values_blank, 1)
            dve.wait_ge(values_blank, 1)
            v_.memset(vaug[:, :, :, HD:HD + 1], 1.0).then_inc(values_blank, 1)
            for s in (a_stats, a_shift, a_xn, rope_ready, a_step, m_stats, m_shift, m_xn, logp_ready, turned, mixed,
                      inv_ready, y_ready, m_step):
                dve.sem_inc(s.sem, s.per_batch)
            dve.wait_ge(values_blank, 2)

            def take_wait():
                dve.sem_inc(waits_taken, 1)

            def step(b, own, instruction):
                instruction.then_inc(*own.one)
                dve.wait_ge(*own.last(b))

            def statistics(b, chain, own, src, stats):
                for t in range(TT):
                    i = v_.bn_stats(norms[:, chain, t, 0:6], src(t))
                i.then_inc(*own.one)
                dve.wait_ge(*own.last(b))
                take_wait()
                for t in range(TT):
                    i = v_.bn_aggr(norms[:, chain, t, 6:8], norms[:, chain, t, 0:6])
                step(b, own, i)
                v_.tensor_scalar(norms[:, chain, :, 8], norms[:, chain, :, 7], EPS, None, ALU.add
                                 ).then_inc(*stats.one)

            def normed(b, chain, src, dst, rstd, n, done):
                dve.wait_ge(*rstd.at(b, n))
                for t in range(TT):
                    i = v_.tensor_scalar(dst[:, t, :], src[:, t, :], norms[:, chain, t, 6:7],
                                         norms[:, chain, t, 9:10], ALU.subtract, ALU.mult)
                i.then_inc(*done.one)

            def shift(b, chain, rstd, n, done):
                dve.wait_ge(*rstd.at(b, n))
                v_.scalar_tensor_tensor(norms[:, chain, :, 10], norms[:, chain, :, 6], -1.0, norms[:, chain, :, 9],
                                        ALU.mult, ALU.mult).then_inc(*done.one)

            def pair_of(tag):
                return lambda t: ps[:, bank(f"{tag}{t // 2}"), t % 2 * D:(t % 2 + 1) * D]

            def rotate(b, plain, swapped, dst):
                is_filled(dve, b, plain)
                v_.tensor_tensor(rtmp[0:DR, 0, :], out_of(plain)[0:DR], rope[:, 0, :], ALU.mult
                                 ).then_inc(*drains(plain))
                is_filled(dve, b, swapped)
                v_.tensor_tensor(rtmp[0:DR, 1, :], out_of(swapped)[0:DR], rope[:, 1, :], ALU.mult
                                 ).then_inc(*drains(swapped))
                is_drained(dve, b, plain)
                is_drained(dve, b, swapped)
                v_.tensor_tensor(dst[0:DR], rtmp[0:DR, 0, :], rtmp[0:DR, 1, :], ALU.add).then_inc(*rope_ready.one)
                dve.wait_ge(*rope_ready.last(b))

            def copied(b, name, dst, src):
                is_filled(dve, b, name)
                v_.tensor_copy(dst, src).then_inc(*drains(name))

            def split(b, kind, n, piece):
                for g in range(DC):
                    name = f"{kind}{g}"
                    dve.wait_ge(*first_piece.at(b, n + g + 1))
                    if n:
                        dve.wait_ge(*third_piece.at(b, g + 1))
                    v_.tensor_tensor(rest[:, g, :], out_of(name), piece[:, g, :], ALU.subtract
                                     ).then_inc(*drains(name))

            def attention(b, item, n):
                if item == "stats":
                    dve.wait_ge(*x_loaded.at(b, 1))
                    statistics(b, 0, a_step, lambda t: x_in[:, t, :], a_stats)
                if item == "norm":
                    dve.wait_ge(*a_sum.at(b, 0))
                    normed(b, 0, x_in, xna, a_rstd, 1, a_xn)
                if item == "fstats":
                    dve.wait_ge(*a_sum.at(b, 1))
                    statistics(b, 0, a_step, lambda t: xa[:, t, :], a_stats)
                if item == "fnorm":
                    normed(b, 0, xa, xna, a_rstd, 3, a_xn)
                if item == "fystats":
                    is_filled(dve, b, "fproj0")
                    is_filled(dve, b, "fproj1")
                    statistics(b, 0, a_step, pair_of("fproj"), a_stats)
                if item == "fsum":
                    shift(b, 0, a_rstd, 4, a_shift)
                if item == "proj" and n == 0:
                    if isinstance(b, int) and b == 0:
                        dve.wait_ge(loaded_first, 16 * n_first[0])
                    copied(b, "ckv", ckv, out_of("ckv"))
                    split(b, "q", 0, q_pieces[:, :, 0])
                    rotate(b, "qr", "qs", qrope)
                if item == "proj" and n == 1:
                    split(b, "k", DC, k_pieces[:, :, 2])
                    rotate(b, "kr", "ks", krope)
                if item == "base":
                    for t in range(TT):
                        name, at = f"base{t}", t * P
                        is_filled(dve, b, name)
                        if t:
                            v_.tensor_copy(base_of(t)[:, 0:at], out_of(name)[:, 0:at])
                        v_.tensor_tensor(base_of(t)[:, at:at + P], out_of(name)[:, at:at + P], mask[:],
                                         ALU.add).then_inc(*drains(name))
                    for t in range(TT):
                        is_drained(dve, b, f"base{t}")
                if item == "slot":
                    if n < 64:
                        qt = HEADS[n][1]
                        nk, name = (qt + 1) * P, f"S{n}"
                        is_filled(dve, b, name)
                        if n >= 4:
                            is_filled(dve, b, f"T{n - 4}")
                        take_wait()
                        v_.tensor_tensor_reduce(sc[:, n % 4, 0:nk], out_of(name)[:, 0:nk], base_of(qt), -SCORE_SCALE,
                                                BIG, ALU.add, ALU.min, nmax[:, n:n + 1]).then_inc(*drains(name))
                    m = n - LAG_T
                    if 0 <= m < 64 and m % 2 == 1:
                        nk = (HEADS[m][1] + 1) * P
                        if m >= 6:
                            dve.wait_ge(*pv_done.at(b, (m - 6) // 4 + 1))
                        copied(b, f"T{m}", pt[:, m % 6, 0:nk], out_of(f"T{m}")[:, 0:nk])
                    if n >= LAG_OT and (n - LAG_OT) % 16 == 0:
                        g = (n - LAG_OT) // 16
                        name = f"OT{g}"
                        o = out_of(name).rearrange("p (t j e) -> p t j e", t=TT, j=4)
                        is_filled(dve, b, name)
                        step(b, a_step, v_.reciprocal(rden, o[:, :, :, HD]))
                        v_.tensor_tensor(att[:].rearrange("p t (g j e) -> p t g j e", g=4, j=4)[:, :, g],
                                         o[:, :, :, 0:HD], rden[:, :, :, None].to_broadcast([P, TT, 4, HD]), ALU.mult
                                         ).then_inc(*drains(name))
                if item == "ystats":
                    is_filled(dve, b, "y0")
                    is_filled(dve, b, "y1")
                    statistics(b, 0, a_step, pair_of("y"), a_stats)
                if item == "sum":
                    shift(b, 0, a_rstd, 2, a_shift)

            def mixer(b, item, n):
                if item == "stats":
                    src = (xa, xr)[n - 1]
                    dve.wait_ge(*(a_sum.at(b, 2) if n == 1 else m_sum.at(b, 1)))
                    statistics(b, 1, m_step, lambda t: src[:, t, :], m_stats)
                if item == "norm":
                    normed(b, 1, (xa, xr)[n - 1], xnr, m_rstd, 2 * n - 1, m_xn)
                if item == "sum":
                    shift(b, 1, m_rstd, 2 * n, m_shift)
                if item == "ystats":
                    tag = ("m_out", "m_prok")[n - 1]
                    for h in range(2):
                        is_filled(dve, b, f"{tag}{h}")
                    if n < 2:
                        statistics(b, 1, m_step, pair_of(tag), m_stats)
                    else:
                        for h in range(2):
                            name = f"{tag}{h}"
                            v_.tensor_tensor(xnr[:, 2 * h:2 * h + 2, :], out_of(name).rearrange("p (t d) -> p t d", t=2),
                                             b2r[:, None, :].to_broadcast([P, 2, D]), ALU.add).then_inc(*drains(name))
                        for h in range(2):
                            is_drained(dve, b, f"{tag}{h}")
                        statistics(b, 1, m_step, lambda t: xnr[:, t, :], m_stats)
                if item == "z":
                    name, kind, r = f"m_z{n}", n % 2, n // 2
                    dve.wait_ge(*last_tap.at(b, n + 1))
                    for j in range(KS - 2, -1, -1):
                        s = KS - 1 - j
                        i = v_.scalar_tensor_tensor(zc[:, kind, r, s:T], out_of(name)[:, 0:T - s],
                                                    taps[:, kind, r, j:j + 1], zc[:, kind, r, s:T], ALU.mult, ALU.add)
                        if j:
                            step(b, m_step, i)
                    i.then_inc(*drains(name))
                if item == "weights":
                    is_drained(dve, b, "m_z1")
                    is_drained(dve, b, "m_z3")
                    for r in range(RH):
                        i = v_.tensor_scalar(zc[:, 1, r, :], zc[:, 1, r, :], sscale[:, r:r + 1], 20.0, ALU.mult, ALU.min)
                    step(b, m_step, i)
                    v_.scalar_tensor_tensor(zc[:, 1], zc[:, 1], -20.0, logw[:], ALU.max, ALU.add
                                            ).then_inc(*logp_ready.one)
                if item == "inv":
                    dve.wait_ge(*pw_ready.at(b, 1))
                    total = inv[:, n, :]
                    step(b, m_step, v_.tensor_tensor_scan(total, zero[:, 0:1].to_broadcast([P, T]), zc[:, 1, n, :],
                                                          0.0, ALU.add, ALU.add))
                    step(b, m_step, v_.tensor_scalar(total, total, 1e-4, None, ALU.max))
                    v_.reciprocal(total, total).then_inc(*inv_ready.one)
                if item == "turn":
                    r = n
                    dve.wait_ge(*kv_sent[r % RL].at(b, (r // RL + 1) * ML))
                    if r >= 1:
                        dve.wait_ge(*turned.at(b, r))
                    if r >= 2:
                        dve.wait_ge(*waved.at(b, r - 1))
                    if r >= 3:
                        dve.wait_ge(*gathered.at(b, r - 2))
                    for m in range(MH):
                        i = v_.tensor_scalar(ring[:, r % 3, m, :], kvr[:, r % RL, :], turns[:, r, m:m + 1], ROUND,
                                             ALU.mult, ALU.add)
                    i.then_inc(*m_step.one)
                if item == "whole":
                    whole = ring[:, n % 3, 0:MH]
                    dve.wait_ge(*m_step.last(b))
                    v_.tensor_scalar(whole, whole, ROUND, None, ALU.subtract).then_inc(*m_step.one)
                if item == "frac":
                    r = n
                    dve.wait_ge(*m_step.last(b))
                    for m in range(MH):
                        i = v_.scalar_tensor_tensor(frac[:, r % 2, m, :], kvr[:, r % RL, :], turns[:, r, m:m + 1],
                                                    ring[:, r % 3, m, :], ALU.mult, ALU.subtract)
                    i.then_inc(*turned.one)
                if item == "scan":
                    r, j = n // (2 * MH), n % (2 * MH)
                    if j == 0:
                        dve.wait_ge(*weighed.at(b, r + 1))
                    v_.tensor_tensor_scan(ring[:, r % 3, j, :], zero[:, 0:1].to_broadcast([P, T]),
                                          ring[:, r % 3, j, :], 0.0, ALU.add, ALU.add).then_inc(*m_step.one)
                if item == "mix":
                    r, half = n // 2, slice(n % 2 * MH, (n % 2 + 1) * MH)
                    if n == 0:
                        is_drained(dve, b, "m_q2")
                        is_drained(dve, b, "m_q3")
                    dve.wait_ge(*m_step.last(b))
                    v_.tensor_tensor(ring[:, r % 3, half], ring[:, r % 3, half], qc[:, half], ALU.mult
                                     ).then_inc(*mixed.one)
                if item == "gate":
                    dve.wait_ge(*inv_ready.at(b, RH))
                    for h in range(RH):
                        dve.wait_ge(*gathered.at(b, (h + 1) * RL))
                        v_.tensor_tensor(inv[:, h, :], out_of(f"m_mem{h}"), inv[:, h, :], ALU.mult
                                         ).then_inc(*drains(f"m_mem{h}"))
                    dve.wait_ge(*y_tanh.at(b, 1))
                    v_.scalar_tensor_tensor(inv, frac[:, 0], 1.0, inv, ALU.add, ALU.mult).then_inc(*y_ready.one)

            count = [0]

            def prep(instruction):
                count[0] += 1
                instruction.then_inc(prep_step, 1)
                dve.wait_ge(prep_step, count[0])

            def magnitudes(raw, k, n_row, n_col):
                mag = tmp_a.rearrange("p (g i) -> p g i", g=n_row)
                scale, hi, lo = (rows[:, k, i, 0:n_row] for i in range(3))
                prep(v_.tensor_scalar(mag, raw, -1.0, None, ALU.mult))
                prep(v_.tensor_tensor(mag, mag, raw, ALU.max))
                prep(v_.tensor_reduce(scale, mag, AX.X, ALU.add))
                prep(v_.tensor_scalar(scale, scale, 1.0 / n_col, 1e-5, ALU.mult, ALU.max))
                prep(v_.tensor_scalar(hi, scale, 0.5, None, ALU.mult))
                prep(v_.tensor_scalar(lo, scale, -0.5, None, ALU.mult))

            def ternary(raw, k, n_row):
                mag = tmp_a.rearrange("p (g i) -> p g i", g=n_row)
                low = tmp_b.rearrange("p (g i) -> p g i", g=n_row)
                scale, hi, lo = (rows[:, k, i, 0:n_row] for i in range(3))
                for g in range(n_row):
                    v_.tensor_scalar(mag[:, g, :], raw[:, g, :], hi[:, g:g + 1], scale[:, g:g + 1], ALU.is_gt, ALU.mult)
                    i = v_.tensor_scalar(low[:, g, :], raw[:, g, :], lo[:, g:g + 1], scale[:, g:g + 1],
                                         ALU.is_lt, ALU.mult)
                prep(i)
                prep(v_.tensor_tensor(raw, mag, low, ALU.subtract))

            def prepare(item, n):
                if item == "ternary" and n == 0:
                    dve.wait_ge(loaded, 16 * n_rest[0])
                    prep(v_.tensor_scalar(soft[:, 0, :], slope, -1.0, None, ALU.mult))
                    prep(v_.tensor_tensor(soft[:, 0, :], soft[:, 0, :], slope, ALU.min))
                    magnitudes(raw_fc, 0, HC, D)
                if item == "ternary" and n == 1:
                    ternary(raw_fc, 0, HC)
                if item == "ternary" and n == 2:
                    magnitudes(raw_pr, 1, DC, HID)
                if item == "ternary" and n == 3:
                    ternary(raw_pr, 1, DC)
                if item == "prep" and 4 <= n < 8:
                    i = n % 2
                    dve.wait_ge(prep_filled[i], n // 2 + 1)
                    for g in range(2):
                        c = (n - 4) * 2 + g
                        k = v_.scalar_tensor_tensor(raw_fc[:, c, :], ps[:, 6 + i, g * D:(g + 1) * D], gcol[:, 0:1],
                                                    raw_fc[:, c, :], ALU.mult, ALU.add)
                    k.then_inc(prep_drained[i], 1)
                if item == "tables":
                    v_.tensor_tensor(fac[:, 0, :], fac[:, 0, :], fac[:, 2, :], ALU.mult)
                    prep(v_.tensor_tensor(fac[:, 1, :], fac[:, 1, :], fac[:, 3, :], ALU.mult))
                    fa, fb = (fac[:, i, None, :].to_broadcast([P, DC * MH, P]) for i in range(2))
                    flat = [a.rearrange("p c m n -> p (c m) n") for a in (raw_re, raw_im, wqc[:, 0], wqc[:, 1])]
                    t0 = tmp_a[:, 0:DC * MH * P].rearrange("p (a n) -> p a n", n=P)
                    t1 = tmp_b[:, 0:DC * MH * P].rearrange("p (a n) -> p a n", n=P)
                    v_.tensor_tensor(t0, flat[0], fa, ALU.mult)
                    prep(v_.tensor_tensor(t1, flat[1], fb, ALU.mult))
                    prep(v_.tensor_tensor(flat[2], t0, t1, ALU.subtract))
                    v_.tensor_tensor(t0, flat[1], fa, ALU.mult)
                    prep(v_.tensor_tensor(t1, flat[0], fb, ALU.mult))
                    prep(v_.tensor_tensor(flat[3], t0, t1, ALU.add))
                    prep(v_.tensor_scalar(wout[:], wout[:], 0.5, None, ALU.mult))
                    prep(v_.tensor_scalar(turns, turns, 1.0 / TWO_PI_EXACT, None, ALU.mult))
                    dve.wait_ge(prep_soft, 2)
                    e, ln, d, one = soft[:, 1, :], soft[:, 2, :], soft[:, 3, :], soft[:, 4, :]
                    prep(v_.tensor_scalar(d, e, 1.0, 1.0, ALU.add, ALU.subtract))
                    prep(v_.tensor_scalar(one, d, 0.0, None, ALU.is_equal))
                    prep(v_.tensor_tensor(d, d, one, ALU.add))
                    prep(v_.reciprocal(d, d))
                    prep(v_.tensor_tensor(ln, ln, d, ALU.mult))
                    prep(v_.tensor_tensor(ln, ln, one, ALU.add))
                    prep(v_.tensor_tensor(ln, ln, e, ALU.mult))
                    prep(v_.tensor_scalar(one, slope, 0.0, None, ALU.max))
                    prep(v_.tensor_tensor(ln, ln, one, ALU.add))
                    for r in range(RH):
                        prep(v_.tensor_scalar(logw[:, r, :], dist[:, r, :], ln[:, r:r + 1], None, ALU.mult))
                    assert count[0] == N_PREP, count[0]

            def between():
                dve.wait_ge(prep_drained[0], 8)
                dve.wait_ge(prep_drained[1], 8)

            run(dve, attention, mixer, prepare, between)

        for name, s in signals.items():
            assert s.given == 3 * s.per_batch, (name, s.given / 3, s.per_batch)


N_PREP = 36
SMALL = HC + REP * MH + 2 * RH * KS + RH + RH + 1
TWO_PI_EXACT = 6.283185307179586


def tables(np):
    f32 = np.float32
    inv_freq = f32(1.0) / np.power(f32(10000.0), np.arange(0, DR, 2, dtype=f32) / f32(DR)).astype(f32)
    freqs = np.outer(np.arange(T, dtype=f32), inv_freq).astype(f32)
    cos, sin = np.cos(freqs).T, np.sin(freqs).T
    rope = np.stack([np.concatenate([cos, cos]), np.concatenate([-sin, sin])], axis=1).astype(f32)
    p = np.arange(P)
    mask = np.where(p[None, :] > p[:, None], f32(MASKED), f32(0.0)).astype(f32)
    pos = np.arange(T, dtype=f32)[None, None, :]
    dist = np.where(slots(np)[:, :, None] < N_DECAY, -(f32(T - 1) - pos), -pos).astype(f32)
    sel = (p[:, None] % W == np.arange(W)[None, :]).astype(f32)
    return {"ident": np.eye(P, dtype=f32), "rope": rope, "mask": mask, "dist": dist, "sel": sel}


def slots(np):
    p = np.arange(P)
    return (p[:, None] % W // H) * REP + np.arange(RH)[None, :] * RL + p[:, None] // W


def layout(np, a):
    p = np.arange(P)
    slot = slots(np)
    chan = slot * H + p[:, None] % H
    w_in = a["L1_attn_W_in"].reshape(DC, P, -1)
    by_slot = np.stack([w_in[:, :, chan.T], w_in[:, :, D + slot.T]], axis=2)
    kq, h, ml = p % W // H, p % H, p // W
    m = np.arange(MH)[None, :] * ML + ml[:, None]
    q0 = D + K + ((kq[:, None] * H + h[:, None]) * M + m) * 2
    conv = a["L1_attn_conv_k"][:, 0, :]
    slopes = np.concatenate([a["L1_attn_decay_slopes"], a["L1_attn_anchor_slopes"]])
    theta = a["L1_attn_theta"][0, 0]
    rep = np.arange(REP)
    turns = theta[kq[:, None, None] * REP + rep[None, :, None], h[:, None, None], m[:, None, :]]
    small = [a["L1_ffn_b1"].reshape(HC, P).T, turns.reshape(P, -1),
             np.stack([conv[:, chan], conv[:, D + slot]]).transpose(2, 0, 3, 1).reshape(P, -1),
             a["L1_attn_score_scale"][slot], slopes[slot],
             np.broadcast_to(a["L0_ffn_gate"].reshape(1, 1), (P, 1))]
    grouped = np.arange(D).reshape(4, 4, HD).transpose(0, 2, 1).reshape(-1)
    ns = a["L1_attn_norm_scale"]
    factors = np.stack([ns[h], ns[H + h], a["L1_attn_W_re"][h, h], a["L1_attn_W_im"][h, h]])
    return {
        "x": a["L0_attn_x"], "w_kv_down": a["L0_attn_W_kv_down"], "w_k_up": a["L0_attn_W_k_up"][:, grouped],
        "w_v_up": a["L0_attn_W_v_up"], "w_q": a["L0_attn_W_q"][:, grouped], "w_q_rope": a["L0_attn_W_q_rope"],
        "w_k_rope": a["L0_attn_W_k_rope"], "w_o": a["L0_attn_W_o"], "fast_b": a["L0_ffn_fast_b"],
        "w_fc": a["L0_ffn_w_fc"], "w_proj": a["L0_ffn_w_proj"], "u": a["L0_ffn_u"], "v": a["L0_ffn_v"],
        "w_in_slots": by_slot.transpose(1, 0, 2, 3, 4),
        "w_in_re": w_in[:, :, q0.T].transpose(1, 0, 2, 3),
        "w_in_im": w_in[:, :, q0.T + 1].transpose(1, 0, 2, 3),
        "w_out": a["L1_attn_W_out"][chan], "w1": a["L1_ffn_W1"], "w2": a["L1_ffn_W2"],
        "small": np.concatenate(small, axis=1), "factors": np.broadcast_to(factors[None], (P, 4, P)),
        "b2": np.broadcast_to(a["L1_ffn_b2"][None], (P, D)),
    }


def kernel(**inputs):
    import numpy as np
    import concourse.bacc as bacc
    from concourse.bass_utils import run_bass_kernel_spmd

    arrays = layout(np, {name: np.asarray(a) for name, a in inputs.items()})
    for name, a in tables(np).items():
        arrays[f"table_{name}"] = a
    arrays = {name: np.ascontiguousarray(a) for name, a in arrays.items()}
    nc = bacc.Bacc("TRN2", target_bir_lowering=False, num_devices=1)
    args = [nc.dram_tensor(name, a.shape, mybir.dt.from_np(a.dtype), kind="ExternalInput").ap()
            for name, a in arrays.items()]
    args.append(nc.dram_tensor("out", (B, T, D), F32, kind="ExternalOutput").ap())
    args.append(nc.dram_tensor("scratch", (B, 2, DC, 2, 3, P // 2, T), BF16, kind="Internal").ap())
    sandwich_kernel(nc, *args)
    r = run_bass_kernel_spmd(nc, [arrays], core_ids=[0])
    return r.results[0]["out"]
```
